# Optimizing a Trainium2 kernel written in Bass

```python
import numpy as np
import jax
import jax.numpy as jnp

def _softmax(x, axis=-1):
    return jax.nn.softmax(x, axis=axis)

def _gelu(x):
    return jax.nn.gelu(x, approximate=True)

def _silu(x):
    return jax.nn.silu(x)

def _sigmoid(x):
    return jax.nn.sigmoid(x)

def _layernorm(x, axis=-1, eps=1e-05):
    m = jnp.mean(x, axis=axis, keepdims=True)
    v = jnp.var(x, axis=axis, keepdims=True)
    return (x - m) / jnp.sqrt(v + eps)

def _scatter_add(tgt, idx, src, axis=0):
    return tgt.at[idx].add(src)

def _segment_sum(src, seg, n):
    return jax.ops.segment_sum(src, seg, n)
kernel_name = 'mk_lm_tower_d1_tok_ids768_r4_43e9fb'

def setup_inputs(seed: int=0):
    np.random.seed(seed)
    _w = jnp.asarray

    def _rec_inputs():
        import jax
        import jax.numpy as jnp
        _rk = jax.random.key(seed)
        x = jax.random.randint(jax.random.fold_in(_rk, 1), (64, 128), 0, 12564, jnp.int32)
        return x
    x = _rec_inputs()

    def _L0_tok_setup():
        import jax, jax.numpy as jnp
        import numpy as np
        VOCAB = 50257
        DIM = 192
        BATCH = 8
        SEQ = 1024
        QMAX = 127.0
        EPS = 1e-08
        key = jax.random.key(seed)
        k_ids, k_w = jax.random.split(key)
        input_ids = jax.random.randint(k_ids, (BATCH, SEQ), 0, VOCAB, dtype=jnp.int64)
        weight = jax.random.normal(k_w, (VOCAB, DIM), dtype=jnp.float32) * 0.02
        return {'input': input_ids, 'weight': weight}
    _L0_tok_all = _L0_tok_setup()
    _L0_tok_in = {k: v for k, v in _L0_tok_all.items() if k in ('weight',)}
    del _L0_tok_all

    def _L0_attn_setup():
        import jax, jax.numpy as jnp
        import numpy as np
        B_SZ, SEQ = (2, 1024)
        D_MODEL, D_STATE, D_CONV, HEADDIM = (192, 128, 4, 64)
        D_INNER = 384
        NHEADS = D_INNER // HEADDIM
        D_XBC = D_INNER + 2 * D_STATE
        D_PROJ = 2 * D_INNER + 2 * D_STATE + NHEADS
        CHUNK = 128
        EPS = 1e-05

        def segsum(x):
            T = x.shape[-1]
            xc = jnp.cumsum(x, axis=-1)
            d = xc[..., :, None] - xc[..., None, :]
            mask = jnp.tril(jnp.ones((T, T), bool))
            return jnp.where(mask, d, -jnp.inf)

        def ssd(xd, Adt, B, C):
            b, L, H, P = xd.shape
            c, Q = (L // CHUNK, CHUNK)
            xd = xd.reshape(b, c, Q, H, P)
            Adt = Adt.reshape(b, c, Q, H).transpose(0, 3, 1, 2)
            Bc = B.reshape(b, c, Q, -1)
            Cc = C.reshape(b, c, Q, -1)
            A_cum = jnp.cumsum(Adt, axis=-1)
            Lmat = jnp.exp(segsum(Adt))
            CB = jnp.einsum('bcln,bcsn->bcls', Cc, Bc)
            Y_diag = jnp.einsum('bcls,bhcls,bcshp->bclhp', CB, Lmat, xd)
            decay_states = jnp.exp(A_cum[..., -1:] - A_cum)
            states = jnp.einsum('bcln,bhcl,bclhp->bchpn', Bc, decay_states, xd)
            A_last = A_cum[..., -1]
            decay_chunk = jnp.exp(segsum(jnp.pad(A_last, ((0, 0), (0, 0), (1, 0)))))
            states_pad = jnp.concatenate([jnp.zeros_like(states[:, :1]), states], axis=1)
            prev = jnp.einsum('bhzc,bchpn->bzhpn', decay_chunk, states_pad)[:, :-1]
            Y_off = jnp.einsum('bcln,bhcl,bchpn->bclhp', Cc, jnp.exp(A_cum), prev)
            return (Y_diag + Y_off).reshape(b, L, H, P)
        key = jax.random.key(seed)
        ks = jax.random.split(key, 10)
        feature = jax.random.normal(ks[0], (B_SZ, SEQ, D_MODEL), jnp.float32)
        in_proj_w = jax.random.normal(ks[1], (D_PROJ, D_MODEL), jnp.float32) * 0.02
        conv_w = jax.random.normal(ks[2], (D_XBC, D_CONV), jnp.float32) * 0.2
        conv_b = jax.random.normal(ks[3], (D_XBC,), jnp.float32) * 0.02
        dt_bias = jnp.log(jnp.expm1(jax.random.uniform(ks[4], (NHEADS,), jnp.float32, 0.001, 0.1)))
        A_log = jnp.log(jax.random.uniform(ks[5], (NHEADS,), jnp.float32, 1.0, 16.0))
        D = jax.random.normal(ks[6], (NHEADS,), jnp.float32) * 0.1 + 1.0
        norm_w = jnp.ones((D_INNER,), jnp.float32)
        out_proj_w = jax.random.normal(ks[7], (D_MODEL, D_INNER), jnp.float32) * 0.02
        gate1 = jnp.float32(0.6)
        return {'feature': feature, 'gate1': gate1, 'in_proj_w': in_proj_w, 'conv_w': conv_w, 'conv_b': conv_b, 'dt_bias': dt_bias, 'A_log': A_log, 'D': D, 'norm_w': norm_w, 'out_proj_w': out_proj_w}
    _L0_attn_all = _L0_attn_setup()
    _L0_attn_in = {k: v for k, v in _L0_attn_all.items() if k in ('gate1', 'in_proj_w', 'conv_w', 'conv_b', 'dt_bias', 'A_log', 'D', 'norm_w', 'out_proj_w')}
    del _L0_attn_all

    def _L0_ffn_setup():
        import jax, jax.numpy as jnp
        import numpy as np
        B, S, H, F = (4, 256, 192, 768)
        EC, EU = (4, 4)
        CAP_FACTOR = 1.0

        def _ffn(x, W1, b1, W2, b2):
            return jax.nn.gelu(x @ W1 + b1, approximate=False) @ W2 + b2

        def _expert_mix(h, route, W1, b1, W2, b2, n_exp):
            out = jnp.zeros_like(h)
            for e in range(n_exp):
                m = (route == e).astype(h.dtype)[:, None]
                out = out + m * _ffn(h, W1[e], b1[e], W2[e], b2[e])
            return out

        def _drop_mask(route, pmax, capacity):
            N = route.shape[0]
            order = jnp.lexsort((-jax.lax.stop_gradient(pmax), route))
            rs = route[order]
            starts = jnp.searchsorted(rs, rs, side='left')
            rank_sorted = jnp.arange(N) - starts
            rank = jnp.zeros((N,), jnp.int32).at[order].set(rank_sorted.astype(jnp.int32))
            return rank >= capacity
        key = jax.random.key(seed)
        ks = jax.random.split(key, 8)

        def w(k, shape, s=0.02):
            return jax.random.normal(k, shape, jnp.float32) * s
        return {'hidden_states': jax.random.normal(ks[0], (B, S, H), jnp.float32), 'Wsc': w(ks[1], (H, EC)), 'bsc': jnp.zeros((EC,), jnp.float32), 'W1c': w(ks[2], (EC, H, F)), 'b1c': jnp.zeros((EC, F), jnp.float32), 'W2c': w(ks[3], (EC, F, H)), 'b2c': jnp.zeros((EC, H), jnp.float32), 'Wsu': w(ks[4], (H, EU)), 'bsu': jnp.zeros((EU,), jnp.float32), 'W1u': w(ks[5], (EU, H, F)), 'b1u': jnp.zeros((EU, F), jnp.float32), 'W2u': w(ks[6], (EU, F, H)), 'b2u': jnp.zeros((EU, H), jnp.float32)}
    _L0_ffn_all = _L0_ffn_setup()
    _L0_ffn_in = {k: v for k, v in _L0_ffn_all.items() if k in ('Wsc', 'bsc', 'W1c', 'b1c', 'W2c', 'b2c', 'Wsu', 'bsu', 'W1u', 'b1u', 'W2u', 'b2u')}
    del _L0_ffn_all
    return {'x': x, 'L0_tok_weight': _L0_tok_in['weight'], 'L0_attn_gate1': _L0_attn_in['gate1'], 'L0_attn_in_proj_w': _L0_attn_in['in_proj_w'], 'L0_attn_conv_w': _L0_attn_in['conv_w'], 'L0_attn_conv_b': _L0_attn_in['conv_b'], 'L0_attn_dt_bias': _L0_attn_in['dt_bias'], 'L0_attn_A_log': _L0_attn_in['A_log'], 'L0_attn_D': _L0_attn_in['D'], 'L0_attn_norm_w': _L0_attn_in['norm_w'], 'L0_attn_out_proj_w': _L0_attn_in['out_proj_w'], 'L0_ffn_Wsc': _L0_ffn_in['Wsc'], 'L0_ffn_bsc': _L0_ffn_in['bsc'], 'L0_ffn_W1c': _L0_ffn_in['W1c'], 'L0_ffn_b1c': _L0_ffn_in['b1c'], 'L0_ffn_W2c': _L0_ffn_in['W2c'], 'L0_ffn_b2c': _L0_ffn_in['b2c'], 'L0_ffn_Wsu': _L0_ffn_in['Wsu'], 'L0_ffn_bsu': _L0_ffn_in['bsu'], 'L0_ffn_W1u': _L0_ffn_in['W1u'], 'L0_ffn_b1u': _L0_ffn_in['b1u'], 'L0_ffn_W2u': _L0_ffn_in['W2u'], 'L0_ffn_b2u': _L0_ffn_in['b2u']}

def reference(x, L0_tok_weight, L0_attn_gate1, L0_attn_in_proj_w, L0_attn_conv_w, L0_attn_conv_b, L0_attn_dt_bias, L0_attn_A_log, L0_attn_D, L0_attn_norm_w, L0_attn_out_proj_w, L0_ffn_Wsc, L0_ffn_bsc, L0_ffn_W1c, L0_ffn_b1c, L0_ffn_W2c, L0_ffn_b2c, L0_ffn_Wsu, L0_ffn_bsu, L0_ffn_W1u, L0_ffn_b1u, L0_ffn_W2u, L0_ffn_b2u):
    import jax
    import jax.numpy as jnp

    def _L0_tok_ref(input, weight):
        import jax, jax.numpy as jnp
        import numpy as np
        VOCAB = 50257
        DIM = 192
        BATCH = 8
        SEQ = 1024
        QMAX = 127.0
        EPS = 1e-08
        scale = jnp.max(jnp.abs(weight), axis=-1, keepdims=True) / QMAX
        scale = jnp.maximum(scale, EPS)
        qw = jnp.clip(jnp.round(weight / scale), -QMAX, QMAX) * scale
        return qw[input]

    def _L0_attn_ref(feature, gate1, in_proj_w, conv_w, conv_b, dt_bias, A_log, D, norm_w, out_proj_w):
        import jax, jax.numpy as jnp
        import numpy as np
        B_SZ, SEQ = (2, 1024)
        D_MODEL, D_STATE, D_CONV, HEADDIM = (192, 128, 4, 64)
        D_INNER = 384
        NHEADS = D_INNER // HEADDIM
        D_XBC = D_INNER + 2 * D_STATE
        D_PROJ = 2 * D_INNER + 2 * D_STATE + NHEADS
        CHUNK = 128
        EPS = 1e-05

        def segsum(x):
            T = x.shape[-1]
            xc = jnp.cumsum(x, axis=-1)
            d = xc[..., :, None] - xc[..., None, :]
            mask = jnp.tril(jnp.ones((T, T), bool))
            return jnp.where(mask, d, -jnp.inf)

        def ssd(xd, Adt, B, C):
            b, L, H, P = xd.shape
            c, Q = (L // CHUNK, CHUNK)
            xd = xd.reshape(b, c, Q, H, P)
            Adt = Adt.reshape(b, c, Q, H).transpose(0, 3, 1, 2)
            Bc = B.reshape(b, c, Q, -1)
            Cc = C.reshape(b, c, Q, -1)
            A_cum = jnp.cumsum(Adt, axis=-1)
            Lmat = jnp.exp(segsum(Adt))
            CB = jnp.einsum('bcln,bcsn->bcls', Cc, Bc)
            Y_diag = jnp.einsum('bcls,bhcls,bcshp->bclhp', CB, Lmat, xd)
            decay_states = jnp.exp(A_cum[..., -1:] - A_cum)
            states = jnp.einsum('bcln,bhcl,bclhp->bchpn', Bc, decay_states, xd)
            A_last = A_cum[..., -1]
            decay_chunk = jnp.exp(segsum(jnp.pad(A_last, ((0, 0), (0, 0), (1, 0)))))
            states_pad = jnp.concatenate([jnp.zeros_like(states[:, :1]), states], axis=1)
            prev = jnp.einsum('bhzc,bchpn->bzhpn', decay_chunk, states_pad)[:, :-1]
            Y_off = jnp.einsum('bcln,bhcl,bchpn->bclhp', Cc, jnp.exp(A_cum), prev)
            return (Y_diag + Y_off).reshape(b, L, H, P)
        b, L, _ = feature.shape
        zxbcdt = feature @ in_proj_w.T
        z = zxbcdt[..., :D_INNER]
        xBC = zxbcdt[..., D_INNER:D_INNER + D_XBC]
        dt = jax.nn.softplus(zxbcdt[..., -NHEADS:] + dt_bias)
        xp = jnp.pad(xBC, ((0, 0), (D_CONV - 1, 0), (0, 0)))
        xconv = sum((conv_w[:, k] * xp[:, k:k + L, :] for k in range(D_CONV))) + conv_b
        xBC = jax.nn.silu(xconv)
        x = xBC[..., :D_INNER].reshape(b, L, NHEADS, HEADDIM)
        Bm = xBC[..., D_INNER:D_INNER + D_STATE]
        Cm = xBC[..., D_INNER + D_STATE:]
        A = -jnp.exp(A_log)
        y = ssd(x * dt[..., None], dt * A, Bm, Cm) + D[:, None] * x
        y = y.reshape(b, L, D_INNER)
        y = y * jax.nn.silu(z)
        y = y * jax.lax.rsqrt(jnp.mean(y * y, axis=-1, keepdims=True) + EPS) * norm_w
        out = y @ out_proj_w.T
        return jax.nn.sigmoid(gate1) * out + feature

    def _L0_ffn_ref(hidden_states, Wsc, bsc, W1c, b1c, W2c, b2c, Wsu, bsu, W1u, b1u, W2u, b2u):
        import jax, jax.numpy as jnp
        import numpy as np
        B, S, H, F = (4, 256, 192, 768)
        EC, EU = (4, 4)
        CAP_FACTOR = 1.0

        def _ffn(x, W1, b1, W2, b2):
            return jax.nn.gelu(x @ W1 + b1, approximate=False) @ W2 + b2

        def _expert_mix(h, route, W1, b1, W2, b2, n_exp):
            out = jnp.zeros_like(h)
            for e in range(n_exp):
                m = (route == e).astype(h.dtype)[:, None]
                out = out + m * _ffn(h, W1[e], b1[e], W2[e], b2[e])
            return out

        def _drop_mask(route, pmax, capacity):
            N = route.shape[0]
            order = jnp.lexsort((-jax.lax.stop_gradient(pmax), route))
            rs = route[order]
            starts = jnp.searchsorted(rs, rs, side='left')
            rank_sorted = jnp.arange(N) - starts
            rank = jnp.zeros((N,), jnp.int32).at[order].set(rank_sorted.astype(jnp.int32))
            return rank >= capacity
        shp = hidden_states.shape
        h = hidden_states.reshape(-1, shp[-1])
        N = h.shape[0]
        capacity = int(CAP_FACTOR * N / EC)
        pc = jax.nn.softmax(h @ Wsc + bsc, axis=-1)
        pmax_c = jnp.max(pc, axis=-1)
        route_c = jnp.argmax(pc, axis=-1)
        dropped = _drop_mask(route_c, pmax_c, capacity)
        scale_c = (pmax_c / jax.lax.stop_gradient(pmax_c))[:, None]
        common = _expert_mix(h, route_c, W1c, b1c, W2c, b2c, EC) * scale_c
        pu = jax.nn.softmax(h @ Wsu + bsu, axis=-1)
        pmax_u = jnp.max(pu, axis=-1)
        route_u = jnp.argmax(pu, axis=-1)
        scale_u = (pmax_u / jax.lax.stop_gradient(pmax_u))[:, None]
        unique = _expert_mix(h, route_u, W1u, b1u, W2u, b2u, EU) * scale_u
        out = common + dropped[:, None].astype(h.dtype) * unique
        return out.reshape(shp)
    h = _L0_tok_ref(x, L0_tok_weight)
    h = h + _L0_attn_ref(_layernorm(h, axis=-1), L0_attn_gate1, L0_attn_in_proj_w, L0_attn_conv_w, L0_attn_conv_b, L0_attn_dt_bias, L0_attn_A_log, L0_attn_D, L0_attn_norm_w, L0_attn_out_proj_w)
    h = h + _L0_ffn_ref(_layernorm(h, axis=-1), L0_ffn_Wsc, L0_ffn_bsc, L0_ffn_W1c, L0_ffn_b1c, L0_ffn_W2c, L0_ffn_b2c, L0_ffn_Wsu, L0_ffn_bsu, L0_ffn_W1u, L0_ffn_b1u, L0_ffn_W2u, L0_ffn_b2u)
    return h

_drawn_inputs = setup_inputs


def setup_inputs(seed=0):
    import zlib

    import numpy as np

    out = dict(_drawn_inputs(seed))
    spreads = {'L0_attn_norm_w': (1.0, 0.2),
     'L0_ffn_bsc': (0.0, 0.1),
     'L0_ffn_b1c': (0.0, 0.286),
     'L0_ffn_b2c': (0.0, 0.1),
     'L0_ffn_bsu': (0.0, 0.467),
     'L0_ffn_b1u': (0.0, 0.791),
     'L0_ffn_b2u': (0.0, 0.1)}
    factors = {'L0_attn_dt_bias': 8.0, 'L0_attn_A_log': 8.0}
    for name, (base, spread) in spreads.items():
        noise = np.random.default_rng([zlib.crc32(name.encode()), seed]).standard_normal(out[name].shape)
        drawn = base * np.exp(spread * noise) if base else spread * noise
        out[name] = jnp.asarray(drawn.astype(out[name].dtype))
    for name, factor in factors.items():
        out[name] = (out[name] * factor).astype(out[name].dtype)
    return out
```

```python
from contextlib import ExitStack

import concourse.bass as bass
from concourse import mybir

F32 = mybir.dt.float32
I32 = mybir.dt.int32
ALU = mybir.AluOpType
ACT = mybir.ActivationFunctionType
AX = mybir.AxisListType
ds = bass.ds

P = 128
SEQS, L = 64, 128
NT = SEQS * L
D = 192
DB = D - P
GS = 4
NG = SEQS // GS
GL = GS * L
INNER, STATE, TAPS, HD = 384, 128, 4, 64
HEADS = INNER // HD
XBC = INNER + 2 * STATE
XT, ZT = XBC // P, INNER // P
PROJ = 2 * INNER + 2 * STATE + HEADS
F = 768
FC = F // P
FH = F // 2
NE = 4
CAP = NT // NE
LIST = NT
NLIST = NE * LIST + P
DUMMY = NT
UT = 4
CT = (NT // P + NE - 1 + UT - 1) // UT * UT
DT_ = ((NT - CAP) // P + NE - 1 + UT - 1) // UT * UT
BITS = 26
CREDIT = 1
MAGIC = 12582912.0
QMAX, QEPS, LNEPS = 127.0, 1e-8, 1e-5
NO_SLOT = 40000.0

STEPS = dict(quant=8, tap=10, dt0=1, soft=13, ssd=4, h1=2, pick1=2, pick2=11, find=6)


def wait(eng, sem, value):
    if not (isinstance(value, int) and value <= 0):
        eng.wait_ge(sem, value)


def wait_apart(eng, sem, value, marks):
    if not (isinstance(value, int) and value <= 0):
        eng.wait_ge(sem, value)
        if not isinstance(value, int):
            eng.sem_inc(marks, 1)


class Chain:

    def __init__(self, eng, sem, turn, steps):
        self.eng, self.sem, self.base, self.steps, self.n = eng, sem, turn * steps, steps, 0

    def __call__(self, ins, marks=None):
        self.n += 1
        ins.then_inc(self.sem, 1)
        if marks is None:
            self.eng.wait_ge(self.sem, self.base + self.n)
        else:
            wait_apart(self.eng, self.sem, self.base + self.n, marks)

    def end(self):
        assert self.n == self.steps, (self.n, self.steps)


def stages(i, u):
    it = 4 * i + u
    return [it - k if not isinstance(it, int) or 0 <= it - k < NG else None for k in range(5)]


def earlier(i, u, k):
    return 2 * i + (u - k) // 2


def pipeline(eng, body):
    for u in range(4):
        body(0, u)
    with eng.Fori(1, NG // 4) as i:
        for u in range(4):
            body(i, u)
    for u in range(4):
        body(NG // 4, u)


def build(nc, A, out):
    with ExitStack() as ctx:
        def sb(name, shape, dt=F32, c=ctx):
            return c.enter_context(nc.sbuf_tensor(name, shape, dt))

        def sem(name):
            return ctx.enter_context(nc.semaphore(name))

        def bank(name):
            return ctx.enter_context(nc.psum_tensor(name, [P, 512], F32))

        hr_dram = nc.dram_tensor("hr_dram", [NT + P, 2 * D], F32, kind="Internal").ap()
        list_c = nc.dram_tensor("list_c", [NLIST, 1], I32, kind="Internal").ap()
        list_u = nc.dram_tensor("list_u", [NLIST, 1], I32, kind="Internal").ap()
        out_rows = out.rearrange("b l c -> (b l) c")

        ident = sb("ident", [P, P])
        ones = sb("ones", [P, P])
        le = sb("le", [P, P])
        lt = sb("lt", [P, P])
        gt = sb("gt", [P, P])
        neghalf = sb("neghalf", [P, GS])
        fill = sb("fill", [P, NLIST // P], I32)
        zrow = sb("zrow", [P, 2 * D])
        tok = sb("tok", [P, SEQS], I32)
        xids = sb("xids", [P, SEQS + GS], I32)
        w4 = sb("w4", [P, NE])
        conf = sb("conf", [P, SEQS])
        ohc = sb("ohc", [P, SEQS, NE])
        ohu = sb("ohu", [P, SEQS, NE])
        acc = sb("acc", [P, GS + 1, NE])
        w1a = sb("w1a", [P, NE * F])
        w1b = sb("w1b", [DB + 1, NE * F])
        w2s = sb("w2s", [P, NE * FC * D])
        b2s = sb("b2s", [1, NE * D])
        tile_c = sb("tile_c", [1, 2, CT], I32)
        tile_u = sb("tile_u", [1, 2, DT_], I32)
        slot_u = sb("slot_u", [P, SEQS], I32)
        iota = sb("iota", [1, CT])
        base_e = sb("base_e", [1, NE])

        a = ctx.enter_context(ExitStack())
        win_a, win_b = sb("win_a", [P, PROJ], c=a), sb("win_b", [DB, PROJ], c=a)
        cw, cb = sb("cw", [P, XT, TAPS], c=a), sb("cb", [P, XT], c=a)
        wo = sb("wo", [P, ZT, D], c=a)
        nw, dskip = sb("nw", [P, ZT], c=a), sb("dskip", [P, ZT], c=a)
        dtb, nega = sb("dtb", [P, HEADS], c=a), sb("nega", [P, HEADS], c=a)
        gate = sb("gate", [P, 1], c=a)
        wr_a, wr_b, rb = sb("wr_a", [P, 2 * NE], c=a), sb("wr_b", [DB, 2 * NE], c=a), sb("rb", [P, 2 * NE], c=a)
        gidx = sb("gidx", [P, 2, GS], I32, c=a)
        gath = sb("gath", [P, 2, GS, D], c=a)
        h0 = sb("h0", [P, GS, D], c=a)
        xn = sb("xn", [P, GS, D], c=a)
        hx = sb("hx", [P, 4, GS, D], c=a)
        q1 = sb("q1", [P, 3, GS], c=a)
        st1, mv1 = sb("st1", [P, GS, 6], c=a), sb("mv1", [P, GS, 2], c=a)
        ve1, rstd1 = sb("ve1", [P, 2, GS], c=a), sb("rstd1", [P, 2, GS], c=a)
        xt_a, xt_b = sb("xt_a", [P, 2, GL], c=a), sb("xt_b", [DB, 2, GL], c=a)
        xbc = sb("xbc", [P, 2, XT, GL], c=a)
        zs = sb("zs", [P, 2, ZT, GL], c=a)
        dtr, dab, dtu = (sb(n, [P, 2, GS, HEADS], c=a) for n in ("dtr", "dab", "dtu"))
        dts, dta = sb("dts", [P, 2, GS, HEADS], c=a), sb("dta", [P, 2, GS, HEADS], c=a)
        sp1, sp2, sp3 = (sb(n, [P, GS, HEADS], c=a) for n in ("sp1", "sp2", "sp3"))
        seg_l = sb("seg_l", [P, 2, HEADS, P], c=a)
        dec = sb("dec", [P, 2, HEADS, P], c=a)
        mix = sb("mix", [P, 2, HEADS, P], c=a)
        cbm = sb("cbm", [P, P], c=a)
        xd = sb("xd", [P, 2, INNER], c=a)
        ybuf = sb("ybuf", [P, 2, ZT, GL], c=a)
        ysq = sb("ysq", [P, ZT, GL], c=a)
        ms, rs = sb("ms", [P, GS], c=a), sb("rs", [P, GS], c=a)
        hr = sb("hr", [P, 2, GS, 2 * D], c=a)
        st2, mv2 = sb("st2", [P, GS, 6], c=a), sb("mv2", [P, GS, 2], c=a)
        ve2, rstd2 = sb("ve2", [P, GS], c=a), sb("rstd2", [P, GS], c=a)
        x2t_a, x2t_b = sb("x2t_a", [P, GL], c=a), sb("x2t_b", [DB, GL], c=a)
        lg, dl, el, pk = (sb(n, [P, GS, 2, NE], c=a) for n in ("lg", "dl", "el", "pk"))
        oh = sb("oh", [P, GS, 2, NE], c=a)
        m8, e8, s8 = (sb(n, [P, GS, 2], c=a) for n in ("m8", "e8", "s8"))
        dst = sb("dst", [P, GS, NE], c=a)
        dest = sb("dest", [P, GS], c=a)
        desti, toki = sb("desti", [P, 2, GS], I32, c=a), sb("toki", [P, 2, GS], I32, c=a)
        a.close()
        w1a_u = sb("w1a_u", [P, NE * F])
        w1b_u = sb("w1b_u", [DB + 1, NE * F])
        w2s_u = sb("w2s_u", [P, NE * FC * D])
        b2s_u = sb("b2s_u", [1, NE * D])

        key, cmp_, eqk = sb("key", [P, NE, SEQS]), sb("cmp_", [P, NE, SEQS]), sb("eqk", [P, NE, SEQS])
        scn, tmp = sb("scn", [P, NE, SEQS]), sb("tmp", [P, NE, SEQS])
        thr, cand, tot, step, need = (sb(n, [P, NE]) for n in ("thr", "cand", "tot", "step", "need"))
        zero = sb("zero", [P, SEQS])
        drop = sb("drop", [P, SEQS])
        slotf = sb("slotf", [P, SEQS])
        lst = sb("lst", [1, 8, NE])
        trow = sb("trow", [1, 5, CT])
        slot4, tok4 = sb("slot4", [P, 2, GS], I32), sb("tok4", [P, 2, GS], I32)
        ids = sb("ids", [P, UT, 1], I32)
        xg = sb("xg", [P, UT, 2 * D])
        og = sb("og", [P, UT, D])
        fx_a, fx_b = sb("fx_a", [P, 2, P]), sb("fx_b", [DB + 1, 2, P])
        hg = sb("hg", [P, 2, F])
        ht = sb("ht", [P, 2, F])
        osb = sb("osb", [P, UT, D])

        tp, mm0, mm1, sg0, sg1, cx, yb, misc = (bank(n) for n in ("tp", "mm0", "mm1", "sg0", "sg1", "cx", "yb", "misc"))
        mm = [mm0, mm1]
        DTC, SQC, RTC, PFC = 0, 32, 64, 128

        s_wa, s_wc, s_wu, s_fill = sem("weights_a"), sem("weights_c"), sem("weights_u"), sem("lists_filled")
        s_const, s_prep, s_pe_, s_sig = sem("constants"), sem("prepared"), sem("exp_a_log"), sem("exp_gate")
        s_idx = sem("gather_index")
        s_gath = [sem(f"gathered{p}") for p in range(2)]
        s_ve, s_rstd, s_xn, s_hx = sem("var1"), sem("rstd1_s"), sem("xn_s"), sem("hx_s")
        s_tr1, s_xt = sem("transposed1"), sem("xt_s")
        s_mm, s_ci, s_cv, s_xbc, s_z = sem("projected"), sem("conv_started"), sem("conv_done"), sem("xbc_s"), sem("z_s")
        s_dtp, s_dab, s_u, s_dt = sem("dt_projected"), sem("dt_abs"), sem("dt_exp"), sem("dt_s")
        s_sl, s_sg, s_e, s_cx, s_xd, s_m, s_yp, s_yd, s_y2 = (sem(n) for n in (
            "seg_left", "seg_sums", "decays", "cb_and_x", "xd_s", "mixed", "y_product", "y_read", "y_gated"))
        s_sq, s_ssq, s_ms, s_rs, s_o, s_h1, s_ve2, s_rstd2, s_xn2 = (sem(n) for n in (
            "y_squared", "y_sums", "mean_square", "rms", "out_product", "h1_s", "var2", "rstd2_s", "xn2_s"))
        s_tr2, s_x2t, s_rt, s_d, s_el, s_oh, s_pf, s_dest = (sem(n) for n in (
            "transposed2", "x2t_s", "routers", "logits", "router_exp", "one_hot", "prefixes", "dest_s"))
        s_st = [sem(f"stored{p}") for p in range(2)]
        s_sc = [sem(f"listed{p}") for p in range(2)]
        c_pool = sem("pool_chain")
        ch = {n: sem(f"chain_{n}") for n in STEPS}
        s_cmp, s_cnt, s_tab, s_slot = sem("compared"), sem("counted"), sem("tiles_listed"), sem("slots_found")
        s_s4 = sem("slot_copied")
        s_scd = sem("listed")
        s_su = [sem(f"listed_u{p}") for p in range(2)]
        s_dts, s_free = sem("dt_values"), sem("stage_a_done")
        marks_dve, marks_pe, marks_pool = sem("marks_dve"), sem("marks_pe"), sem("marks_pool")
        c_setup, c_find = sem("chain_setup"), sem("chain_lists")

        block = ctx.enter_context(nc.Block())

        hr_by_seq = hr_dram[0:NT, :].rearrange("(b l) c -> l b c", l=L)
        n_wa = 16 * 17

        fm2 = sem("tile_out_product")
        f_id = [sem(f"tile_ids{u}") for u in range(UT)]
        f_g = [sem(f"tile_gathered{u}") for u in range(UT)]
        f_s = [sem(f"tile_scattered{u}") for u in range(UT)]
        f_t, f_x, f_m1, f_ge, f_h, f_ht, f_o = (sem(n) for n in (
            "tile_transposed", "tile_x", "tile_hidden_product", "tile_gelu", "tile_hidden_transposed", "tile_hidden", "tile_out"))
        TURNS = [CT // UT, DT_ // UT]
        T0 = [0, CT]
        I0 = [0, CT // UT]

        def tiles(eng, m, body):
            for u in range(UT):
                body(0, u, u)
            with eng.Fori(1, TURNS[m]) as i:
                for u in range(UT):
                    body(i, u, i * UT + u)

        def load_experts(sp, to, names, done):
            w1a_, w1b_, w2_, b2_ = to
            w1, w2, b2 = (A[n] for n in names)
            sp.dma_start(w1a_[:, :].rearrange("p (e f) -> p e f", e=NE), w1[:, 0:P, :].rearrange("e p f -> p e f")).then_inc(done, 16)
            sp.dma_start(w1b_[:, :].rearrange("p (e f) -> p e f", e=NE), w1[:, P:D + 1, :].rearrange("e p f -> p e f")).then_inc(done, 16)
            for e in range(NE):
                sp.dma_start(w2_[:, e * FC * D:(e + 1) * FC * D].rearrange("p (c n) -> p c n", c=FC),
                             w2[e].rearrange("(c p) n -> p c n", p=P)).then_inc(done, 16)
            sp.dma_start(b2_[:, :], b2).then_inc(done, 16)

        def experts_sp(sp, m):
            sp.wait_ge(s_tab, m + 1)
            if m == 0:
                sp.wait_ge(s_fill, 48)
                for p in range(2):
                    sp.wait_ge(s_sc[p], 64 * (NG // 2))
            else:
                for p in range(2):
                    sp.wait_ge(s_su[p], 64 * (NG // 2))
            lists, table, n = ((list_c, tile_c, CT), (list_u, tile_u, DT_))[m]

            def body(i, u, t):
                wait(sp, f_s[u], 16 * (I0[m] + i))
                row = sp.value_load(table[0:1, 0, ds(t, 1)], min_val=0, max_val=NLIST - P)
                sp.dma_start(ids[:, u, :], lists[ds(row, P), :]).then_inc(f_id[u], 16)
            tiles(sp, m, body)

        @block.sync
        def _(sp):
            for dst_, src in (
                (xids[:, 0:SEQS], A["x_t"]), (win_a[:, :], A["w_in"][0:P, :]), (win_b[:, :], A["w_in"][P:D, :]),
                (cw[:, :, :], A["conv_w"].rearrange("(m p) k -> p m k", p=P)),
                (cb[:, :], A["conv_b"]),
                (dtb[:, :], A["dt_bias"]), (nega[:, :], A["a_log"]), (dskip[:, :], A["d_skip"]),
                (nw[:, :], A["norm_w"]), (gate[:, :], A["gate"]),
                (wo[:, :, :], A["w_out"].rearrange("(m p) n -> p m n", p=P)),
                (wr_a[:, :], A["w_route"][0:P, :]), (wr_b[:, :], A["w_route"][P:D, :]), (rb[:, :], A["b_route"]),
                (w4[:, :], A["w4"]), (iota[:, :], A["iota"]), (base_e[:, :], A["base_e"]),
            ):
                sp.dma_start(dst_, src).then_inc(s_wa, 16)
            sp.wait_ge(s_const, 1)
            for lst_ in (list_c, list_u):
                sp.dma_start(lst_.rearrange("(p n) o -> p (n o)", p=P), fill[:, :]).then_inc(s_fill, 16)
            sp.dma_start(hr_dram[NT:NT + P, :], zrow[:, :]).then_inc(s_fill, 16)
            load_experts(sp, (w1a, w1b, w2s, b2s), ("w1c", "w2c", "b2c"), s_wc)

            def body(i, u):
                g = stages(i, u)[3]
                if g is not None:
                    sp.wait_ge(s_xn2, g + 1)
                    sp.dma_start(hr_by_seq[:, ds(GS * g, GS), :], hr[:, (u + 1) % 2, :, :]).then_inc(s_st[(u + 1) % 2], 16)
            pipeline(sp, body)

            sp.wait_ge(s_free, 1)
            load_experts(sp, (w1a_u, w1b_u, w2s_u, b2s_u), ("w1u", "w2u", "b2u"), s_wu)
            experts_sp(sp, 0)
            experts_sp(sp, 1)

        @block.gpsimd
        def _(pool):
            chain = [0]

            def link(ins):
                chain[0] += 1
                ins.then_inc(c_pool, 1)
                pool.wait_ge(c_pool, chain[0])

            nc.gpsimd.memset(fill[:, :], DUMMY)
            link(nc.gpsimd.memset(zrow[:, :], 0.0))
            nc.gpsimd.memset(xids[:, SEQS:SEQS + GS], 0)
            nc.gpsimd.memset(neghalf[:, :], -0.5)
            nc.gpsimd.iota(tok[:, :], pattern=[[L, SEQS]], base=0, channel_multiplier=1)
            link(nc.gpsimd.memset(ones[:, :], 1.0))
            for t_, off, mul, pat in ((le, 0, -1, 1), (lt, -1, -1, 1), (gt, -1, 1, -1)):
                nc.gpsimd.affine_select(out=t_[:, :], in_=ones[:, :], compare_op=ALU.is_ge, fill=0.0, base=off,
                                        pattern=[[pat, P]], channel_multiplier=mul)
            link(nc.gpsimd.affine_select(out=ident[:, :], in_=ones[:, :], compare_op=ALU.is_equal, fill=0.0, base=0,
                                         pattern=[[-1, P]], channel_multiplier=1))
            for e in range(NE):
                last = nc.gpsimd.memset(acc[:, 0, e:e + 1], float(e * LIST // P))
            for s_ in (s_oh, s_el, s_dest, s_scd, *s_st):
                pool.sem_inc(s_, CREDIT)
            last.then_inc(s_const, 1)
            pool.wait_ge(s_const, 1)
            pool.wait_ge(s_wa, n_wa)

            def gather(g, u):
                p = u % 2
                wait_apart(pool, s_ve, g - 1, marks_pool)
                nc.gpsimd.tensor_copy(gidx[:, p, :], xids[:, ds(GS * g, GS)]).then_inc(s_idx, 1)
                wait_apart(pool, s_idx, g + 1, marks_pool)
                for j in range(GS):
                    nc.gpsimd.indirect_dma_start(
                        out=gath[:, p, j, :], out_offset=None, in_=A["table"][:, :],
                        in_offset=bass.IndirectOffsetOnAxis(ap=gidx[:, p, j:j + 1], axis=0)).then_inc(s_gath[p], 16)

            def body(i, u):
                g1, g2, g3, g4, g5 = stages(i, u)
                if g1 is not None:
                    gather(g1 + 1, u + 1)
                    wait_apart(pool, s_ve, g1 + 1, marks_pool)
                    nc.gpsimd.tensor_tensor(rstd1[:, u % 2, :], ve1[:, u % 2, :], neghalf[:, :], ALU.pow).then_inc(s_rstd, 1)
                if g4 is not None:
                    wait_apart(pool, s_ms, g4 + 1, marks_pool)
                    nc.gpsimd.tensor_tensor(rs[:, :], ms[:, :], neghalf[:, :], ALU.pow).then_inc(s_rs, 1)
                    wait_apart(pool, s_ve2, g4 + 1, marks_pool)
                    nc.gpsimd.tensor_tensor(rstd2[:, :], ve2[:, :], neghalf[:, :], ALU.pow).then_inc(s_rstd2, 1)
                if g3 is not None:
                    p = u % 2
                    wait_apart(pool, s_dt, g3 + 1, marks_pool)
                    for j in range(GS):
                        wait_apart(pool, s_sg, GS * g3 + j - 1, marks_pool)
                        for h in range(HEADS):
                            last = nc.gpsimd.tensor_scalar(seg_l[:, j % 2, h, :], gt[:, :], dta[:, p, j, h:h + 1],
                                                           1.0, ALU.mult, ALU.mult)
                        last.then_inc(s_sl, 1)
                if g5 is not None:
                    p = u % 2
                    wait_apart(pool, s_dest, CREDIT + g5 + 1, marks_pool)
                    for j in range(GS):
                        nc.gpsimd.indirect_dma_start(
                            out=list_c[:, :], out_offset=bass.IndirectOffsetOnAxis(ap=desti[:, p, j:j + 1], axis=0),
                            in_=toki[:, p, j:j + 1], in_offset=None).then_inc(s_sc[p], 16)
                if g1 is not None:
                    wait_apart(pool, s_xn, g1 + 1, marks_pool)
                    wait_apart(pool, s_h1, 2 * (g1 - 3), marks_pool)
                    nc.gpsimd.tensor_tensor(hx[:, u % 4, :, :], h0[:, :, :], xn[:, :, :], ALU.add).then_inc(s_hx, 1)
                if g5 is not None:
                    wait_apart(pool, s_sc[u % 2], 64 * (earlier(i, u, 4) + 1), marks_pool)
                    pool.sem_inc(s_scd, 1)

            gather(0, 0)
            wait_apart(pool, s_fill, 48, marks_pool)
            pipeline(pool, body)

            wait_apart(pool, s_slot, 1, marks_pool)

            def list_dropped(i, p):
                wait_apart(pool, s_su[p], 64 * i, marks_pool)
                g = 2 * i + p
                nc.gpsimd.tensor_copy(slot4[:, p, :], slot_u[:, ds(GS * g, GS)])
                nc.gpsimd.tensor_copy(tok4[:, p, :], tok[:, ds(GS * g, GS)]).then_inc(s_s4, 1)
                wait_apart(pool, s_s4, g + 1, marks_pool)
                for j in range(GS):
                    nc.gpsimd.indirect_dma_start(
                        out=list_u[:, :], out_offset=bass.IndirectOffsetOnAxis(ap=slot4[:, p, j:j + 1], axis=0),
                        in_=tok4[:, p, j:j + 1], in_offset=None,
                        bounds_check=NE * LIST - 1, oob_is_err=False).then_inc(s_su[p], 16)

            for p in range(2):
                list_dropped(0, p)
            with pool.Fori(1, NG // 2) as i:
                for p in range(2):
                    list_dropped(i, p)

            def experts(m):
                def gather_tile(i, u, t):
                    wait_apart(pool, f_id[u], 16 * (I0[m] + i + 1), marks_pool)
                    nc.gpsimd.indirect_dma_start(
                        out=xg[:, u, :], out_offset=None, in_=hr_dram[:, :],
                        in_offset=bass.IndirectOffsetOnAxis(ap=ids[:, u, :], axis=0)).then_inc(f_g[u], 16)
                    if m == 1:
                        nc.gpsimd.indirect_dma_start(
                            out=og[:, u, :], out_offset=None, in_=out_rows,
                            in_offset=bass.IndirectOffsetOnAxis(ap=ids[:, u, :], axis=0),
                            bounds_check=NT - 1, oob_is_err=False).then_inc(f_g[u], 16)

                def scatter_tile(u, t):
                    wait_apart(pool, f_o, T0[m] + t + 1, marks_pool)
                    nc.gpsimd.indirect_dma_start(
                        out=out_rows, out_offset=bass.IndirectOffsetOnAxis(ap=ids[:, u, :], axis=0),
                        in_=osb[:, u, :], in_offset=None, bounds_check=NT - 1, oob_is_err=False).then_inc(f_s[u], 16)

                def body(i, u, t):
                    gather_tile(i, u, t)
                    if not (isinstance(t, int) and t < 2):
                        scatter_tile((u - 2) % UT, t - 2)
                tiles(pool, m, body)
                n = TURNS[m] * UT
                for t in (n - 2, n - 1):
                    scatter_tile(t % UT, t)
                for u in range(UT):
                    wait_apart(pool, f_s[u], 16 * (I0[m] + TURNS[m]), marks_pool)

            for p in range(2):
                wait_apart(pool, s_st[p], CREDIT + 16 * (NG // 2), marks_pool)
            experts(0)
            experts(1)

        @block.scalar
        def _(act):
            act.wait_ge(s_wa, n_wa)
            nc.scalar.activation(nega[:, :], nega[:, :], ACT.Exp).then_inc(s_pe_, 1)
            nc.scalar.activation(gate[:, :], gate[:, :], ACT.Exp, scale=-1.0).then_inc(s_sig, 1)

            def body(i, u):
                g1, g2, g3, g4, g5 = stages(i, u)
                if g4 is not None:
                    p = (u + 1) % 2
                    act.wait_ge(s_y2, g4 + 1)
                    wait(act, s_ssq, g4)
                    nc.scalar.activation(ysq[:, :, :], ybuf[:, p, :, :], ACT.Square).then_inc(s_sq, 1)
                if g5 is not None:
                    act.wait_ge(s_d, g5 + 1)
                    wait(act, s_oh, CREDIT + g5)
                    nc.scalar.activation(el[:, :, :, :], dl[:, :, :, :], ACT.Exp).then_inc(s_el, 1)
                if g3 is not None:
                    p = u % 2
                    act.wait_ge(s_dab, g3 + 1)
                    nc.scalar.activation(dtu[:, p, :, :], dab[:, p, :, :], ACT.Exp, scale=-1.0).then_inc(s_u, 1)
                    for j in range(GS):
                        act.wait_ge(s_sg, GS * g3 + j + 1)
                        wait(act, s_m, GS * g3 + j - 1)
                        nc.scalar.activation(dec[:, j % 2, 0:3, :], sg0[:, 0:3 * P].rearrange("p (h s) -> p h s", h=3), ACT.Exp)
                        nc.scalar.activation(dec[:, j % 2, 3:6, :], sg1[:, 0:3 * P].rearrange("p (h s) -> p h s", h=3),
                                             ACT.Exp).then_inc(s_e, 1)
                if g4 is not None:
                    for half, (dst_, rows) in enumerate(((x2t_a, P), (x2t_b, DB))):
                        act.wait_ge(s_tr2, 2 * g4 + half + 1)
                        wait(act, s_rt, g4)
                        nc.scalar.copy(dst_[:, :], tp[0:rows, :]).then_inc(s_x2t, 1)
                if g1 is not None:
                    for half, (dst_, rows) in enumerate(((xt_a, P), (xt_b, DB))):
                        act.wait_ge(s_tr1, 2 * g1 + half + 1)
                        wait(act, s_mm, (XT + ZT) * (g1 - 1))
                        nc.scalar.copy(dst_[:, u % 2, :], tp[0:rows, :]).then_inc(s_xt, 1)
                if g2 is not None:
                    p = (u + 1) % 2
                    wait(act, s_y2, g2 - 1)

                    def start(m):
                        act.wait_ge(s_mm, (XT + ZT) * g2 + m + 1)
                        nc.scalar.activation(xbc[:, p, m, :], mm[m % 2][:, :], ACT.Identity, bias=cb[:, m:m + 1],
                                             scale=cw[:, m, TAPS - 1:TAPS]).then_inc(s_ci, 1)

                    def silu(m):
                        act.wait_ge(s_cv, XT * g2 + m + 1)
                        nc.scalar.activation(xbc[:, p, m, :], xbc[:, p, m, :], ACT.Silu).then_inc(s_xbc, 1)

                    def gate_z(m):
                        act.wait_ge(s_mm, (XT + ZT) * g2 + m + 1)
                        nc.scalar.activation(zs[:, p, m - XT, :], mm[m % 2][:, :], ACT.Silu).then_inc(s_z, 1)

                    start(0)
                    for m in range(1, XT):
                        start(m)
                        silu(m - 1)
                    gate_z(XT)
                    silu(XT - 1)
                    gate_z(XT + 1)
                    gate_z(XT + 2)

            pipeline(act, body)

            def experts(m):
                def body(i, u, t):
                    T = T0[m] + t
                    act.wait_ge(f_t, T + 1)
                    wait(act, f_m1, 2 * (T - 1))
                    nc.scalar.copy(fx_a[:, u % 2, :], tp[:, 0:P])
                    nc.scalar.copy(fx_b[0:DB, u % 2, :], tp[0:DB, P:2 * P]).then_inc(f_x, 1)
                    wait(act, f_h, 2 * (T - 1))
                    for n, b in enumerate((mm0, mm1)):
                        act.wait_ge(f_m1, 2 * T + n + 1)
                        nc.scalar.activation(hg[:, u % 2, n * FH:(n + 1) * FH], b[:, 0:FH], ACT.Gelu).then_inc(f_ge, 1)
                tiles(act, m, body)
            experts(0)
            experts(1)

        @block.tensor
        def _(pe):
            mmul = nc.tensor.matmul
            pe.wait_ge(s_const, 1)
            pe.wait_ge(s_wa, n_wa)
            pe.wait_ge(s_prep, 1)

            def body(i, u):
                g1, g2, g3, g4, g5 = stages(i, u)

                def cap(v):
                    return min(v, NG) if isinstance(v, int) else v

                if g4 is not None:
                    p = (u + 1) % 2
                    pe.wait_ge(s_sq, g4 + 1)
                    wait(pe, s_ms, g4)
                    for j in range(GS):
                        for c in range(ZT):
                            last = mmul(misc[:, SQC + j:SQC + j + 1], ysq[:, c, j * L:(j + 1) * L], ones[:, 0:1],
                                        start=(c == 0), stop=(c == ZT - 1))
                    last.then_inc(s_ssq, 1)
                    for q in range(2):
                        wait(pe, s_z, ZT * cap(g4 + 2) - 1 + q)
                        wait(pe, s_h1, 2 * g4 - 1 + q)
                        for j in range(2):
                            for c in range(ZT):
                                last = mmul(mm[q][:, j * D:(j + 1) * D], ybuf[:, p, c, (2 * q + j) * L:(2 * q + j + 1) * L],
                                            wo[:, c, :], start=(c == 0), stop=(c == ZT - 1))
                        last.then_inc(s_o, 1)
                if g3 is not None:
                    p = u % 2

                    def seg(j):
                        pe.wait_ge(s_sl, GS * g3 + j + 1)
                        wait(pe, s_e, GS * g3 + j)
                        for h in range(HEADS):
                            last = mmul((sg0, sg1)[h // 3][:, (h % 3) * P:(h % 3 + 1) * P], seg_l[:, j % 2, h, :], le[:, :],
                                        start=True, stop=True)
                        last.then_inc(s_sg, 1)

                    def cbx(j):
                        wait(pe, s_xd, GS * g3 + j)
                        js = slice(j * L, (j + 1) * L)
                        mmul(cx[:, 0:P], xbc[:, p, ZT, js], xbc[:, p, ZT + 1, js], start=True, stop=True)
                        for c in range(ZT):
                            last = nc.tensor.transpose(cx[:, (c + 1) * P:(c + 2) * P], xbc[:, p, c, js], ident[:, :])
                        last.then_inc(s_cx, 1)

                    def y(j):
                        pe.wait_ge(s_m, GS * g3 + j + 1)
                        wait(pe, s_yd, GS * g3 + j)
                        for h in range(HEADS):
                            r = (h % 2) * HD
                            last = mmul(yb[r:r + HD, (h // 2) * P:(h // 2 + 1) * P], xd[:, j % 2, h * HD:(h + 1) * HD],
                                        mix[:, j % 2, h, :], start=True, stop=True)
                        last.then_inc(s_yp, 1)

                    pe.wait_ge(s_xbc, XT * (g3 + 1))
                    for j in range(GS):
                        seg(j)
                        cbx(j)
                        if j:
                            y(j - 1)
                    y(GS - 1)
                if g5 is not None:
                    pe.wait_ge(s_oh, CREDIT + g5 + 1)
                    wait(pe, s_dest, CREDIT + g5)
                    mmul(misc[:, PFC:PFC + GS * NE], lt[:, :], oh[:, :, 0, :], start=True, stop=False)
                    mmul(misc[:, PFC:PFC + GS * NE], ones[:, :], acc[:, 0:GS, :], start=False, stop=True).then_inc(s_pf, 1)
                if g4 is not None:
                    pe.wait_ge(s_xn2, g4 + 1)
                    p = (u + 1) % 2
                    wait(pe, s_xt, 2 * cap(g4 + 3))
                    wait(pe, s_x2t, 2 * g4)
                    for j in range(GS):
                        last = nc.tensor.transpose(tp[:, j * L:(j + 1) * L], hr[:, p, j, D:D + P], ident[:, :])
                    last.then_inc(s_tr2, 1)
                    wait_apart(pe, s_x2t, 2 * g4 + 1, marks_pe)
                    for j in range(GS):
                        last = nc.tensor.transpose(tp[0:DB, j * L:(j + 1) * L], hr[:, p, j, D + P:2 * D], ident[:, :])
                    last.then_inc(s_tr2, 1)
                    pe.wait_ge(s_x2t, 2 * g4 + 2)
                    wait(pe, s_d, g4)
                    for j in range(GS):
                        o = misc[:, RTC + j * 2 * NE:RTC + (j + 1) * 2 * NE]
                        mmul(o, x2t_a[:, j * L:(j + 1) * L], wr_a[:, :], start=True, stop=False)
                        last = mmul(o, x2t_b[:, j * L:(j + 1) * L], wr_b[:, :], start=False, stop=True)
                    last.then_inc(s_rt, 1)
                if g1 is not None:
                    pe.wait_ge(s_xn, g1 + 1)
                    wait(pe, s_x2t, 2 * (g1 - 2))
                    wait(pe, s_xt, 2 * g1)
                    for j in range(GS):
                        last = nc.tensor.transpose(tp[:, j * L:(j + 1) * L], xn[:, j, 0:P], ident[:, :])
                    last.then_inc(s_tr1, 1)
                    wait_apart(pe, s_xt, 2 * g1 + 1, marks_pe)
                    for j in range(GS):
                        last = nc.tensor.transpose(tp[0:DB, j * L:(j + 1) * L], xn[:, j, P:D], ident[:, :])
                    last.then_inc(s_tr1, 1)
                if g2 is not None:
                    p = (u + 1) % 2
                    pe.wait_ge(s_xt, 2 * (g2 + 1))
                    wait(pe, s_dab, g2)
                    for j in range(GS):
                        o = misc[:, DTC + j * HEADS:DTC + (j + 1) * HEADS]
                        js = slice(j * L, (j + 1) * L)
                        mmul(o, xt_a[:, p, js], win_a[:, PROJ - HEADS:PROJ], start=True, stop=False)
                        last = mmul(o, xt_b[:, p, js], win_b[:, PROJ - HEADS:PROJ], start=False, stop=True)
                    last.then_inc(s_dtp, 1)
                    for m in range(XT + ZT):
                        if m < 2:
                            wait(pe, s_h1, 2 * (g2 - 2) + m + 1)
                            wait(pe, s_z, ZT * (g2 - 1) + m + 2)
                        elif m - 2 < XT:
                            pe.wait_ge(s_cv, XT * g2 + m - 1)
                        else:
                            pe.wait_ge(s_z, ZT * g2 + m - 1 - XT)
                        c0 = INNER + m * P if m < XT else (m - XT) * P
                        mmul(mm[m % 2][:, :], win_a[:, c0:c0 + P], xt_a[:, p, :], start=True, stop=False)
                        mmul(mm[m % 2][:, :], win_b[:, c0:c0 + P], xt_b[:, p, :], start=False, stop=True).then_inc(s_mm, 1)

            pipeline(pe, body)

            def count(rhs_ins, k):
                pe.wait_ge(s_cmp, k)
                for n, (l_, r_) in enumerate(rhs_ins):
                    last = mmul(sg0[:, 0:NE * SEQS], l_, r_, start=(n == 0), stop=(n == len(rhs_ins) - 1))
                last.then_inc(s_cnt, 1)

            pe.wait_ge(s_cmp, 1)
            mmul(sg1[:, 0:NE], ones[:, :], acc[:, 0, :], start=True, stop=True).then_inc(s_cnt, 1)
            with pe.Fori(0, BITS) as k:
                pe.wait_ge(s_cmp, k + 2)
                mmul(sg0[:, 0:NE * SEQS], ones[:, :], cmp_[:, :, :], start=True, stop=True).then_inc(s_cnt, 1)
            count([(ones[:, :], cmp_[:, :, :])], BITS + 2)
            count([(lt[:, :], eqk[:, :, :]), (ones[:, :], scn[:, :, :])], BITS + 3)
            count([(lt[:, :], cmp_[:, :, :]), (ones[:, :], scn[:, :, :])], BITS + 4)
            pe.wait_ge(s_cmp, BITS + 4)
            mmul(sg1[:, 0:NE], ones[:, :], tot[:, :], start=True, stop=True).then_inc(s_cnt, 1)

            def experts(m):
                table = (tile_c, tile_u)[m]
                w1a_, w1b_, w2_, b2_ = ((w1a, w1b, w2s, b2s), (w1a_u, w1b_u, w2s_u, b2s_u))[m]

                def hidden_transposed(T, u):
                    for n in range(2):
                        pe.wait_ge(f_ge, 2 * T + n + 1)
                        wait(pe, f_ht, 2 * (T - 1) + n + 1)
                        for c in range(3):
                            last = nc.tensor.transpose((sg0, sg1)[n][:, c * P:(c + 1) * P],
                                                       hg[:, u % 2, (3 * n + c) * P:(3 * n + c + 1) * P], ident[:, :])
                        last.then_inc(f_h, 1)

                def out_product(t, u):
                    T = T0[m] + t
                    e = pe.value_load(table[0:1, 1, ds(t, 1)], min_val=0, max_val=NE - 1)
                    pe.wait_ge(f_ht, 2 * T + 2)
                    wait(pe, f_o, T)
                    for c in range(FC):
                        mmul(cx[:, 0:D], ht[:, u % 2, c * P:(c + 1) * P], w2_[:, ds(e * (FC * D) + c * D, D)],
                             start=(c == 0), stop=False)
                    mmul(cx[:, 0:D], ones[0:1, :], b2_[:, ds(e * D, D)], start=False, stop=True).then_inc(fm2, 1)

                def body(i, u, t):
                    T = T0[m] + t
                    first = isinstance(t, int) and t == 0
                    pe.wait_ge(f_g[u], (16 * (i + 1)) if m == 0 else 16 * I0[1] + 32 * (i + 1))
                    wait(pe, f_x, T)
                    nc.tensor.transpose(tp[:, 0:P], xg[:, u, D:D + P], ident[:, :])
                    nc.tensor.transpose(tp[0:DB, P:2 * P], xg[:, u, D + P:2 * D], ident[:, :]).then_inc(f_t, 1)
                    if not first:
                        hidden_transposed(T - 1, u - 1)
                    e = pe.value_load(table[0:1, 1, ds(t, 1)], min_val=0, max_val=NE - 1)
                    pe.wait_ge(f_x, T + 1)
                    for n in range(2):
                        wait(pe, f_ge, 2 * (T - 1) + n + 1)
                        mmul(mm[n][:, 0:FH], fx_a[:, u % 2, :], w1a_[:, ds(e * F + n * FH, FH)], start=True, stop=False)
                        mmul(mm[n][:, 0:FH], fx_b[:, u % 2, :], w1b_[:, ds(e * F + n * FH, FH)],
                             start=False, stop=True).then_inc(f_m1, 1)
                    if not first:
                        out_product(t - 1, u - 1)

                tiles(pe, m, body)
                n = TURNS[m] * UT
                hidden_transposed(T0[m] + n - 1, n - 1)
                out_product(n - 1, n - 1)

            pe.wait_ge(s_wc, 16 * 7)
            pe.wait_ge(s_tab, 2)
            experts(0)
            pe.wait_ge(s_wu, 16 * 7)
            experts(1)

        @block.vector
        def _(dve):
            v = nc.vector
            ts, tt, stt = v.tensor_scalar, v.tensor_tensor, v.scalar_tensor_tensor
            n_setup = [0]

            def link(ins):
                n_setup[0] += 1
                ins.then_inc(c_setup, 1)
                dve.wait_ge(c_setup, n_setup[0])

            dve.wait_ge(s_sig, 1)
            link(ts(gate[:, :], gate[:, :], 1.0, None, ALU.add))
            link(v.reciprocal(gate[:, :], gate[:, :]))
            for c in range(ZT):
                ts(wo[:, c, :], wo[:, c, :], nw[:, c:c + 1], gate[:, 0:1], ALU.mult, ALU.mult)
            ts(nega[:, :], nega[:, :], -1.0, None, ALU.mult).then_inc(s_prep, 1)
            dve.wait_ge(s_prep, 1)
            dve.wait_ge(s_const, 1)

            def norm_stats(x, st, mv, ve, link):
                for j in range(GS):
                    last = v.bn_stats(st[:, j, :], x(j))
                link(last, marks_dve)
                for j in range(GS):
                    last = v.bn_aggr(mv[:, j, :], st[:, j, :])
                link(last)
                return ts(ve, mv[:, :, 1], LNEPS, None, ALU.add)

            def body(i, u):
                g1, g2, g3, g4, g5 = stages(i, u)
                if g1 is not None:
                    p = u % 2
                    link = Chain(dve, ch["quant"], g1, STEPS["quant"])
                    dve.wait_ge(s_gath[p], 64 * (earlier(i, u, 0) + 1))
                    link(v.tensor_reduce(q1[:, 0, :], gath[:, p, :, :], AX.X, ALU.max, apply_absolute_value=True))
                    link(ts(q1[:, 1, :], q1[:, 0, :], 1.0 / QMAX, QEPS, ALU.mult, ALU.max))
                    link(v.reciprocal(q1[:, 2, :], q1[:, 1, :]))
                    wait(dve, s_hx, g1)
                    for j in range(GS):
                        last = ts(h0[:, j, :], gath[:, p, j, :], q1[:, 2, j:j + 1], MAGIC, ALU.mult, ALU.add)
                    link(last)
                    last = ts(h0[:, :, :], h0[:, :, :], MAGIC, QMAX, ALU.subtract, ALU.min)
                    link(last)
                    for j in range(GS):
                        last = ts(h0[:, j, :], h0[:, j, :], -QMAX, q1[:, 1, j:j + 1], ALU.max, ALU.mult)
                    link(last)
                    norm_stats(lambda j: h0[:, j, :], st1, mv1, ve1[:, p, :], link).then_inc(s_ve, 1)
                    link.end()
                if g4 is not None:
                    p = (u + 1) % 2
                    link = Chain(dve, ch["h1"], g4, STEPS["h1"])
                    dve.wait_ge(s_ssq, g4 + 1)
                    ts(ms[:, :], misc[:, SQC:SQC + GS], 1.0 / INNER, LNEPS, ALU.mult, ALU.add).then_inc(s_ms, 1)
                    dve.wait_ge(s_rs, g4 + 1)
                    dve.wait_ge(s_hx, g4 + 1)
                    wait(dve, s_st[p], CREDIT + 16 * earlier(i, u, 3))
                    for q in range(2):
                        dve.wait_ge(s_o, 2 * g4 + q + 1)
                        for j in range(2):
                            last = stt(out=hr[:, p, 2 * q + j, 0:D], in0=mm[q][:, j * D:(j + 1) * D],
                                       scalar=rs[:, 2 * q + j:2 * q + j + 1], in1=hx[:, (u + 1) % 4, 2 * q + j, :],
                                       op0=ALU.mult, op1=ALU.add)
                        last.then_inc(s_h1, 1)
                    dve.wait_ge(s_h1, 2 * g4 + 2)
                    norm_stats(lambda j: hr[:, p, j, 0:D], st2, mv2, ve2[:, :], link).then_inc(s_ve2, 1)
                    link.end()
                if g5 is not None:
                    link = Chain(dve, ch["pick1"], g5, STEPS["pick1"])
                    dve.wait_ge(s_rt, g5 + 1)
                    wait(dve, s_el, CREDIT + g5)
                    link(tt(lg[:, :, :, :].rearrange("p j r e -> p j (r e)"),
                            misc[:, RTC:RTC + GS * 2 * NE].rearrange("p (j n) -> p j n", j=GS),
                            rb[:, :].unsqueeze(1).broadcast_to([P, GS, 2 * NE]), ALU.add))
                    link(v.tensor_reduce(m8[:, :, :], lg[:, :, :, :], AX.X, ALU.max))
                    tt(dl[:, :, :, :].rearrange("p j r e -> p (j r) e"), lg[:, :, :, :].rearrange("p j r e -> p (j r) e"),
                       m8[:, :, :].rearrange("p j r -> p (j r)").unsqueeze(2).broadcast_to([P, GS * 2, NE]),
                       ALU.subtract).then_inc(s_d, 1)
                    link.end()
                if g3 is not None:
                    p = u % 2
                    link = Chain(dve, ch["soft"], g3, STEPS["soft"])
                    flat = lambda t_: t_.rearrange("p j h -> p (j h)")
                    U, DTR, DTS, DTA = flat(dtu[:, p, :, :]), flat(dtr[:, p, :, :]), flat(dts[:, p, :, :]), flat(dta[:, p, :, :])
                    S1, S2, S3 = flat(sp1[:, :, :]), flat(sp2[:, :, :]), flat(sp3[:, :, :])
                    dve.wait_ge(s_u, g3 + 1)
                    link(ts(S1, U, 2.0, None, ALU.add))
                    link(v.reciprocal(S2, S1))
                    link(tt(S1, S2, U, ALU.mult))
                    link(tt(S2, S1, S1, ALU.mult))
                    link(ts(S3, S2, 1.0 / 15, None, ALU.mult))
                    for d in (13, 11, 9, 7, 5, 3):
                        link(stt(out=S3, in0=S3, scalar=1.0 / d, in1=S2, op0=ALU.add, op1=ALU.mult))
                    link(stt(out=S3, in0=S3, scalar=1.0, in1=S1, op0=ALU.add, op1=ALU.mult))
                    ts(S2, DTR, 0.0, None, ALU.max)
                    link(ts(S3, S3, 2.0, None, ALU.mult))
                    link.end()
                    tt(DTS, S3, S2, ALU.add).then_inc(s_dts, 1)
                    dve.wait_ge(s_dts, g3 + 1)
                    tt(dta[:, p, :, :], dts[:, p, :, :], nega[:, :].unsqueeze(1).broadcast_to([P, GS, HEADS]),
                       ALU.mult).then_inc(s_dt, 1)
                    wait(dve, s_o, 2 * (g3 - 1))
                    link = Chain(dve, ch["ssd"], g3, STEPS["ssd"])

                    def weights(j):
                        dve.wait_ge(s_cx, GS * g3 + j + 1)
                        link(tt(cbm[:, :], cx[:, 0:P], le[:, :], ALU.mult))
                        wait(dve, s_yp, GS * g3 + j - 1)
                        tt(xd[:, j % 2, :].rearrange("p (h n) -> p h n", h=HEADS),
                           cx[:, P:4 * P].rearrange("p (h n) -> p h n", h=HEADS),
                           dts[:, p, j, :].unsqueeze(2).broadcast_to([P, HEADS, HD]), ALU.mult).then_inc(s_xd, 1)
                        dve.wait_ge(s_e, GS * g3 + j + 1)
                        tt(mix[:, j % 2, :, :], dec[:, j % 2, :, :], cbm[:, :].unsqueeze(1).broadcast_to([P, HEADS, P]),
                           ALU.mult).then_inc(s_m, 1)

                    def y(j):
                        dve.wait_ge(s_yp, GS * g3 + j + 1)
                        for c in range(ZT):
                            js = slice(j * L, (j + 1) * L)
                            last = stt(out=ybuf[:, p, c, js], in0=xbc[:, p, c, js], scalar=dskip[:, c:c + 1],
                                       in1=yb[:, c * P:(c + 1) * P], op0=ALU.mult, op1=ALU.add)
                        last.then_inc(s_yd, 1)

                    for j in range(GS):
                        weights(j)
                        dve.wait_ge(s_m, GS * g3 + j + 1)
                        if j:
                            y(j - 1)
                    y(GS - 1)
                    link.end()
                    dve.wait_ge(s_yd, GS * (g3 + 1))
                    dve.wait_ge(s_z, ZT * (g3 + 1))
                    tt(ybuf[:, p, :, :].rearrange("p c t -> p (c t)"), ybuf[:, p, :, :].rearrange("p c t -> p (c t)"),
                       zs[:, p, :, :].rearrange("p c t -> p (c t)"), ALU.mult).then_inc(s_y2, 1)
                if g5 is not None:
                    p = u % 2
                    link = Chain(dve, ch["pick2"], g5, STEPS["pick2"])
                    r8 = lambda t_: t_[:, :, :, :].rearrange("p j r e -> p (j r) e")
                    b8 = lambda t_: t_[:, :, :].rearrange("p j r -> p (j r)").unsqueeze(2).broadcast_to([P, GS * 2, NE])
                    dve.wait_ge(s_el, CREDIT + g5 + 1)
                    wait(dve, s_dest, CREDIT + g5)
                    link(v.tensor_reduce(e8[:, :, :], el[:, :, :, :], AX.X, ALU.max))
                    v.tensor_reduce(s8[:, :, :], el[:, :, :, :], AX.X, ALU.add)
                    link(tt(r8(pk), r8(el), b8(e8), ALU.is_equal))
                    link(tt(r8(pk), r8(pk), w4[:, :].unsqueeze(1).broadcast_to([P, GS * 2, NE]), ALU.mult))
                    link(v.tensor_reduce(m8[:, :, :], pk[:, :, :, :], AX.X, ALU.max))
                    link(tt(r8(oh), r8(pk), b8(m8), ALU.is_equal))
                    link(v.reciprocal(s8[:, :, :], s8[:, :, :]))
                    tt(conf[:, ds(GS * g5, GS)], s8[:, :, 0], e8[:, :, 0], ALU.mult)
                    v.tensor_copy(ohc[:, ds(GS * g5, GS), :], oh[:, :, 0, :])
                    v.tensor_copy(ohu[:, ds(GS * g5, GS), :], oh[:, :, 1, :])
                    for j in range(GS):
                        ins = tt(acc[:, j + 1, :], acc[:, j, :], oh[:, j, 0, :], ALU.add)
                        if j < GS - 1:
                            link(ins)
                    ins.then_inc(s_oh, 1)
                    dve.wait_ge(s_pf, g5 + 1)
                    link(tt(dst[:, :, :], misc[:, PFC:PFC + GS * NE].rearrange("p (j e) -> p j e", j=GS), oh[:, :, 0, :],
                            ALU.mult))
                    link(v.tensor_reduce(dest[:, :], dst[:, :, :], AX.X, ALU.add))
                    link.end()
                    wait(dve, s_scd, CREDIT + g5 - 1)
                    v.tensor_copy(acc[:, 0, :], acc[:, GS, :])
                    v.tensor_copy(desti[:, p, :], dest[:, :])
                    v.tensor_copy(toki[:, p, :], tok[:, ds(GS * g5, GS)]).then_inc(s_dest, 1)
                if g4 is not None:
                    p = (u + 1) % 2
                    dve.wait_ge(s_rstd2, g4 + 1)
                    for j in range(GS):
                        last = ts(hr[:, p, j, D:2 * D], hr[:, p, j, 0:D], mv2[:, j, 0:1], rstd2[:, j:j + 1],
                                  ALU.subtract, ALU.mult)
                    last.then_inc(s_xn2, 1)
                if g1 is not None:
                    dve.wait_ge(s_rstd, g1 + 1)
                    wait(dve, s_tr1, 2 * g1)
                    for j in range(GS):
                        last = ts(xn[:, j, :], h0[:, j, :], mv1[:, j, 0:1], rstd1[:, u % 2, j:j + 1], ALU.subtract, ALU.mult)
                    last.then_inc(s_xn, 1)
                if g2 is not None:
                    p = (u + 1) % 2
                    dve.wait_ge(s_dtp, g2 + 1)
                    link = Chain(dve, ch["dt0"], g2, STEPS["dt0"])
                    link(tt(dtr[:, p, :, :], misc[:, DTC:DTC + GS * HEADS].rearrange("p (j h) -> p j h", j=GS),
                            dtb[:, :].unsqueeze(1).broadcast_to([P, GS, HEADS]), ALU.add))
                    link.end()
                    x_ = dtr[:, p, :, :].rearrange("p j h -> p (j h)")
                    stt(out=dab[:, p, :, :].rearrange("p j h -> p (j h)"), in0=x_, scalar=-1.0, in1=x_,
                        op0=ALU.mult, op1=ALU.max).then_inc(s_dab, 1)
                    link = Chain(dve, ch["tap"], g2, STEPS["tap"])
                    for m in range(XT):
                        dve.wait_ge(s_ci, XT * g2 + m + 1)
                        src = mm[m % 2][:, :].rearrange("p (j t) -> p j t", j=GS)
                        dst_ = xbc[:, p, m, :].rearrange("p (j t) -> p j t", j=GS)
                        for back in range(1, TAPS):
                            ins = stt(out=dst_[:, :, back:L], in0=src[:, :, 0:L - back],
                                      scalar=cw[:, m, TAPS - 1 - back:TAPS - back], in1=dst_[:, :, back:L],
                                      op0=ALU.mult, op1=ALU.add)
                            if back < TAPS - 1:
                                link(ins)
                        ins.then_inc(s_cv, 1)
                    link.end()

            pipeline(dve, body)
            for p in range(2):
                dve.wait_ge(s_st[p], CREDIT + 16 * (NG // 2))
                dve.wait_ge(s_sc[p], 64 * (NG // 2))
            dve.wait_ge(s_gath[0], 64 * (NG // 2 + 1))
            dve.wait_ge(s_dest, CREDIT + NG)
            dve.sem_inc(s_free, 1)

            nf = [0]

            def link(ins):
                nf[0] += 1
                ins.then_inc(c_find, 1)
                dve.wait_ge(c_find, nf[0])

            link(v.memset(fx_b[DB:DB + 1, :, :], 1.0))
            link(v.memset(zero[:, :], 0.0))
            v.memset(og[:, :, :], 0.0)
            v.memset(step[:, :], 1.0)
            link(v.tensor_copy(trow[:, 0, :], iota[:, :]))
            v.memset(thr[:, :], 0.0).then_inc(s_cmp, 1)
            dve.wait_ge(s_cnt, 1)

            def tile_table(table, n, counts):
                link(tt(lst[:, 0, :], counts, base_e[:, :], ALU.subtract))
                link(ts(lst[:, 1, :], lst[:, 0, :], float(P - 1), 1.0 / P, ALU.add, ALU.mult))
                link(ts(lst[:, 1, :], lst[:, 1, :], 0.5 - 0.5 / P, MAGIC, ALU.subtract, ALU.add))
                link(ts(lst[:, 1, :], lst[:, 1, :], MAGIC, None, ALU.subtract))
                link(v.tensor_copy(lst[:, 2, 0:1], lst[:, 1, 0:1]))
                for e in range(1, NE):
                    link(tt(lst[:, 2, e:e + 1], lst[:, 2, e - 1:e], lst[:, 1, e:e + 1], ALU.add))
                link(ts(lst[:, 3, :], lst[:, 1, :], -float(P), float(LIST), ALU.mult, ALU.add))
                r = trow[:, :, 0:n]
                link(ts(r[:, 1, :], r[:, 0, :], float(P), None, ALU.mult))
                link(v.memset(r[:, 2, :], 0.0))
                for e in range(NE - 1):
                    link(ts(r[:, 3, :], r[:, 0, :], lst[:, 2, e:e + 1], None, ALU.is_ge))
                    link(tt(r[:, 2, :], r[:, 2, :], r[:, 3, :], ALU.add))
                    link(stt(out=r[:, 1, :], in0=r[:, 3, :], scalar=lst[:, 3, e:e + 1], in1=r[:, 1, :],
                             op0=ALU.mult, op1=ALU.add))
                v.tensor_copy(table[:, 0, :], r[:, 1, :])
                v.tensor_copy(table[:, 1, :], r[:, 2, :]).then_inc(s_tab, 1)

            tile_table(tile_c, CT, sg1[0:1, 0:NE])

            by_e = lambda t_: t_[:, :, :].rearrange("p b e -> p e b")
            confb = conf[:, :].unsqueeze(1).broadcast_to([P, NE, SEQS])
            eb = lambda t_: t_[:, :].unsqueeze(2).broadcast_to([P, NE, SEQS])
            link(tt(key[:, :, :], by_e(ohc), confb, ALU.mult))
            link(stt(out=key[:, :, :], in0=by_e(ohc), scalar=1.0, in1=key[:, :, :], op0=ALU.subtract, op1=ALU.add))
            f0 = nf[0]
            with dve.Fori(0, BITS) as k:
                link = Chain(dve, ch["find"], k, STEPS["find"])
                link(tt(cand[:, :], thr[:, :], step[:, :], ALU.add))
                tt(cmp_[:, :, :], key[:, :, :], eb(cand), ALU.is_ge).then_inc(s_cmp, 1)
                dve.wait_ge(s_cnt, k + 2)
                link(v.tensor_reduce(tot[:, :], sg0[:, 0:NE * SEQS].rearrange("p (e b) -> p e b", e=NE), AX.X, ALU.add))
                link(ts(tot[:, :], tot[:, :], float(CAP), None, ALU.is_ge))
                link(tt(tot[:, :], tot[:, :], step[:, :], ALU.mult))
                link(tt(thr[:, :], thr[:, :], tot[:, :], ALU.add))
                link(ts(step[:, :], step[:, :], 0.5, None, ALU.mult))
                link.end()
            nf[0] = f0

            def link(ins):
                nf[0] += 1
                ins.then_inc(c_find, 1)
                dve.wait_ge(c_find, nf[0])

            ps4 = sg0[:, 0:NE * SEQS].rearrange("p (e b) -> p e b", e=NE)
            tt(cmp_[:, :, :], key[:, :, :], eb(thr), ALU.is_gt).then_inc(s_cmp, 1)
            link(tt(eqk[:, :, :], key[:, :, :], eb(thr), ALU.is_equal))
            dve.wait_ge(s_cnt, BITS + 2)
            link(v.tensor_reduce(tot[:, :], ps4, AX.X, ALU.add))
            link(ts(need[:, :], tot[:, :], -1.0, float(CAP), ALU.mult, ALU.add))
            for e in range(NE):
                last = v.tensor_tensor_scan(out=scn[:, e, :], data0=eqk[:, e, :], data1=zero[:, :], initial=0.0,
                                            op0=ALU.add, op1=ALU.add)
            link(last)
            tt(scn[:, :, :], scn[:, :, :], eqk[:, :, :], ALU.subtract).then_inc(s_cmp, 1)
            dve.wait_ge(s_cnt, BITS + 3)
            link(tt(tmp[:, :, :], ps4, eb(need), ALU.is_lt))
            link(tt(tmp[:, :, :], tmp[:, :, :], eqk[:, :, :], ALU.mult))
            link(tt(tmp[:, :, :], tmp[:, :, :], cmp_[:, :, :], ALU.add))
            link(ts(tmp[:, :, :], tmp[:, :, :], -1.0, 1.0, ALU.mult, ALU.add))
            link(tt(tmp[:, :, :], tmp[:, :, :], by_e(ohc), ALU.mult))
            link(v.tensor_reduce(drop[:, :], tmp[:, :, :].rearrange("p e b -> p b e"), AX.X, ALU.add))
            link(tt(cmp_[:, :, :], by_e(ohu), drop[:, :].unsqueeze(1).broadcast_to([P, NE, SEQS]), ALU.mult))
            for e in range(NE):
                last = v.tensor_tensor_scan(out=scn[:, e, :], data0=cmp_[:, e, :], data1=zero[:, :],
                                            initial=float(e * LIST // P), op0=ALU.add, op1=ALU.add)
            link(last)
            link(v.tensor_copy(tot[:, :], scn[:, :, SEQS - 1]))
            tt(scn[:, :, :], scn[:, :, :], cmp_[:, :, :], ALU.subtract).then_inc(s_cmp, 1)
            dve.wait_ge(s_cnt, BITS + 4)
            link(tt(tmp[:, :, :], ps4, cmp_[:, :, :], ALU.mult))
            link(v.tensor_reduce(slotf[:, :], tmp[:, :, :].rearrange("p e b -> p b e"), AX.X, ALU.add))
            link(ts(drop[:, :], drop[:, :], -NO_SLOT, NO_SLOT, ALU.mult, ALU.add))
            link(tt(slotf[:, :], slotf[:, :], drop[:, :], ALU.add))
            v.tensor_copy(slot_u[:, :], slotf[:, :]).then_inc(s_slot, 1)
            dve.wait_ge(s_cnt, BITS + 5)
            tile_table(tile_u, DT_, sg1[0:1, 0:NE])

            def experts(m):
                def body(i, u, t):
                    T = T0[m] + t
                    wait(dve, fm2, T - 1)
                    for n, b in enumerate((sg0, sg1)):
                        dve.wait_ge(f_h, 2 * T + n + 1)
                        v.tensor_copy(ht[:, u % 2, n * FH:(n + 1) * FH], b[:, 0:FH]).then_inc(f_ht, 1)
                    dve.wait_ge(fm2, T + 1)
                    rest = xg[:, u, 0:D] if m == 0 else og[:, u, :]
                    tt(osb[:, u, :], cx[:, 0:D], rest, ALU.add).then_inc(f_o, 1)
                tiles(dve, m, body)
            experts(0)
            experts(1)


_INS = ["x_t", "table", "w_in", "conv_w", "conv_b", "dt_bias", "a_log", "d_skip", "norm_w", "gate", "w_out",
        "w_route", "b_route", "w4", "iota", "base_e", "w1c", "w2c", "b2c", "w1u", "w2u", "b2u"]


def kernel(x, L0_tok_weight, L0_attn_gate1, L0_attn_in_proj_w, L0_attn_conv_w, L0_attn_conv_b, L0_attn_dt_bias,
           L0_attn_A_log, L0_attn_D, L0_attn_norm_w, L0_attn_out_proj_w, L0_ffn_Wsc, L0_ffn_bsc, L0_ffn_W1c, L0_ffn_b1c,
           L0_ffn_W2c, L0_ffn_b2c, L0_ffn_Wsu, L0_ffn_bsu, L0_ffn_W1u, L0_ffn_b1u, L0_ffn_W2u, L0_ffn_b2u):
    import numpy as np
    import concourse.bacc as bacc
    from concourse.bass_utils import run_bass_kernel_spmd as run

    def rows(v):
        return np.broadcast_to(np.asarray(v).reshape(1, -1), (P, np.asarray(v).size))

    a = {
        "x_t": np.asarray(x).T, "table": L0_tok_weight, "w_in": np.asarray(L0_attn_in_proj_w).T, "conv_w": L0_attn_conv_w,
        "conv_b": np.asarray(L0_attn_conv_b).reshape(XT, P).T, "dt_bias": rows(L0_attn_dt_bias), "a_log": rows(L0_attn_A_log),
        "d_skip": np.repeat(np.asarray(L0_attn_D), HD).reshape(ZT, P).T, "norm_w": np.asarray(L0_attn_norm_w).reshape(ZT, P).T,
        "gate": rows(L0_attn_gate1), "w_out": np.asarray(L0_attn_out_proj_w).T,
        "w_route": np.concatenate([L0_ffn_Wsc, L0_ffn_Wsu], axis=1),
        "b_route": rows(np.concatenate([L0_ffn_bsc, L0_ffn_bsu])),
        "w4": np.broadcast_to(np.arange(NE, 0, -1, dtype=np.float32), (P, NE)),
        "iota": np.arange(CT, dtype=np.float32).reshape(1, CT),
        "base_e": (np.arange(NE) * LIST).astype(np.float32).reshape(1, NE),
        "w1c": np.concatenate([L0_ffn_W1c, np.asarray(L0_ffn_b1c)[:, None, :]], axis=1), "w2c": L0_ffn_W2c,
        "b2c": np.asarray(L0_ffn_b2c).reshape(1, -1),
        "w1u": np.concatenate([L0_ffn_W1u, np.asarray(L0_ffn_b1u)[:, None, :]], axis=1), "w2u": L0_ffn_W2u,
        "b2u": np.asarray(L0_ffn_b2u).reshape(1, -1),
    }
    nc = bacc.Bacc("TRN2", target_bir_lowering=False, num_devices=1)
    arrays, args = {}, {}
    for name in _INS:
        arrays[f"in_{name}_dram"] = np.ascontiguousarray(a[name])
        args[name] = nc.dram_tensor(f"in_{name}_dram", arrays[f"in_{name}_dram"].shape,
                                    mybir.dt.from_np(arrays[f"in_{name}_dram"].dtype), kind="ExternalInput").ap()
    out = nc.dram_tensor("out_0_dram", (SEQS, L, D), F32, kind="ExternalOutput").ap()
    build(nc, args, out)
    r = run(nc, [arrays], core_ids=[0])
    return r.results[0]["out_0_dram"]
```

```python
from contextlib import ExitStack

import concourse.bass as bass
from concourse import mybir

F32 = mybir.dt.float32
I32 = mybir.dt.int32
ALU = mybir.AluOpType
ACT = mybir.ActivationFunctionType
AX = mybir.AxisListType
ds = bass.ds

P = 128
SEQS, L = 64, 128
NT = SEQS * L
D = 192
DB = D - P
GS = 4
NG = SEQS // GS
GL = GS * L
INNER, STATE, TAPS, HD = 384, 128, 4, 64
HEADS = INNER // HD
XBC = INNER + 2 * STATE
XT, ZT = XBC // P, INNER // P
PROJ = 2 * INNER + 2 * STATE + HEADS
F = 768
FC = F // P
FH = F // 2
NE = 4
CAP = NT // NE
LIST = NT
NLIST = NE * LIST + P
DUMMY = NT
UT = 4
CT = (NT // P + NE - 1 + UT - 1) // UT * UT
DT_ = ((NT - CAP) // P + NE - 1 + UT - 1) // UT * UT
BITS = 28
SEARCH = BITS // UT
LISTING = SEARCH + 2
CREDIT = 1
MAGIC = 12582912.0
QMAX, QEPS, LNEPS = 127.0, 1e-8, 1e-5
NO_SLOT = 40000.0

STEPS = dict(quant=4, clip=4, tap=10, dt0=1, soft=12, ssd=4, h1=2, pick1=2, pick2=11, find=6)


def wait(eng, sem, value):
    if not (isinstance(value, int) and value <= 0):
        eng.wait_ge(sem, value)


def wait_apart(eng, sem, value, marks):
    if not (isinstance(value, int) and value <= 0):
        eng.wait_ge(sem, value)
        if not isinstance(value, int):
            eng.sem_inc(marks, 1)


class Chain:

    def __init__(self, eng, sem, turn, steps):
        self.eng, self.sem, self.base, self.steps, self.n = eng, sem, turn * steps, steps, 0

    def __call__(self, ins, marks=None):
        self.n += 1
        ins.then_inc(self.sem, 1)
        if marks is None:
            self.eng.wait_ge(self.sem, self.base + self.n)
        else:
            wait_apart(self.eng, self.sem, self.base + self.n, marks)

    def end(self):
        assert self.n == self.steps, (self.n, self.steps)


def stages(i, u):
    it = 4 * i + u
    return [it - k if not isinstance(it, int) or 0 <= it - k < NG else None for k in range(5)]


def earlier(i, u, k):
    return 2 * i + (u - k) // 2


def pipeline(eng, body):
    for u in range(4):
        body(0, u)
    with eng.Fori(1, NG // 4) as i:
        for u in range(4):
            body(i, u)
    for u in range(4):
        body(NG // 4, u)


def build(nc, A, out):
    with ExitStack() as ctx:
        def sb(name, shape, dt=F32, c=ctx):
            return c.enter_context(nc.sbuf_tensor(name, shape, dt))

        def sem(name):
            return ctx.enter_context(nc.semaphore(name))

        def bank(name):
            return ctx.enter_context(nc.psum_tensor(name, [P, 512], F32))

        hr_dram = nc.dram_tensor("hr_dram", [NT + P, 2 * D], F32, kind="Internal").ap()
        list_c = nc.dram_tensor("list_c", [NLIST, 1], I32, kind="Internal").ap()
        list_u = nc.dram_tensor("list_u", [NLIST, 1], I32, kind="Internal").ap()
        out_rows = out.rearrange("b l c -> (b l) c")

        ident = sb("ident", [P, P])
        ones = sb("ones", [P, P])
        le = sb("le", [P, P])
        lt = sb("lt", [P, P])
        gt = sb("gt", [P, P])
        neghalf = sb("neghalf", [P, GS])
        fill = sb("fill", [P, NLIST // P], I32)
        zrow = sb("zrow", [P, 2 * D])
        tok = sb("tok", [P, SEQS], I32)
        xids = sb("xids", [P, SEQS + GS], I32)
        w4 = sb("w4", [P, NE])
        conf = sb("conf", [P, SEQS])
        ohc = sb("ohc", [P, SEQS, NE])
        ohu = sb("ohu", [P, SEQS, NE])
        acc = sb("acc", [P, GS + 1, NE])
        w1a = sb("w1a", [P, NE * F])
        w1b = sb("w1b", [DB + 1, NE * F])
        w2s = sb("w2s", [P, NE * FC * D])
        b2s = sb("b2s", [1, NE * D])
        tile_c = sb("tile_c", [1, 2, CT], I32)
        tile_u = sb("tile_u", [1, 2, DT_], I32)
        turns_u = sb("turns_u", [1, 1], I32)
        lst = sb("lst", [1, 4, NE])
        trow = sb("trow", [1, 4, CT])
        slot_u = sb("slot_u", [P, SEQS], I32)
        iota = sb("iota", [1, CT])
        base_e = sb("base_e", [1, NE])

        a = ctx.enter_context(ExitStack())
        win_a, win_b = sb("win_a", [P, PROJ], c=a), sb("win_b", [DB, PROJ], c=a)
        cw, cb = sb("cw", [P, XT, TAPS], c=a), sb("cb", [P, XT], c=a)
        wo = sb("wo", [P, ZT, D], c=a)
        nw, dskip = sb("nw", [P, ZT], c=a), sb("dskip", [P, ZT], c=a)
        dtb, nega = sb("dtb", [P, HEADS], c=a), sb("nega", [P, HEADS], c=a)
        gate = sb("gate", [P, 1], c=a)
        wr_a, wr_b, rb = sb("wr_a", [P, 2 * NE], c=a), sb("wr_b", [DB, 2 * NE], c=a), sb("rb", [P, 2 * NE], c=a)
        gidx = sb("gidx", [P, 2, GS], I32, c=a)
        gath = sb("gath", [P, 2, GS, D], c=a)
        h0 = sb("h0", [P, GS, D], c=a)
        xn = sb("xn", [P, GS, D], c=a)
        hx = sb("hx", [P, 4, GS, D], c=a)
        q1 = sb("q1", [P, 3, GS], c=a)
        st1, mv1 = sb("st1", [P, GS, 6], c=a), sb("mv1", [P, GS, 2], c=a)
        ve1, rstd1 = sb("ve1", [P, 2, GS], c=a), sb("rstd1", [P, 2, GS], c=a)
        xt_a, xt_b = sb("xt_a", [P, 2, GL], c=a), sb("xt_b", [DB, 2, GL], c=a)
        xbc = sb("xbc", [P, 2, XT, GL], c=a)
        zs = sb("zs", [P, 2, ZT, GL], c=a)
        dtr, dab, dtu = (sb(n, [P, 2, GS, HEADS], c=a) for n in ("dtr", "dab", "dtu"))
        dts, dta = sb("dts", [P, 2, GS, HEADS], c=a), sb("dta", [P, 2, GS, HEADS], c=a)
        sp1, sp2, sp3 = (sb(n, [P, GS, HEADS], c=a) for n in ("sp1", "sp2", "sp3"))
        seg_l = sb("seg_l", [P, 2, HEADS, P], c=a)
        dec = sb("dec", [P, 2, HEADS, P], c=a)
        mix = sb("mix", [P, 2, HEADS, P], c=a)
        cbm = sb("cbm", [P, P], c=a)
        xd = sb("xd", [P, 2, INNER], c=a)
        ybuf = sb("ybuf", [P, 2, ZT, GL], c=a)
        ysq = sb("ysq", [P, ZT, GL], c=a)
        ms, rs = sb("ms", [P, GS], c=a), sb("rs", [P, GS], c=a)
        hr = sb("hr", [P, 2, GS, 2 * D], c=a)
        st2, mv2 = sb("st2", [P, GS, 6], c=a), sb("mv2", [P, GS, 2], c=a)
        ve2, rstd2, nm2 = (sb(n, [P, GS], c=a) for n in ("ve2", "rstd2", "nm2"))
        x2t_a, x2t_b = sb("x2t_a", [P, GL], c=a), sb("x2t_b", [DB, GL], c=a)
        lg, dl, el, pk = (sb(n, [P, GS, 2, NE], c=a) for n in ("lg", "dl", "el", "pk"))
        oh = sb("oh", [P, GS, 2, NE], c=a)
        m8, e8, s8 = (sb(n, [P, GS, 2], c=a) for n in ("m8", "e8", "s8"))
        dst = sb("dst", [P, GS, NE], c=a)
        dest = sb("dest", [P, GS], c=a)
        desti, toki = sb("desti", [P, 2, GS], I32, c=a), sb("toki", [P, 2, GS], I32, c=a)
        a.close()
        w1a_u = sb("w1a_u", [P, NE * F])
        w1b_u = sb("w1b_u", [DB + 1, NE * F])
        w2s_u = sb("w2s_u", [P, NE * FC * D])
        b2s_u = sb("b2s_u", [1, NE * D])

        key, cmp_, eqk = sb("key", [P, NE, SEQS]), sb("cmp_", [P, NE, SEQS]), sb("eqk", [P, NE, SEQS])
        scn, tmp = sb("scn", [P, NE, SEQS]), sb("tmp", [P, NE, SEQS])
        thr, cand, tot, step, need = (sb(n, [P, NE]) for n in ("thr", "cand", "tot", "step", "need"))
        zero = sb("zero", [P, SEQS])
        drop = sb("drop", [P, SEQS])
        slotf = sb("slotf", [P, SEQS])
        slot4, tok4 = sb("slot4", [P, 2, GS], I32), sb("tok4", [P, 2, GS], I32)
        ids = sb("ids", [P, UT, 1], I32)
        xg = sb("xg", [P, UT, 2 * D])
        og = sb("og", [P, UT, D])
        fx_a, fx_b = sb("fx_a", [P, 2, P]), sb("fx_b", [DB + 1, 2, P])
        hg = sb("hg", [P, 2, F])
        ht = sb("ht", [P, 2, F])
        osb = sb("osb", [P, UT, D])

        tp, mm0, mm1, sg0, sg1, cx, yb, misc = (bank(n) for n in ("tp", "mm0", "mm1", "sg0", "sg1", "cx", "yb", "misc"))
        mm = [mm0, mm1]
        DTC, SQC, RTC, PFC, OUTC = 0, 32, 64, 96, 128

        s_wa, s_wc, s_wu, s_fill = sem("weights_a"), sem("weights_c"), sem("weights_u"), sem("lists_filled")
        s_const, s_prep, s_pe_, s_sig = sem("constants"), sem("prepared"), sem("exp_a_log"), sem("exp_gate")
        s_idx = sem("gather_index")
        s_gath = [sem(f"gathered{p}") for p in range(2)]
        s_ve, s_rstd, s_xn, s_hx = sem("var1"), sem("rstd1_s"), sem("xn_s"), sem("hx_s")
        s_tr1, s_xt = sem("transposed1"), sem("xt_s")
        s_mm, s_ci, s_cv, s_xbc, s_z = sem("projected"), sem("conv_started"), sem("conv_done"), sem("xbc_s"), sem("z_s")
        s_zc = sem("z_copied")
        s_nm2, s_nr2 = sem("mean_times_rstd"), sem("shift2_s")
        s_dtp, s_dab, s_u, s_dt = sem("dt_projected"), sem("dt_abs"), sem("dt_exp"), sem("dt_s")
        s_sl, s_sg, s_e, s_cx, s_xd, s_m, s_yp, s_yd, s_y2 = (sem(n) for n in (
            "seg_left", "seg_sums", "decays", "cb_and_x", "xd_s", "mixed", "y_product", "y_read", "y_gated"))
        s_sq, s_sqa, s_ssq, s_ms, s_rs, s_o, s_h1, s_ve2, s_rstd2, s_xn2 = (sem(n) for n in (
            "y_squared", "y_squares_added", "y_sums", "mean_square", "rms", "out_product", "h1_s", "var2", "rstd2_s", "xn2_s"))
        s_tr2, s_x2t, s_rt, s_d, s_el, s_oh, s_pf, s_dest = (sem(n) for n in (
            "transposed2", "x2t_s", "routers", "logits", "router_exp", "one_hot", "prefixes", "dest_s"))
        s_st = [sem(f"stored{p}") for p in range(2)]
        s_sc = [sem(f"listed{p}") for p in range(2)]
        c_pool, c_sqa = sem("pool_chain"), sem("chain_squares")
        ch = {n: sem(f"chain_{n}") for n in STEPS}
        s_cmp, s_cnt, s_tab, s_slot = sem("compared"), sem("counted"), sem("tiles_listed"), sem("slots_found")
        s_s4 = sem("slot_copied")
        s_scd = sem("listed")
        s_su = [sem(f"listed_u{p}") for p in range(2)]
        s_dts, s_free, s_keys = sem("dt_values"), sem("stage_a_done"), sem("search_begun")
        marks_dve, marks_pe, marks_pool = sem("marks_dve"), sem("marks_pe"), sem("marks_pool")
        c_setup, c_find = sem("chain_setup"), sem("chain_lists")

        block = ctx.enter_context(nc.Block())

        hr_by_seq = hr_dram[0:NT, :].rearrange("(b l) c -> l b c", l=L)
        n_wa = 16 * 17

        fm2 = sem("tile_out_product")
        f_id = [sem(f"tile_ids{u}") for u in range(UT)]
        f_g = [sem(f"tile_gathered{u}") for u in range(UT)]
        f_s = [sem(f"tile_scattered{u}") for u in range(UT)]
        f_t, f_x, f_m1, f_ge, f_h, f_ht, f_o = (sem(n) for n in (
            "tile_transposed", "tile_x", "tile_hidden_product", "tile_gelu", "tile_hidden_transposed", "tile_hidden", "tile_out"))
        TURNS = [CT // UT, DT_ // UT]
        T0 = [0, CT]
        I0 = [0, CT // UT]

        def turn(i, body):
            for u in range(UT):
                body(i, u, i * UT + u)

        def turns(eng, m, body):
            turn(0, body)
            if m == 0:
                with eng.Fori(1, TURNS[0]) as i:
                    turn(i, body)
                return TURNS[0]
            n = eng.value_load(turns_u[0:1, 0:1], min_val=1, max_val=TURNS[1])
            with eng.Fori(1, TURNS[1]) as i:
                with eng.If(i < n):
                    turn(i, body)
            return n

        def load_experts(eng, to, names, done):
            w1a_, w1b_, w2_, b2_ = to
            w1, w2, b2 = (A[n] for n in names)
            eng.dma_start(w1a_[:, :].rearrange("p (e f) -> p e f", e=NE), w1[:, 0:P, :].rearrange("e p f -> p e f")).then_inc(done, 16)
            eng.dma_start(w1b_[:, :].rearrange("p (e f) -> p e f", e=NE), w1[:, P:D + 1, :].rearrange("e p f -> p e f")).then_inc(done, 16)
            for e in range(NE):
                eng.dma_start(w2_[:, e * FC * D:(e + 1) * FC * D].rearrange("p (c n) -> p c n", c=FC),
                             w2[e].rearrange("(c p) n -> p c n", p=P)).then_inc(done, 16)
            eng.dma_start(b2_[:, :], b2).then_inc(done, 16)

        def experts_sp(sp, m):
            sp.wait_ge(s_tab, m + 1)
            if m == 0:
                sp.wait_ge(s_fill, 48)
                for p in range(2):
                    sp.wait_ge(s_sc[p], 64 * (NG // 2))
            else:
                for p in range(2):
                    sp.wait_ge(s_su[p], 64 * (NG // 2))
            lists, table, n = ((list_c, tile_c, CT), (list_u, tile_u, DT_))[m]

            def body(i, u, t):
                wait(sp, f_s[u], 16 * (I0[m] + i))
                row = sp.value_load(table[0:1, 0, ds(t, 1)], min_val=0, max_val=NLIST - P)
                sp.dma_start(ids[:, u, :], lists[ds(row, P), :]).then_inc(f_id[u], 16)
            turns(sp, m, body)

        @block.sync
        def _(sp):
            for dst_, src in (
                (xids[:, 0:SEQS], A["x_t"]), (win_a[:, :], A["w_in"][0:P, :]), (win_b[:, :], A["w_in"][P:D, :]),
                (cw[:, :, :], A["conv_w"].rearrange("(m p) k -> p m k", p=P)),
                (cb[:, :], A["conv_b"]),
                (dtb[:, :], A["dt_bias"]), (nega[:, :], A["a_log"]), (dskip[:, :], A["d_skip"]),
                (nw[:, :], A["norm_w"]), (gate[:, :], A["gate"]),
                (wo[:, :, :], A["w_out"].rearrange("(m p) n -> p m n", p=P)),
                (wr_a[:, :], A["w_route"][0:P, :]), (wr_b[:, :], A["w_route"][P:D, :]), (rb[:, :], A["b_route"]),
                (w4[:, :], A["w4"]), (iota[:, :], A["iota"]), (base_e[:, :], A["base_e"]),
            ):
                sp.dma_start(dst_, src).then_inc(s_wa, 16)
            sp.wait_ge(s_const, 1)
            for lst_ in (list_c, list_u):
                sp.dma_start(lst_.rearrange("(p n) o -> p (n o)", p=P), fill[:, :]).then_inc(s_fill, 16)
            sp.dma_start(hr_dram[NT:NT + P, :], zrow[:, :]).then_inc(s_fill, 16)
            load_experts(sp, (w1a, w1b, w2s, b2s), ("w1c", "w2c", "b2c"), s_wc)

            def body(i, u):
                g = stages(i, u)[3]
                if g is not None:
                    sp.wait_ge(s_xn2, g + 1)
                    sp.dma_start(hr_by_seq[:, ds(GS * g, GS), :], hr[:, (u + 1) % 2, :, :]).then_inc(s_st[(u + 1) % 2], 16)
            pipeline(sp, body)

            experts_sp(sp, 0)
            experts_sp(sp, 1)

        @block.gpsimd
        def _(pool):
            chain = [0]

            def link(ins):
                chain[0] += 1
                ins.then_inc(c_pool, 1)
                pool.wait_ge(c_pool, chain[0])

            nc.gpsimd.memset(fill[:, :], DUMMY)
            link(nc.gpsimd.memset(zrow[:, :], 0.0))
            nc.gpsimd.memset(xids[:, SEQS:SEQS + GS], 0)
            nc.gpsimd.memset(neghalf[:, :], -0.5)
            nc.gpsimd.iota(tok[:, :], pattern=[[L, SEQS]], base=0, channel_multiplier=1)
            link(nc.gpsimd.memset(ones[:, :], 1.0))
            for t_, off, mul, pat in ((le, 0, -1, 1), (lt, -1, -1, 1), (gt, -1, 1, -1)):
                nc.gpsimd.affine_select(out=t_[:, :], in_=ones[:, :], compare_op=ALU.is_ge, fill=0.0, base=off,
                                        pattern=[[pat, P]], channel_multiplier=mul)
            link(nc.gpsimd.affine_select(out=ident[:, :], in_=ones[:, :], compare_op=ALU.is_equal, fill=0.0, base=0,
                                         pattern=[[-1, P]], channel_multiplier=1))
            for e in range(NE):
                last = nc.gpsimd.memset(acc[:, 0, e:e + 1], float(e * LIST // P))
            for s_ in (s_oh, s_el, s_dest, s_scd, *s_st):
                pool.sem_inc(s_, CREDIT)
            last.then_inc(s_const, 1)
            pool.wait_ge(s_const, 1)
            pool.wait_ge(s_wa, n_wa)

            def gather(g, u):
                p = u % 2
                wait_apart(pool, s_ve, g - 1, marks_pool)
                nc.gpsimd.tensor_copy(gidx[:, p, :], xids[:, ds(GS * g, GS)]).then_inc(s_idx, 1)
                wait_apart(pool, s_idx, g + 1, marks_pool)
                for j in range(GS):
                    nc.gpsimd.indirect_dma_start(
                        out=gath[:, p, j, :], out_offset=None, in_=A["table"][:, :],
                        in_offset=bass.IndirectOffsetOnAxis(ap=gidx[:, p, j:j + 1], axis=0)).then_inc(s_gath[p], 16)

            def body(i, u):
                g1, g2, g3, g4, g5 = stages(i, u)

                def seg_left(g, p, j):
                    wait_apart(pool, s_dt, g + 1, marks_pool)
                    wait_apart(pool, s_sg, GS * g + j - 1, marks_pool)
                    nc.gpsimd.tensor_tensor(seg_l[:, j % 2, :, :], le[:, :].unsqueeze(1).broadcast_to([P, HEADS, P]),
                                            dta[:, p, j, :].unsqueeze(2).broadcast_to([P, HEADS, P]),
                                            ALU.mult).then_inc(s_sl, 1)

                def gate_y(j):
                    if g3 is None:
                        return
                    p, js = u % 2, slice(j * L, (j + 1) * L)
                    if j == 0:
                        wait_apart(pool, s_z, g3 + 1, marks_pool)
                        wait_apart(pool, s_zc, ZT * (g3 + 1), marks_pool)
                    wait_apart(pool, s_yd, GS * g3 + j + 1, marks_pool)
                    nc.gpsimd.tensor_tensor(ybuf[:, p, :, js], ybuf[:, p, :, js], zs[:, p, :, js], ALU.mult).then_inc(s_y2, 1)

                if g4 is not None:
                    wait_apart(pool, s_sq, g4 + 1, marks_pool)
                    nc.gpsimd.tensor_tensor(ysq[:, 0, :], ysq[:, 0, :], ysq[:, 1, :], ALU.add).then_inc(c_sqa, 1)
                    wait_apart(pool, c_sqa, g4 + 1, marks_pool)
                    nc.gpsimd.tensor_tensor(ysq[:, 0, :], ysq[:, 0, :], ysq[:, 2, :], ALU.add).then_inc(s_sqa, 1)
                if g3 is not None:
                    seg_left(g3, u % 2, 2)
                gate_y(0)
                if g4 is not None:
                    wait_apart(pool, s_ms, g4 + 1, marks_pool)
                    nc.gpsimd.tensor_tensor(rs[:, :], ms[:, :], neghalf[:, :], ALU.pow).then_inc(s_rs, 1)
                if g3 is not None:
                    seg_left(g3, u % 2, 3)
                if g1 is not None:
                    wait_apart(pool, s_ve, g1 + 1, marks_pool)
                    nc.gpsimd.tensor_tensor(rstd1[:, u % 2, :], ve1[:, u % 2, :], neghalf[:, :], ALU.pow).then_inc(s_rstd, 1)
                    wait_apart(pool, s_rstd, g1 + 1, marks_pool)
                    wait_apart(pool, s_tr1, 2 * g1, marks_pool)
                    for j in range(GS):
                        last = nc.gpsimd.tensor_scalar(xn[:, j, :], h0[:, j, :], mv1[:, j, 0:1],
                                                       rstd1[:, u % 2, j:j + 1], ALU.subtract, ALU.mult)
                    last.then_inc(s_xn, 1)
                gate_y(1)
                if g1 is not None:
                    gather(g1 + 1, u + 1)
                if g1 is not None:
                    wait_apart(pool, s_xn, g1 + 1, marks_pool)
                    wait_apart(pool, s_h1, 2 * (g1 - 3), marks_pool)
                    nc.gpsimd.tensor_tensor(hx[:, u % 4, :, :], h0[:, :, :], xn[:, :, :], ALU.add).then_inc(s_hx, 1)
                if g2 is not None:
                    seg_left(g2, (u + 1) % 2, 0)
                gate_y(2)
                if g4 is not None:
                    wait_apart(pool, s_ve2, g4 + 1, marks_pool)
                    nc.gpsimd.tensor_tensor(rstd2[:, :], ve2[:, :], neghalf[:, :], ALU.pow).then_inc(s_rstd2, 1)
                    wait_apart(pool, s_rstd2, g4 + 1, marks_pool)
                    nc.gpsimd.tensor_tensor(nm2[:, :], mv2[:, :, 0], rstd2[:, :], ALU.mult).then_inc(s_nm2, 1)
                    wait_apart(pool, s_nm2, g4 + 1, marks_pool)
                    nc.gpsimd.tensor_scalar(nm2[:, :], nm2[:, :], -1.0, 1.0, ALU.mult, ALU.mult).then_inc(s_nr2, 1)
                gate_y(3)
                if g2 is not None:
                    seg_left(g2, (u + 1) % 2, 1)
                if g5 is not None:
                    p = u % 2
                    wait_apart(pool, s_dest, CREDIT + g5 + 1, marks_pool)
                    for j in range(GS):
                        nc.gpsimd.indirect_dma_start(
                            out=list_c[:, :], out_offset=bass.IndirectOffsetOnAxis(ap=desti[:, p, j:j + 1], axis=0),
                            in_=toki[:, p, j:j + 1], in_offset=None).then_inc(s_sc[p], 16)
                if g5 is not None:
                    wait_apart(pool, s_sc[u % 2], 64 * (earlier(i, u, 4) + 1), marks_pool)
                    pool.sem_inc(s_scd, 1)

            gather(0, 0)
            wait_apart(pool, s_fill, 48, marks_pool)
            pipeline(pool, body)

            def list_dropped(i, p):
                wait_apart(pool, s_su[p], 64 * i, marks_pool)
                g = 2 * i + p
                nc.gpsimd.tensor_copy(slot4[:, p, :], slot_u[:, ds(GS * g, GS)])
                nc.gpsimd.tensor_copy(tok4[:, p, :], tok[:, ds(GS * g, GS)]).then_inc(s_s4, 1)
                wait_apart(pool, s_s4, g + 1, marks_pool)
                for j in range(GS):
                    nc.gpsimd.indirect_dma_start(
                        out=list_u[:, :], out_offset=bass.IndirectOffsetOnAxis(ap=slot4[:, p, j:j + 1], axis=0),
                        in_=tok4[:, p, j:j + 1], in_offset=None,
                        bounds_check=NE * LIST - 1, oob_is_err=False).then_inc(s_su[p], 16)

            def experts(m):
                def gather_tile(i, u, t):
                    wait_apart(pool, f_id[u], 16 * (I0[m] + i + 1), marks_pool)
                    nc.gpsimd.indirect_dma_start(
                        out=xg[:, u, :], out_offset=None, in_=hr_dram[:, :],
                        in_offset=bass.IndirectOffsetOnAxis(ap=ids[:, u, :], axis=0)).then_inc(f_g[u], 16)
                    if m == 1:
                        nc.gpsimd.indirect_dma_start(
                            out=og[:, u, :], out_offset=None, in_=out_rows,
                            in_offset=bass.IndirectOffsetOnAxis(ap=ids[:, u, :], axis=0),
                            bounds_check=NT - 1, oob_is_err=False).then_inc(f_g[u], 16)

                def scatter_tile(u, t):
                    wait_apart(pool, f_o, T0[m] + t + 1, marks_pool)
                    nc.gpsimd.indirect_dma_start(
                        out=out_rows, out_offset=bass.IndirectOffsetOnAxis(ap=ids[:, u, :], axis=0),
                        in_=osb[:, u, :], in_offset=None, bounds_check=NT - 1, oob_is_err=False).then_inc(f_s[u], 16)

                def body(i, u, t):
                    gather_tile(i, u, t)
                    if not (isinstance(t, int) and t < 2):
                        scatter_tile((u - 2) % UT, t - 2)
                if m == 0:
                    turn(0, body)
                    with pool.Fori(1, LISTING) as i:
                        turn(i, body)

                    def listing_turn(i):
                        for u in range(UT):
                            body(i, u, i * UT + u)
                            if u % 2:
                                list_dropped(i - LISTING, u // 2)

                    wait_apart(pool, s_slot, 1, marks_pool)
                    listing_turn(LISTING)
                    with pool.Fori(LISTING + 1, TURNS[0]) as i:
                        listing_turn(i)
                    n = TURNS[0]
                else:
                    n = turns(pool, 1, body)
                for u in (UT - 2, UT - 1):
                    scatter_tile(u, (n - 1) * UT + u)
                for u in range(UT):
                    wait_apart(pool, f_s[u], 16 * (I0[m] + n), marks_pool)

            for p in range(2):
                wait_apart(pool, s_st[p], CREDIT + 16 * (NG // 2), marks_pool)
            experts(0)
            pool.wait_ge(s_tab, 2)
            experts(1)

        @block.scalar
        def _(act):
            act.wait_ge(s_wa, n_wa)
            nc.scalar.activation(nega[:, :], nega[:, :], ACT.Exp).then_inc(s_pe_, 1)
            nc.scalar.activation(gate[:, :], gate[:, :], ACT.Exp, scale=-1.0).then_inc(s_sig, 1)

            def body(i, u):
                g1, g2, g3, g4, g5 = stages(i, u)

                def decays(j):
                    if g3 is None:
                        return
                    act.wait_ge(s_sg, GS * g3 + j + 1)
                    wait(act, s_m, GS * g3 + j - 1)
                    nc.scalar.activation(dec[:, j % 2, 0:3, :], sg0[:, 0:3 * P].rearrange("p (h s) -> p h s", h=3), ACT.Exp)
                    nc.scalar.activation(dec[:, j % 2, 3:6, :], sg1[:, 0:3 * P].rearrange("p (h s) -> p h s", h=3),
                                         ACT.Exp).then_inc(s_e, 1)

                def start(m):
                    if g2 is None:
                        return
                    p = (u + 1) % 2
                    if m == 0:
                        wait(act, s_y2, GS * (g2 - 1))
                    act.wait_ge(s_mm, (XT + ZT) * g2 + m + 1)
                    if m < XT:
                        nc.scalar.activation(xbc[:, p, m, :], mm[m % 2][:, :], ACT.Identity, bias=cb[:, m:m + 1],
                                             scale=cw[:, m, TAPS - 1:TAPS]).then_inc(s_ci, 1)
                    elif m == XT:
                        nc.scalar.copy(zs[:, p, m - XT, :], mm[m % 2][:, :]).then_inc(s_zc, 1)
                    else:
                        nc.scalar.activation(zs[:, p, m - XT, :], mm[m % 2][:, :], ACT.Silu).then_inc(s_zc, 1)

                def silus():
                    if g2 is None:
                        return
                    p = (u + 1) % 2
                    act.wait_ge(s_cv, XT * (g2 + 1))
                    nc.scalar.activation(xbc[:, p, :, :], xbc[:, p, :, :], ACT.Silu).then_inc(s_xbc, 1)
                    act.wait_ge(s_zc, ZT * g2 + 1)
                    nc.scalar.activation(zs[:, p, 0, :], zs[:, p, 0, :], ACT.Silu).then_inc(s_z, 1)

                def from_tp(g, k, half):
                    rows = (P, DB)[half]
                    if g is None:
                        return
                    if k == 2:
                        act.wait_ge(s_tr2, 2 * g + half + 1)
                        wait(act, s_rt, g)
                        nc.scalar.copy((x2t_a, x2t_b)[half][:, :], tp[0:rows, :]).then_inc(s_x2t, 1)
                    else:
                        act.wait_ge(s_tr1, 2 * g + half + 1)
                        wait(act, s_mm, (XT + ZT) * (g - 1))
                        nc.scalar.copy((xt_a, xt_b)[half][:, u % 2, :], tp[0:rows, :]).then_inc(s_xt, 1)

                decays(0)
                if g2 is not None:
                    act.wait_ge(s_dab, g2 + 1)
                    nc.scalar.activation(dtu[:, (u + 1) % 2, :, :], dab[:, (u + 1) % 2, :, :], ACT.Exp,
                                         scale=-1.0).then_inc(s_u, 1)
                start(0)
                from_tp(g5, 2, 0)
                from_tp(g5, 2, 1)
                if g4 is not None:
                    act.wait_ge(s_y2, GS * (g4 + 1))
                    wait(act, s_ssq, g4)
                    nc.scalar.activation(ysq[:, :, :], ybuf[:, (u + 1) % 2, :, :], ACT.Square).then_inc(s_sq, 1)
                start(1)
                decays(1)
                start(2)
                start(3)
                decays(2)
                start(4)
                if g5 is not None:
                    act.wait_ge(s_d, g5 + 1)
                    wait(act, s_oh, CREDIT + g5)
                    nc.scalar.activation(el[:, :, :, :], dl[:, :, :, :], ACT.Exp).then_inc(s_el, 1)
                start(5)
                decays(3)
                silus()
                start(6)
                from_tp(g1, 1, 0)
                start(7)
                from_tp(g1, 1, 1)
                if g4 is not None:
                    p = (u + 1) % 2
                    act.wait_ge(s_nr2, g4 + 1)
                    for j in range(GS):
                        last = nc.scalar.activation(hr[:, p, j, D:2 * D], hr[:, p, j, 0:D], ACT.Identity,
                                                    bias=nm2[:, j:j + 1], scale=rstd2[:, j:j + 1])
                    last.then_inc(s_xn2, 1)

            pipeline(act, body)

            def experts(m):
                def body(i, u, t):
                    T = T0[m] + t
                    act.wait_ge(f_t, T + 1)
                    wait(act, f_m1, 2 * (T - 1))
                    nc.scalar.copy(fx_a[:, u % 2, :], tp[:, 0:P])
                    nc.scalar.copy(fx_b[0:DB, u % 2, :], tp[0:DB, P:2 * P]).then_inc(f_x, 1)
                    wait(act, f_h, 2 * (T - 1))
                    for n, b in enumerate((mm0, mm1)):
                        act.wait_ge(f_m1, 2 * T + n + 1)
                        nc.scalar.activation(hg[:, u % 2, n * FH:(n + 1) * FH], b[:, 0:FH], ACT.Gelu).then_inc(f_ge, 1)
                turns(act, m, body)

            act.wait_ge(s_free, 1)
            load_experts(act, (w1a_u, w1b_u, w2s_u, b2s_u), ("w1u", "w2u", "b2u"), s_wu)
            experts(0)
            act.wait_ge(s_tab, 2)
            experts(1)

        @block.tensor
        def _(pe):
            mmul = nc.tensor.matmul
            pe.wait_ge(s_const, 1)
            pe.wait_ge(s_wa, n_wa)
            pe.wait_ge(s_prep, 1)

            def body(i, u):
                g1, g2, g3, g4, g5 = stages(i, u)

                def cap(v):
                    return min(v, NG) if isinstance(v, int) else v

                def seg(j):
                    if g3 is None:
                        return
                    pe.wait_ge(s_sl, GS * g3 + j + 1)
                    wait(pe, s_e, GS * g3 + j)
                    for b, bank_ in enumerate((sg0, sg1)):
                        last = mmul(bank_[:, 0:3 * P], gt[:, :], seg_l[:, j % 2, 3 * b:3 * b + 3, :], start=True, stop=True)
                    last.then_inc(s_sg, 1)

                def cbx(j):
                    if g3 is None:
                        return
                    p, js = u % 2, slice(j * L, (j + 1) * L)
                    pe.wait_ge(s_xbc, g3 + 1)
                    wait(pe, s_xd, GS * g3 + j)
                    mmul(cx[:, 0:P], xbc[:, p, ZT, js], xbc[:, p, ZT + 1, js], start=True, stop=True)
                    for c in range(ZT):
                        last = nc.tensor.transpose(cx[:, (c + 1) * P:(c + 2) * P], xbc[:, p, c, js], ident[:, :])
                    last.then_inc(s_cx, 1)

                def y(j):
                    if g3 is None:
                        return
                    pe.wait_ge(s_m, GS * g3 + j + 1)
                    wait(pe, s_yd, GS * g3 + j)
                    for h in range(HEADS):
                        r = (h % 2) * HD
                        last = mmul(yb[r:r + HD, (h // 2) * P:(h // 2 + 1) * P], xd[:, j % 2, h * HD:(h + 1) * HD],
                                    mix[:, j % 2, h, :], start=True, stop=True)
                    last.then_inc(s_yp, 1)

                def dt():
                    if g2 is None:
                        return
                    p = (u + 1) % 2
                    pe.wait_ge(s_xt, 2 * (g2 + 1))
                    wait(pe, s_dab, g2)
                    wait(pe, s_h1, 2 * (g2 - 2))
                    if not (isinstance(g2, int) and g2 < 4):
                        pe.wait_ge(s_dest, CREDIT + g2 - 3)
                    for j in range(GS):
                        o = misc[:, DTC + j * HEADS:DTC + (j + 1) * HEADS]
                        js = slice(j * L, (j + 1) * L)
                        mmul(o, xt_a[:, p, js], win_a[:, PROJ - HEADS:PROJ], start=True, stop=False)
                        last = mmul(o, xt_b[:, p, js], win_b[:, PROJ - HEADS:PROJ], start=False, stop=True)
                    last.then_inc(s_dtp, 1)

                def project(m):
                    if g2 is None:
                        return
                    p = (u + 1) % 2
                    if m < 2:
                        wait(pe, s_zc, ZT * (g2 - 1) + m + 2)
                    elif m - 2 < XT:
                        pe.wait_ge(s_cv, XT * g2 + m - 1)
                    else:
                        pe.wait_ge(s_zc, ZT * g2 + m - 1 - XT)
                    c0 = INNER + m * P if m < XT else (m - XT) * P
                    mmul(mm[m % 2][:, :], win_a[:, c0:c0 + P], xt_a[:, p, :], start=True, stop=False)
                    mmul(mm[m % 2][:, :], win_b[:, c0:c0 + P], xt_b[:, p, :], start=False, stop=True).then_inc(s_mm, 1)

                def sums():
                    if g4 is None:
                        return
                    pe.wait_ge(s_sqa, g4 + 1)
                    wait(pe, s_ms, g4)
                    wait(pe, s_dab, cap(g4 + 2))
                    wait(pe, s_h1, 2 * g4)
                    if not (isinstance(g4, int) and g4 == 0):
                        pe.wait_ge(s_dest, CREDIT + g4 - 1)
                    for j in range(GS):
                        last = mmul(misc[:, SQC + j:SQC + j + 1], ysq[:, 0, j * L:(j + 1) * L], ones[:, 0:1],
                                    start=True, stop=True)
                    last.then_inc(s_ssq, 1)

                def out_product(q):
                    if g4 is None:
                        return
                    wait(pe, s_h1, 2 * g4 + q)
                    if q == 0:
                        pe.wait_ge(s_ms, g4 + 1)
                        wait(pe, s_d, g4)
                    for j in range(2):
                        for c in range(ZT):
                            last = mmul(misc[:, OUTC + j * D:OUTC + (j + 1) * D],
                                        ybuf[:, (u + 1) % 2, c, (2 * q + j) * L:(2 * q + j + 1) * L],
                                        wo[:, c, :], start=(c == 0), stop=(c == ZT - 1))
                    last.then_inc(s_o, 1)

                def to_tp(g, k, half):
                    if g is None:
                        return
                    rows, c0 = (P, DB)[half], half * P
                    if half == 0:
                        pe.wait_ge((s_xn, s_xn2)[k - 1], g + 1)
                        if k == 2:
                            wait(pe, s_x2t, 2 * g)
                            wait(pe, s_xt, 2 * (min(g + 4, NG) if isinstance(g, int) else g + 4))
                        else:
                            wait(pe, s_xt, 2 * g)
                            wait(pe, s_x2t, 2 * (g - 3))
                    else:
                        wait_apart(pe, (s_xt, s_x2t)[k - 1], 2 * g + 1, marks_pe)
                    for j in range(GS):
                        src = xn[:, j, c0:c0 + rows] if k == 1 else hr[:, u % 2, j, D + c0:D + c0 + rows]
                        last = nc.tensor.transpose(tp[0:rows, j * L:(j + 1) * L], src, ident[:, :])
                    last.then_inc((s_tr1, s_tr2)[k - 1], 1)

                def routers():
                    if g5 is None:
                        return
                    pe.wait_ge(s_x2t, 2 * g5 + 2)
                    wait(pe, s_d, g5)
                    wait(pe, s_dab, cap(g5 + 3))
                    wait(pe, s_ms, cap(g5 + 2))
                    wait(pe, s_h1, 2 * cap(g5 + 1))
                    wait(pe, s_dest, CREDIT + g5)
                    for j in range(GS):
                        o = misc[:, RTC + j * 2 * NE:RTC + (j + 1) * 2 * NE]
                        mmul(o, x2t_a[:, j * L:(j + 1) * L], wr_a[:, :], start=True, stop=False)
                        last = mmul(o, x2t_b[:, j * L:(j + 1) * L], wr_b[:, :], start=False, stop=True)
                    last.then_inc(s_rt, 1)

                def prefixes():
                    if g5 is None:
                        return
                    pe.wait_ge(s_oh, CREDIT + g5 + 1)
                    wait(pe, s_dest, CREDIT + g5)
                    wait(pe, s_h1, 2 * cap(g5 + 2))
                    mmul(misc[:, PFC:PFC + GS * NE], lt[:, :], oh[:, :, 0, :], start=True, stop=False)
                    mmul(misc[:, PFC:PFC + GS * NE], ones[:, :], acc[:, 0:GS, :], start=False, stop=True).then_inc(s_pf, 1)

                seg(0)
                dt()
                project(0)
                to_tp(g5, 2, 0)
                cbx(0)
                to_tp(g5, 2, 1)
                project(1)
                seg(1)
                y(0)
                sums()
                project(2)
                cbx(1)
                routers()
                project(3)
                seg(2)
                y(1)
                project(4)
                cbx(2)
                out_product(0)
                project(5)
                seg(3)
                y(2)
                project(6)
                out_product(1)
                cbx(3)
                to_tp(g1, 1, 0)
                project(7)
                to_tp(g1, 1, 1)
                prefixes()
                y(3)

            pipeline(pe, body)

            pe.wait_ge(s_cmp, 1)
            mmul(yb[:, 0:NE], ones[:, :], acc[:, 0, :], start=True, stop=True).then_inc(s_cnt, 1)

            def count(pairs, k):
                pe.wait_ge(s_cmp, k)
                for n, (l_, r_) in enumerate(pairs):
                    last = mmul(misc[:, 0:NE * SEQS], l_, r_, start=(n == 0), stop=(n == len(pairs) - 1))
                last.then_inc(s_cnt, 1)

            def experts(m):
                table = (tile_c, tile_u)[m]
                w1a_, w1b_, w2_, b2_ = ((w1a, w1b, w2s, b2s), (w1a_u, w1b_u, w2s_u, b2s_u))[m]

                def hidden_transposed(T, u):
                    for n in range(2):
                        pe.wait_ge(f_ge, 2 * T + n + 1)
                        wait(pe, f_ht, 2 * (T - 1) + n + 1)
                        for c in range(3):
                            last = nc.tensor.transpose((sg0, sg1)[n][:, c * P:(c + 1) * P],
                                                       hg[:, u % 2, (3 * n + c) * P:(3 * n + c + 1) * P], ident[:, :])
                        last.then_inc(f_h, 1)

                def out_product(t, u):
                    T = T0[m] + t
                    e = pe.value_load(table[0:1, 1, ds(t, 1)], min_val=0, max_val=NE - 1)
                    pe.wait_ge(f_ht, 2 * T + 2)
                    wait(pe, f_o, T)
                    for c in range(FC):
                        mmul(cx[:, 0:D], ht[:, u % 2, c * P:(c + 1) * P], w2_[:, ds(e * (FC * D) + c * D, D)],
                             start=(c == 0), stop=False)
                    mmul(cx[:, 0:D], ones[0:1, :], b2_[:, ds(e * D, D)], start=False, stop=True).then_inc(fm2, 1)

                def body(i, u, t):
                    T = T0[m] + t
                    first = isinstance(t, int) and t == 0
                    pe.wait_ge(f_g[u], (16 * (i + 1)) if m == 0 else 16 * I0[1] + 32 * (i + 1))
                    wait(pe, f_x, T)
                    nc.tensor.transpose(tp[:, 0:P], xg[:, u, D:D + P], ident[:, :])
                    nc.tensor.transpose(tp[0:DB, P:2 * P], xg[:, u, D + P:2 * D], ident[:, :]).then_inc(f_t, 1)
                    if not first:
                        hidden_transposed(T - 1, u - 1)
                    e = pe.value_load(table[0:1, 1, ds(t, 1)], min_val=0, max_val=NE - 1)
                    pe.wait_ge(f_x, T + 1)
                    for n in range(2):
                        wait(pe, f_ge, 2 * (T - 1) + n + 1)
                        mmul(mm[n][:, 0:FH], fx_a[:, u % 2, :], w1a_[:, ds(e * F + n * FH, FH)], start=True, stop=False)
                        mmul(mm[n][:, 0:FH], fx_b[:, u % 2, :], w1b_[:, ds(e * F + n * FH, FH)],
                             start=False, stop=True).then_inc(f_m1, 1)
                    if not first:
                        out_product(t - 1, u - 1)

                def search(i, u, t):
                    body(i, u, t)
                    count([(ones[:, :], cmp_[:, :, :])], t + 2)

                def ranks(i, u, t):
                    body(i, u, t)
                    if u:
                        count([[(ones[:, :], cmp_[:, :, :])],
                               [(lt[:, :], eqk[:, :, :]), (ones[:, :], scn[:, :, :])],
                               [(lt[:, :], cmp_[:, :, :]), (ones[:, :], scn[:, :, :])]][u - 1], BITS + 2 + u)
                    if u == UT - 1:
                        mmul(yb[:, 0:NE], ones[:, :], tot[:, :], start=True, stop=True).then_inc(s_cnt, 1)

                if m == 0:
                    turn(0, search)
                    with pe.Fori(1, SEARCH) as i:
                        turn(i, search)
                    turn(SEARCH, ranks)
                    with pe.Fori(SEARCH + 1, TURNS[0]) as i:
                        turn(i, body)
                    n = TURNS[0]
                else:
                    n = turns(pe, 1, body)
                hidden_transposed(T0[m] + n * UT - 1, UT - 1)
                out_product(n * UT - 1, UT - 1)

            pe.wait_ge(s_wc, 16 * 7)
            pe.wait_ge(s_keys, 1)
            experts(0)
            pe.wait_ge(s_tab, 2)
            pe.wait_ge(s_wu, 16 * 7)
            experts(1)

        @block.vector
        def _(dve):
            v = nc.vector
            ts, tt, stt = v.tensor_scalar, v.tensor_tensor, v.scalar_tensor_tensor
            n_setup = [0]

            def link(ins):
                n_setup[0] += 1
                ins.then_inc(c_setup, 1)
                dve.wait_ge(c_setup, n_setup[0])

            dve.wait_ge(s_sig, 1)
            link(ts(gate[:, :], gate[:, :], 1.0, None, ALU.add))
            link(v.reciprocal(gate[:, :], gate[:, :]))
            for c in range(ZT):
                ts(wo[:, c, :], wo[:, c, :], nw[:, c:c + 1], gate[:, 0:1], ALU.mult, ALU.mult)
            ts(nega[:, :], nega[:, :], -1.0, None, ALU.mult).then_inc(s_prep, 1)
            dve.wait_ge(s_prep, 1)
            dve.wait_ge(s_const, 1)

            def norm_stats(x, st, mv, ve, link):
                for j in range(GS):
                    last = v.bn_stats(st[:, j, :], x(j))
                link(last, marks_dve)
                for j in range(GS):
                    last = v.bn_aggr(mv[:, j, :], st[:, j, :])
                link(last)
                return ts(ve, mv[:, :, 1], LNEPS, None, ALU.add)

            def quantise(g, u, turn_):
                p, link = u % 2, Chain(dve, ch["quant"], g, STEPS["quant"])
                dve.wait_ge(s_gath[p], 64 * (turn_ + 1))
                link(v.tensor_reduce(q1[:, 0, :], gath[:, p, :, :], AX.X, ALU.max, apply_absolute_value=True))
                link(ts(q1[:, 1, :], q1[:, 0, :], 1.0 / QMAX, QEPS, ALU.mult, ALU.max))
                link(v.reciprocal(q1[:, 2, :], q1[:, 1, :]))
                wait(dve, s_hx, g)
                for j in range(GS):
                    last = ts(h0[:, j, :], gath[:, p, j, :], q1[:, 2, j:j + 1], MAGIC, ALU.mult, ALU.add)
                link(last)
                link.end()

            quantise(0, 0, 0)

            def body(i, u):
                g1, g2, g3, g4, g5 = stages(i, u)
                chains = {n: Chain(dve, ch[n], g, STEPS[n]) for n, g in (
                    ("clip", g1), ("dt0", g2), ("tap", g2), ("soft", g2), ("ssd", g3), ("h1", g4),
                    ("pick1", g5), ("pick2", g5)) if g is not None}
                r8 = lambda t_: t_[:, :, :, :].rearrange("p j r e -> p (j r) e")
                b8 = lambda t_: t_[:, :, :].rearrange("p j r -> p (j r)").unsqueeze(2).broadcast_to([P, GS * 2, NE])

                def clip():
                    if g1 is None:
                        return
                    p, link = u % 2, chains["clip"]
                    link(ts(h0[:, :, :], h0[:, :, :], MAGIC, QMAX, ALU.subtract, ALU.min))
                    for j in range(GS):
                        last = ts(h0[:, j, :], h0[:, j, :], -QMAX, q1[:, 1, j:j + 1], ALU.max, ALU.mult)
                    link(last)
                    norm_stats(lambda j: h0[:, j, :], st1, mv1, ve1[:, p, :], link).then_inc(s_ve, 1)
                    link.end()

                def steps_abs():
                    if g2 is None:
                        return
                    p, link = (u + 1) % 2, chains["dt0"]
                    dve.wait_ge(s_dtp, g2 + 1)
                    link(tt(dtr[:, p, :, :], misc[:, DTC:DTC + GS * HEADS].rearrange("p (j h) -> p j h", j=GS),
                            dtb[:, :].unsqueeze(1).broadcast_to([P, GS, HEADS]), ALU.add))
                    link.end()
                    x_ = dtr[:, p, :, :].rearrange("p j h -> p (j h)")
                    stt(out=dab[:, p, :, :].rearrange("p j h -> p (j h)"), in0=x_, scalar=-1.0, in1=x_,
                        op0=ALU.mult, op1=ALU.max).then_inc(s_dab, 1)

                def steps_softplus():
                    if g2 is None:
                        return
                    p, link = (u + 1) % 2, chains["soft"]
                    flat = lambda t_: t_.rearrange("p j h -> p (j h)")
                    U, DTR, DTS = flat(dtu[:, p, :, :]), flat(dtr[:, p, :, :]), flat(dts[:, p, :, :])
                    S1, S2, S3 = flat(sp1[:, :, :]), flat(sp2[:, :, :]), flat(sp3[:, :, :])
                    dve.wait_ge(s_u, g2 + 1)
                    link(ts(S1, U, 2.0, None, ALU.add))
                    link(v.reciprocal(S2, S1))
                    link(tt(S1, S2, U, ALU.mult))
                    link(tt(S2, S1, S1, ALU.mult))
                    link(ts(S3, S2, 1.0 / 13, None, ALU.mult))
                    for d in (11, 9, 7, 5, 3):
                        link(stt(out=S3, in0=S3, scalar=1.0 / d, in1=S2, op0=ALU.add, op1=ALU.mult))
                    link(stt(out=S3, in0=S3, scalar=1.0, in1=S1, op0=ALU.add, op1=ALU.mult))
                    ts(S2, DTR, 0.0, None, ALU.max)
                    link(ts(S3, S3, 2.0, None, ALU.mult))
                    link.end()
                    tt(DTS, S3, S2, ALU.add).then_inc(s_dts, 1)
                    dve.wait_ge(s_dts, g2 + 1)
                    tt(dta[:, p, :, :], dts[:, p, :, :], nega[:, :].unsqueeze(1).broadcast_to([P, GS, HEADS]),
                       ALU.mult).then_inc(s_dt, 1)

                def conv(m):
                    if g2 is None:
                        return
                    p, link = (u + 1) % 2, chains["tap"]
                    dve.wait_ge(s_ci, XT * g2 + m + 1)
                    src = mm[m % 2][:, :].rearrange("p (j t) -> p j t", j=GS)
                    dst_ = xbc[:, p, m, :].rearrange("p (j t) -> p j t", j=GS)
                    for back in range(1, TAPS):
                        ins = stt(out=dst_[:, :, back:L], in0=src[:, :, 0:L - back],
                                  scalar=cw[:, m, TAPS - 1 - back:TAPS - back], in1=dst_[:, :, back:L],
                                  op0=ALU.mult, op1=ALU.add)
                        if back < TAPS - 1:
                            link(ins)
                    ins.then_inc(s_cv, 1)

                def weights(j):
                    if g3 is None:
                        return
                    p, link = u % 2, chains["ssd"]
                    dve.wait_ge(s_cx, GS * g3 + j + 1)
                    wait(dve, s_m, GS * g3 + j)
                    link(tt(cbm[:, :], cx[:, 0:P], le[:, :], ALU.mult))
                    wait(dve, s_yp, GS * g3 + j - 1)
                    tt(xd[:, j % 2, :].rearrange("p (h n) -> p h n", h=HEADS),
                       cx[:, P:4 * P].rearrange("p (h n) -> p h n", h=HEADS),
                       dts[:, p, j, :].unsqueeze(2).broadcast_to([P, HEADS, HD]), ALU.mult).then_inc(s_xd, 1)
                    dve.wait_ge(s_e, GS * g3 + j + 1)
                    tt(mix[:, j % 2, :, :], dec[:, j % 2, :, :], cbm[:, :].unsqueeze(1).broadcast_to([P, HEADS, P]),
                       ALU.mult).then_inc(s_m, 1)

                def y(j):
                    if g3 is None:
                        return
                    p, js = u % 2, slice(j * L, (j + 1) * L)
                    if j == 0:
                        wait(dve, s_o, 2 * (g3 - 1))
                    dve.wait_ge(s_yp, GS * g3 + j + 1)
                    for c in range(ZT):
                        last = stt(out=ybuf[:, p, c, js], in0=xbc[:, p, c, js], scalar=dskip[:, c:c + 1],
                                   in1=yb[:, c * P:(c + 1) * P], op0=ALU.mult, op1=ALU.add)
                    last.then_inc(s_yd, 1)

                def mean_square():
                    if g4 is None:
                        return
                    dve.wait_ge(s_ssq, g4 + 1)
                    ts(ms[:, :], misc[:, SQC:SQC + GS], 1.0 / INNER, LNEPS, ALU.mult, ALU.add).then_inc(s_ms, 1)

                def residual(q):
                    if g4 is None:
                        return
                    p = (u + 1) % 2
                    if q == 0:
                        dve.wait_ge(s_rs, g4 + 1)
                        dve.wait_ge(s_hx, g4 + 1)
                        wait(dve, s_st[p], CREDIT + 16 * earlier(i, u, 3))
                    dve.wait_ge(s_o, 2 * g4 + q + 1)
                    for j in range(2):
                        last = stt(out=hr[:, p, 2 * q + j, 0:D], in0=misc[:, OUTC + j * D:OUTC + (j + 1) * D],
                                   scalar=rs[:, 2 * q + j:2 * q + j + 1], in1=hx[:, (u + 1) % 4, 2 * q + j, :],
                                   op0=ALU.mult, op1=ALU.add)
                    last.then_inc(s_h1, 1)

                def stats2():
                    if g4 is None:
                        return
                    dve.wait_ge(s_h1, 2 * g4 + 2)
                    norm_stats(lambda j: hr[:, (u + 1) % 2, j, 0:D], st2, mv2, ve2[:, :], chains["h1"]).then_inc(s_ve2, 1)
                    chains["h1"].end()

                def logits():
                    if g5 is None:
                        return
                    link = chains["pick1"]
                    dve.wait_ge(s_rt, g5 + 1)
                    wait(dve, s_el, CREDIT + g5)
                    link(tt(lg[:, :, :, :].rearrange("p j r e -> p j (r e)"),
                            misc[:, RTC:RTC + GS * 2 * NE].rearrange("p (j n) -> p j n", j=GS),
                            rb[:, :].unsqueeze(1).broadcast_to([P, GS, 2 * NE]), ALU.add))
                    link(v.tensor_reduce(m8[:, :, :], lg[:, :, :, :], AX.X, ALU.max))
                    tt(r8(dl), r8(lg), b8(m8), ALU.subtract).then_inc(s_d, 1)
                    link.end()

                def pick():
                    if g5 is None:
                        return
                    link = chains["pick2"]
                    dve.wait_ge(s_el, CREDIT + g5 + 1)
                    wait(dve, s_dest, CREDIT + g5)
                    link(v.tensor_reduce(e8[:, :, :], el[:, :, :, :], AX.X, ALU.max))
                    v.tensor_reduce(s8[:, :, :], el[:, :, :, :], AX.X, ALU.add)
                    link(tt(r8(pk), r8(el), b8(e8), ALU.is_equal))
                    link(tt(r8(pk), r8(pk), w4[:, :].unsqueeze(1).broadcast_to([P, GS * 2, NE]), ALU.mult))
                    link(v.tensor_reduce(m8[:, :, :], pk[:, :, :, :], AX.X, ALU.max))
                    link(tt(r8(oh), r8(pk), b8(m8), ALU.is_equal))
                    link(v.reciprocal(s8[:, :, :], s8[:, :, :]))
                    tt(conf[:, ds(GS * g5, GS)], s8[:, :, 0], e8[:, :, 0], ALU.mult)
                    v.tensor_copy(ohc[:, ds(GS * g5, GS), :], oh[:, :, 0, :])
                    v.tensor_copy(ohu[:, ds(GS * g5, GS), :], oh[:, :, 1, :])
                    for j in range(GS):
                        ins = tt(acc[:, j + 1, :], acc[:, j, :], oh[:, j, 0, :], ALU.add)
                        if j < GS - 1:
                            link(ins)
                    ins.then_inc(s_oh, 1)

                def places():
                    if g5 is None:
                        return
                    p, link = u % 2, chains["pick2"]
                    dve.wait_ge(s_pf, g5 + 1)
                    link(tt(dst[:, :, :], misc[:, PFC:PFC + GS * NE].rearrange("p (j e) -> p j e", j=GS), oh[:, :, 0, :],
                            ALU.mult))
                    link(v.tensor_reduce(dest[:, :], dst[:, :, :], AX.X, ALU.add))
                    link.end()
                    wait(dve, s_scd, CREDIT + g5 - 1)
                    v.tensor_copy(acc[:, 0, :], acc[:, GS, :])
                    v.tensor_copy(desti[:, p, :], dest[:, :])
                    v.tensor_copy(toki[:, p, :], tok[:, ds(GS * g5, GS)]).then_inc(s_dest, 1)

                steps_abs()
                conv(0)
                weights(0)
                clip()
                conv(1)
                y(0)
                mean_square()
                conv(2)
                weights(1)
                steps_softplus()
                conv(3)
                logits()
                y(1)
                conv(4)
                weights(2)
                residual(0)
                pick()
                y(2)
                residual(1)
                weights(3)
                stats2()
                y(3)
                places()
                if g1 is not None:
                    quantise(g1 + 1, u + 1, earlier(i, u + 1, 0))
                for n in ("tap", "ssd", "soft"):
                    if n in chains:
                        chains[n].end()

            pipeline(dve, body)
            nf = [0]

            def link(ins):
                nf[0] += 1
                ins.then_inc(c_find, 1)
                dve.wait_ge(c_find, nf[0])

            dve.wait_ge(s_dest, CREDIT + NG)
            dve.sem_inc(s_cmp, 1)
            link(v.tensor_copy(trow[:, 0, :], iota[:, :]))
            dve.wait_ge(s_cnt, 1)

            def tile_table(table, n, counts):
                link(tt(lst[:, 0, :], counts, base_e[:, :], ALU.subtract))
                link(ts(lst[:, 1, :], lst[:, 0, :], float(P - 1), 1.0 / P, ALU.add, ALU.mult))
                link(ts(lst[:, 1, :], lst[:, 1, :], 0.5 - 0.5 / P, MAGIC, ALU.subtract, ALU.add))
                link(ts(lst[:, 1, :], lst[:, 1, :], MAGIC, None, ALU.subtract))
                link(v.tensor_copy(lst[:, 2, 0:1], lst[:, 1, 0:1]))
                for e in range(1, NE):
                    link(tt(lst[:, 2, e:e + 1], lst[:, 2, e - 1:e], lst[:, 1, e:e + 1], ALU.add))
                link(ts(lst[:, 3, :], lst[:, 1, :], -float(P), float(LIST), ALU.mult, ALU.add))
                r = trow[:, :, 0:n]
                link(ts(r[:, 1, :], r[:, 0, :], float(P), None, ALU.mult))
                link(v.memset(r[:, 2, :], 0.0))
                for e in range(NE - 1):
                    link(ts(r[:, 3, :], r[:, 0, :], lst[:, 2, e:e + 1], None, ALU.is_ge))
                    link(tt(r[:, 2, :], r[:, 2, :], r[:, 3, :], ALU.add))
                    link(stt(out=r[:, 1, :], in0=r[:, 3, :], scalar=lst[:, 3, e:e + 1], in1=r[:, 1, :],
                             op0=ALU.mult, op1=ALU.add))
                link(ts(lst[:, 3, 0:1], lst[:, 2, NE - 1:NE], 0.5 * (UT - 1), 1.0 / UT, ALU.add, ALU.mult))
                link(ts(lst[:, 3, 0:1], lst[:, 3, 0:1], MAGIC, MAGIC, ALU.add, ALU.subtract))
                link(ts(lst[:, 3, 0:1], lst[:, 3, 0:1], 1.0, None, ALU.max))
                v.tensor_copy(turns_u[:, :], lst[:, 3, 0:1])
                v.tensor_copy(table[:, 0, :], r[:, 1, :])
                v.tensor_copy(table[:, 1, :], r[:, 2, :]).then_inc(s_tab, 1)

            tile_table(tile_c, CT, yb[0:1, 0:NE])

            for p in range(2):
                dve.wait_ge(s_st[p], CREDIT + 16 * (NG // 2))
                dve.wait_ge(s_sc[p], 64 * (NG // 2))
            dve.wait_ge(s_gath[0], 64 * (NG // 2 + 1))
            dve.sem_inc(s_free, 1)
            v.memset(fx_b[DB:DB + 1, :, :], 1.0)
            v.memset(zero[:, :], 0.0)
            v.memset(og[:, :, :], 0.0)
            link(v.memset(step[:, :], 1.0))
            link(v.memset(thr[:, :], 0.0))

            by_e = lambda t_: t_[:, :, :].rearrange("p b e -> p e b")
            confb = conf[:, :].unsqueeze(1).broadcast_to([P, NE, SEQS])
            eb = lambda t_: t_[:, :].unsqueeze(2).broadcast_to([P, NE, SEQS])
            link(tt(key[:, :, :], by_e(ohc), confb, ALU.mult))
            link(stt(out=key[:, :, :], in0=by_e(ohc), scalar=1.0, in1=key[:, :, :], op0=ALU.subtract, op1=ALU.add))
            link(tt(cand[:, :], thr[:, :], step[:, :], ALU.add))
            tt(cmp_[:, :, :], key[:, :, :], eb(cand), ALU.is_ge).then_inc(s_cmp, 1)
            dve.sem_inc(s_keys, 1)
            counts = misc[:, 0:NE * SEQS].rearrange("p (e b) -> p e b", e=NE)

            def search(t):
                link = Chain(dve, ch["find"], t, STEPS["find"])
                dve.wait_ge(s_cnt, t + 2)
                link(v.tensor_reduce(tot[:, :], counts, AX.X, ALU.add))
                link(ts(tot[:, :], tot[:, :], float(CAP), None, ALU.is_ge))
                link(tt(tot[:, :], tot[:, :], step[:, :], ALU.mult))
                link(tt(thr[:, :], thr[:, :], tot[:, :], ALU.add))
                link(ts(step[:, :], step[:, :], 0.5, None, ALU.mult))
                link(tt(cand[:, :], thr[:, :], step[:, :], ALU.add))
                link.end()
                tt(cmp_[:, :, :], key[:, :, :], eb(cand), ALU.is_ge).then_inc(s_cmp, 1)

            def above():
                dve.wait_ge(s_cmp, BITS + 2)
                tt(cmp_[:, :, :], key[:, :, :], eb(thr), ALU.is_gt).then_inc(s_cmp, 1)
                link(tt(eqk[:, :, :], key[:, :, :], eb(thr), ALU.is_equal))

            def at_threshold():
                dve.wait_ge(s_cnt, BITS + 2)
                link(v.tensor_reduce(tot[:, :], counts, AX.X, ALU.add))
                link(ts(need[:, :], tot[:, :], -1.0, float(CAP), ALU.mult, ALU.add))
                for e in range(NE):
                    last = v.tensor_tensor_scan(out=scn[:, e, :], data0=eqk[:, e, :], data1=zero[:, :], initial=0.0,
                                                op0=ALU.add, op1=ALU.add)
                link(last)
                tt(scn[:, :, :], scn[:, :, :], eqk[:, :, :], ALU.subtract).then_inc(s_cmp, 1)

            def dropped():
                dve.wait_ge(s_cnt, BITS + 3)
                link(tt(tmp[:, :, :], counts, eb(need), ALU.is_lt))
                link(tt(tmp[:, :, :], tmp[:, :, :], eqk[:, :, :], ALU.mult))
                link(tt(tmp[:, :, :], tmp[:, :, :], cmp_[:, :, :], ALU.add))
                link(ts(tmp[:, :, :], tmp[:, :, :], -1.0, 1.0, ALU.mult, ALU.add))
                link(tt(tmp[:, :, :], tmp[:, :, :], by_e(ohc), ALU.mult))
                link(v.tensor_reduce(drop[:, :], tmp[:, :, :].rearrange("p e b -> p b e"), AX.X, ALU.add))
                link(tt(cmp_[:, :, :], by_e(ohu), drop[:, :].unsqueeze(1).broadcast_to([P, NE, SEQS]), ALU.mult))
                for e in range(NE):
                    last = v.tensor_tensor_scan(out=scn[:, e, :], data0=cmp_[:, e, :], data1=zero[:, :],
                                                initial=float(e * LIST // P), op0=ALU.add, op1=ALU.add)
                link(last)
                link(v.tensor_copy(tot[:, :], scn[:, :, SEQS - 1]))
                tt(scn[:, :, :], scn[:, :, :], cmp_[:, :, :], ALU.subtract).then_inc(s_cmp, 1)

            def slots():
                dve.wait_ge(s_cnt, BITS + 4)
                link(tt(tmp[:, :, :], counts, cmp_[:, :, :], ALU.mult))
                link(v.tensor_reduce(slotf[:, :], tmp[:, :, :].rearrange("p e b -> p b e"), AX.X, ALU.add))
                link(ts(drop[:, :], drop[:, :], -NO_SLOT, NO_SLOT, ALU.mult, ALU.add))
                link(tt(slotf[:, :], slotf[:, :], drop[:, :], ALU.add))
                v.tensor_copy(slot_u[:, :], slotf[:, :]).then_inc(s_slot, 1)
                dve.wait_ge(s_cnt, BITS + 5)
                tile_table(tile_u, DT_, yb[0:1, 0:NE])

            def experts(m):
                def body(i, u, t, between=None):
                    T = T0[m] + t
                    wait(dve, fm2, T - 1)
                    for n, b in enumerate((sg0, sg1)):
                        dve.wait_ge(f_h, 2 * T + n + 1)
                        v.tensor_copy(ht[:, u % 2, n * FH:(n + 1) * FH], b[:, 0:FH]).then_inc(f_ht, 1)
                    if between is not None:
                        between()
                    dve.wait_ge(fm2, T + 1)
                    rest = xg[:, u, 0:D] if m == 0 else og[:, u, :]
                    tt(osb[:, u, :], cx[:, 0:D], rest, ALU.add).then_inc(f_o, 1)

                def searching(i, u, t):
                    body(i, u, t, lambda: search(t))

                def ranking(i, u, t):
                    body(i, u, t, (above, at_threshold, dropped, slots)[u])

                if m == 0:
                    turn(0, searching)
                    with dve.Fori(1, SEARCH) as i:
                        turn(i, searching)
                    turn(SEARCH, ranking)
                    with dve.Fori(SEARCH + 1, TURNS[0]) as i:
                        turn(i, body)
                else:
                    dve.wait_ge(s_tab, 2)
                    turns(dve, 1, body)
            experts(0)
            experts(1)


_INS = ["x_t", "table", "w_in", "conv_w", "conv_b", "dt_bias", "a_log", "d_skip", "norm_w", "gate", "w_out",
        "w_route", "b_route", "w4", "iota", "base_e", "w1c", "w2c", "b2c", "w1u", "w2u", "b2u"]


def kernel(x, L0_tok_weight, L0_attn_gate1, L0_attn_in_proj_w, L0_attn_conv_w, L0_attn_conv_b, L0_attn_dt_bias,
           L0_attn_A_log, L0_attn_D, L0_attn_norm_w, L0_attn_out_proj_w, L0_ffn_Wsc, L0_ffn_bsc, L0_ffn_W1c, L0_ffn_b1c,
           L0_ffn_W2c, L0_ffn_b2c, L0_ffn_Wsu, L0_ffn_bsu, L0_ffn_W1u, L0_ffn_b1u, L0_ffn_W2u, L0_ffn_b2u):
    import numpy as np
    import concourse.bacc as bacc
    from concourse.bass_utils import run_bass_kernel_spmd as run

    def rows(v):
        return np.broadcast_to(np.asarray(v).reshape(1, -1), (P, np.asarray(v).size))

    a = {
        "x_t": np.asarray(x).T, "table": L0_tok_weight, "w_in": np.asarray(L0_attn_in_proj_w).T, "conv_w": L0_attn_conv_w,
        "conv_b": np.asarray(L0_attn_conv_b).reshape(XT, P).T, "dt_bias": rows(L0_attn_dt_bias), "a_log": rows(L0_attn_A_log),
        "d_skip": np.repeat(np.asarray(L0_attn_D), HD).reshape(ZT, P).T, "norm_w": np.asarray(L0_attn_norm_w).reshape(ZT, P).T,
        "gate": rows(L0_attn_gate1), "w_out": np.asarray(L0_attn_out_proj_w).T,
        "w_route": np.concatenate([L0_ffn_Wsc, L0_ffn_Wsu], axis=1),
        "b_route": rows(np.concatenate([L0_ffn_bsc, L0_ffn_bsu])),
        "w4": np.broadcast_to(np.arange(NE, 0, -1, dtype=np.float32), (P, NE)),
        "iota": np.arange(CT, dtype=np.float32).reshape(1, CT),
        "base_e": (np.arange(NE) * LIST).astype(np.float32).reshape(1, NE),
        "w1c": np.concatenate([L0_ffn_W1c, np.asarray(L0_ffn_b1c)[:, None, :]], axis=1), "w2c": L0_ffn_W2c,
        "b2c": np.asarray(L0_ffn_b2c).reshape(1, -1),
        "w1u": np.concatenate([L0_ffn_W1u, np.asarray(L0_ffn_b1u)[:, None, :]], axis=1), "w2u": L0_ffn_W2u,
        "b2u": np.asarray(L0_ffn_b2u).reshape(1, -1),
    }
    nc = bacc.Bacc("TRN2", target_bir_lowering=False, num_devices=1)
    arrays, args = {}, {}
    for name in _INS:
        arrays[f"in_{name}_dram"] = np.ascontiguousarray(a[name])
        args[name] = nc.dram_tensor(f"in_{name}_dram", arrays[f"in_{name}_dram"].shape,
                                    mybir.dt.from_np(arrays[f"in_{name}_dram"].dtype), kind="ExternalInput").ap()
    out = nc.dram_tensor("out_0_dram", (SEQS, L, D), F32, kind="ExternalOutput").ap()
    build(nc, args, out)
    r = run(nc, [arrays], core_ids=[0])
    return r.results[0]["out_0_dram"]
```

```python
from contextlib import ExitStack

import concourse.bass as bass
from concourse import mybir

F32 = mybir.dt.float32
I32 = mybir.dt.int32
BF16 = mybir.dt.bfloat16
ALU = mybir.AluOpType
ACT = mybir.ActivationFunctionType
AX = mybir.AxisListType
ds = bass.ds

P = 128
SEQS, L = 64, 128
NT = SEQS * L
D = 192
DB = D - P
GS = 4
NG = SEQS // GS
GL = GS * L
INNER, STATE, TAPS, HD = 384, 128, 4, 64
HEADS = INNER // HD
XBC = INNER + 2 * STATE
XT, ZT = XBC // P, INNER // P
PROJ = 2 * INNER + 2 * STATE + HEADS
F = 768
FC = F // P
FH = F // 2
NE = 4
CAP = NT // NE
LIST = NT
NLIST = NE * LIST + P
DUMMY = NT
UT = 4
TL = UT * P
TT = (NT // TL + NE, (NT - CAP) // TL + NE)
TS = NT // TL
BITS = 28
SEARCH = BITS // UT
LISTING = SEARCH + 2
CREDIT = 1
MAGIC = 12582912.0
QMAX, QEPS, LNEPS = 127.0, 1e-8, 1e-5
NO_SLOT = 40000.0

STEPS = dict(quant=4, clip=4, tap=10, dt0=1, soft=12, ssd=4, h1=2, pick1=2, pick2=11, find=6)


def wait(eng, sem, value):
    if not (isinstance(value, int) and value <= 0):
        eng.wait_ge(sem, value)


def wait_apart(eng, sem, value, marks):
    if not (isinstance(value, int) and value <= 0):
        eng.wait_ge(sem, value)
        if not isinstance(value, int):
            eng.sem_inc(marks, 1)


class Chain:

    def __init__(self, eng, sem, turn, steps):
        self.eng, self.sem, self.base, self.steps, self.n = eng, sem, turn * steps, steps, 0

    def __call__(self, ins, marks=None):
        self.n += 1
        ins.then_inc(self.sem, 1)
        if marks is None:
            self.eng.wait_ge(self.sem, self.base + self.n)
        else:
            wait_apart(self.eng, self.sem, self.base + self.n, marks)

    def end(self):
        assert self.n == self.steps, (self.n, self.steps)


def stages(i, u):
    it = 4 * i + u
    return [it - k if not isinstance(it, int) or 0 <= it - k < NG else None for k in range(5)]


def earlier(i, u, k):
    return 2 * i + (u - k) // 2


def pipeline(eng, body):
    for u in range(4):
        body(0, u)
    with eng.Fori(1, NG // 4) as i:
        for u in range(4):
            body(i, u)
    for u in range(4):
        body(NG // 4, u)


def build(nc, A, out):
    with ExitStack() as ctx:
        def sb(name, shape, dt=F32, c=ctx):
            return c.enter_context(nc.sbuf_tensor(name, shape, dt))

        def sem(name):
            return ctx.enter_context(nc.semaphore(name))

        def bank(name):
            return ctx.enter_context(nc.psum_tensor(name, [P, 512], F32))

        hr_dram = nc.dram_tensor("hr_dram", [NT + P, 2 * D], F32, kind="Internal").ap()
        list_c = nc.dram_tensor("list_c", [NLIST, 1], I32, kind="Internal").ap()
        list_u = nc.dram_tensor("list_u", [NLIST, 1], I32, kind="Internal").ap()
        out_rows = out.rearrange("b l c -> (b l) c")

        ident = sb("ident", [P, P])
        ones = sb("ones", [P, P])
        le = sb("le", [P, P])
        lt = sb("lt", [P, P])
        gt = sb("gt", [P, P])
        neghalf = sb("neghalf", [P, GS])
        fill = sb("fill", [P, NLIST // P], I32)
        zrow = sb("zrow", [P, 2 * D])
        tok = sb("tok", [P, SEQS], I32)
        xids = sb("xids", [P, SEQS + GS], I32)
        w4 = sb("w4", [P, NE])
        conf = sb("conf", [P, SEQS])
        ohc = sb("ohc", [P, SEQS, NE])
        ohu = sb("ohu", [P, SEQS, NE])
        acc = sb("acc", [P, GS + 1, NE])
        w1a = sb("w1a", [P, NE * F])
        w1b = sb("w1b", [P, NE * FH])
        w2s = sb("w2s", [P, NE * FC * D])
        b1s, b2s = sb("b1s", [P, NE * FC]), sb("b2s", [P, NE * D])
        turn_of = [sb(f"turn_of{m}", [1, 2, TT[m] + 1], I32) for m in range(2)]
        turns_n = [sb(f"turns_n{m}", [1, 1], I32) for m in range(2)]
        lst = sb("lst", [1, 4, NE])
        trow = sb("trow", [1, 4, TT[0] + 1])
        slot_u = sb("slot_u", [P, SEQS], I32)
        iota = sb("iota", [1, TT[0] + 1])
        base_e = sb("base_e", [1, NE])

        a = ctx.enter_context(ExitStack())
        win_a, win_b = sb("win_a", [P, PROJ], c=a), sb("win_b", [DB, PROJ], c=a)
        cw, cb = sb("cw", [P, XT, TAPS], c=a), sb("cb", [P, XT], c=a)
        wo = sb("wo", [P, ZT, D], c=a)
        nw, dskip = sb("nw", [P, ZT], c=a), sb("dskip", [P, ZT], c=a)
        dtb, nega = sb("dtb", [P, HEADS], c=a), sb("nega", [P, HEADS], c=a)
        gate = sb("gate", [P, 1], c=a)
        wr_a, wr_b, rb = sb("wr_a", [P, 2 * NE], c=a), sb("wr_b", [DB, 2 * NE], c=a), sb("rb", [P, 2 * NE], c=a)
        gidx = sb("gidx", [P, 2, GS], I32, c=a)
        gath = sb("gath", [P, 2, GS, D], c=a)
        h0 = sb("h0", [P, GS, D], c=a)
        xn = sb("xn", [P, GS, D], c=a)
        hx = sb("hx", [P, 4, GS, D], c=a)
        q1 = sb("q1", [P, 3, GS], c=a)
        st1, mv1 = sb("st1", [P, GS, 6], c=a), sb("mv1", [P, GS, 2], c=a)
        ve1, rstd1 = sb("ve1", [P, 2, GS], c=a), sb("rstd1", [P, 2, GS], c=a)
        xt_a, xt_b = sb("xt_a", [P, 2, GL], c=a), sb("xt_b", [DB, 2, GL], c=a)
        xbc = sb("xbc", [P, 2, XT, GL], c=a)
        zs = sb("zs", [P, 2, ZT, GL], c=a)
        dtr, dab, dtu = (sb(n, [P, 2, GS, HEADS], c=a) for n in ("dtr", "dab", "dtu"))
        dts, dta = sb("dts", [P, 2, GS, HEADS], c=a), sb("dta", [P, 2, GS, HEADS], c=a)
        sp1, sp2, sp3 = (sb(n, [P, GS, HEADS], c=a) for n in ("sp1", "sp2", "sp3"))
        seg_l = sb("seg_l", [P, 2, HEADS, P], c=a)
        dec = sb("dec", [P, 2, HEADS, P], c=a)
        mix = sb("mix", [P, 2, HEADS, P], c=a)
        cbm = sb("cbm", [P, P], c=a)
        xd = sb("xd", [P, 2, INNER], c=a)
        ybuf = sb("ybuf", [P, 2, ZT, GL], c=a)
        ysq = sb("ysq", [P, ZT, GL], c=a)
        ms, rs = sb("ms", [P, GS], c=a), sb("rs", [P, GS], c=a)
        hr = sb("hr", [P, 2, GS, 2 * D], c=a)
        st2, mv2 = sb("st2", [P, GS, 6], c=a), sb("mv2", [P, GS, 2], c=a)
        ve2, rstd2, nm2 = (sb(n, [P, GS], c=a) for n in ("ve2", "rstd2", "nm2"))
        x2t_a, x2t_b = sb("x2t_a", [P, GL], c=a), sb("x2t_b", [DB, GL], c=a)
        lg, dl, el, pk = (sb(n, [P, GS, 2, NE], c=a) for n in ("lg", "dl", "el", "pk"))
        oh = sb("oh", [P, GS, 2, NE], c=a)
        m8, e8, s8 = (sb(n, [P, GS, 2], c=a) for n in ("m8", "e8", "s8"))
        dst = sb("dst", [P, GS, NE], c=a)
        dest = sb("dest", [P, GS], c=a)
        desti, toki = sb("desti", [P, 2, GS], I32, c=a), sb("toki", [P, 2, GS], I32, c=a)
        a.close()
        w1a_u = sb("w1a_u", [P, NE * F])
        w1b_u = sb("w1b_u", [P, NE * FH])
        w2s_u = sb("w2s_u", [P, NE * FC * D])
        b1s_u, b2s_u = sb("b1s_u", [P, NE * FC]), sb("b2s_u", [P, NE * D])

        key, cmp_, eqk = sb("key", [P, NE, SEQS]), sb("cmp_", [P, NE, SEQS]), sb("eqk", [P, NE, SEQS])
        scn, tmp = sb("scn", [P, NE, SEQS]), sb("tmp", [P, NE, SEQS])
        thr, cand, tot, step, need = (sb(n, [P, NE]) for n in ("thr", "cand", "tot", "step", "need"))
        zero = sb("zero", [P, SEQS])
        drop = sb("drop", [P, SEQS])
        slotf = sb("slotf", [P, SEQS])
        slot4, tok4 = sb("slot4", [P, 2, GS], I32), sb("tok4", [P, 2, GS], I32)
        ids = sb("ids", [P, UT, 1], I32)
        xg = sb("xg", [P, UT, 2 * D])
        og = sb("og", [P, UT, D])
        w1a_t, w1b_t = sb("w1a_t", [P, F]), sb("w1b_t", [P, FH])
        ids_s = sb("ids_s", [P, UT, 1], I32)
        fx_a, fx_b = sb("fx_a", [P, 2, P]), sb("fx_b", [P, 2, P])
        NC = NE * SEQS + NE
        cnt_a, cnt_b, ones_b, lt_b = (sb(n, [P, w], BF16) for n, w in (("cnt_a", NC), ("cnt_b", NC), ("ones_b", P), ("lt_b", P)))
        ht = sb("ht", [P, 2, F])
        osb = sb("osb", [P, UT, D])

        tp, mm0, mm1, sg0, sg1, cx, yb, misc = (bank(n) for n in ("tp", "mm0", "mm1", "sg0", "sg1", "cx", "yb", "misc"))
        mm = [mm0, mm1]
        hid, outp = ((mm0, mm1), (sg0, sg1)), (cx, yb)
        DTC, SQC, RTC, PFC, OUTC = 0, 32, 64, 96, 128

        s_ids, s_wa, s_wc, s_wu, s_fill = sem("token_ids"), sem("weights_a"), sem("weights_c"), sem("weights_u"), sem("lists_filled")
        s_const, s_prep, s_pe_, s_sig = sem("constants"), sem("prepared"), sem("exp_a_log"), sem("exp_gate")
        s_idx = sem("gather_index")
        s_gath = [sem(f"gathered{p}") for p in range(2)]
        s_ve, s_rstd, s_xn, s_hx = sem("var1"), sem("rstd1_s"), sem("xn_s"), sem("hx_s")
        s_tr1, s_xt = sem("transposed1"), sem("xt_s")
        s_mm, s_ci, s_cv, s_xbc, s_z = sem("projected"), sem("conv_started"), sem("conv_done"), sem("xbc_s"), sem("z_s")
        s_zc = sem("z_copied")
        s_nm2, s_nr2 = sem("mean_times_rstd"), sem("shift2_s")
        s_dtp, s_dab, s_u, s_dt = sem("dt_projected"), sem("dt_abs"), sem("dt_exp"), sem("dt_s")
        s_sl, s_sg, s_e, s_cx, s_xd, s_m, s_yp, s_yd, s_y2 = (sem(n) for n in (
            "seg_left", "seg_sums", "decays", "cb_and_x", "xd_s", "mixed", "y_product", "y_read", "y_gated"))
        s_sq, s_sqa, s_ssq, s_ms, s_rs, s_o, s_h1, s_ve2, s_rstd2, s_xn2 = (sem(n) for n in (
            "y_squared", "y_squares_added", "y_sums", "mean_square", "rms", "out_product", "h1_s", "var2", "rstd2_s", "xn2_s"))
        s_tr2, s_x2t, s_rt, s_d, s_el, s_oh, s_pf, s_dest = (sem(n) for n in (
            "transposed2", "x2t_s", "routers", "logits", "router_exp", "one_hot", "prefixes", "dest_s"))
        s_st = [sem(f"stored{p}") for p in range(2)]
        s_sc = [sem(f"listed{p}") for p in range(2)]
        c_pool, c_sqa = sem("pool_chain"), sem("chain_squares")
        ch = {n: sem(f"chain_{n}") for n in STEPS}
        s_cmp, s_cnt, s_tab, s_slot = sem("compared"), sem("counted"), sem("tiles_listed"), sem("slots_found")
        s_s4 = sem("slot_copied")
        s_scd = sem("listed")
        s_su = [sem(f"listed_u{p}") for p in range(2)]
        s_dts, s_free = sem("dt_values"), sem("stage_a_done")
        marks_dve, marks_pe, marks_pool, marks_act, marks_sp = (
            sem(f"marks_{n}") for n in ("dve", "pe", "pool", "act", "sp"))
        c_setup, c_find = sem("chain_setup"), sem("chain_lists")

        block = ctx.enter_context(nc.Block())

        hr_by_seq = hr_dram[0:NT, :].rearrange("(b l) c -> l b c", l=L)
        n_wa = 16 * 16
        n_w = 16 * (2 + 4 * NE)

        def of_both(name):
            return [sem(f"{name}{m}") for m in range(2)]

        f_w, f_c, f_t, f_x, f_m1, f_ge, f_m2, f_r, f_o = (of_both(n) for n in (
            "turn_weights", "tile_ids_copied",
            "tile_transposed", "tile_x", "tile_hidden_product", "tile_gelu", "tile_out_product", "tile_rest", "tile_out"))
        f_id, f_g, f_s = ([[sem(f"{n}{m}_{u}") for u in range(UT)] for m in range(2)]
                          for n in ("tile_ids", "tile_gathered", "tile_scattered"))
        s_first = sem("first_mixture_done")

        def turn(i, body):
            for u in range(UT):
                body(i, u, i * UT + u)

        def turns(eng, m, body, start=1):
            n = 2 + eng.value_load(turns_n[m][0:1, 0:1], min_val=0, max_val=TT[m] - 2)
            with eng.Fori(start, TT[m]) as i:
                with eng.If(i < n):
                    turn(i, body)
            return n

        def load_biases(eng, to, names, done):
            for dst_, name in zip(to, names):
                eng.dma_start(dst_[:, :], A[name]).then_inc(done, 16)

        def load_expert(eng, e, to, names, done):
            w1a_, w1b_, w2_ = to
            w1, w2 = (A[n] for n in names)
            eng.dma_start(w1a_[:, ds(e * F, F)], w1[ds(e, 1), 0:P, :].rearrange("e p f -> p (e f)")).then_inc(done, 16)
            for n in range(2):
                eng.dma_start(w1b_[n * DB:(n + 1) * DB, ds(e * FH, FH)],
                              w1[ds(e, 1), P:D, n * FH:(n + 1) * FH].rearrange("e p f -> p (e f)")).then_inc(done, 16)
            eng.dma_start(w2_[:, ds(e * FC * D, FC * D)].rearrange("p (c n) -> p c n", c=FC),
                          w2[ds(e, 1), :, :].rearrange("e (c p) n -> p (e c) n", p=P)).then_inc(done, 16)

        def experts_sp(sp, m):
            sp.wait_ge(s_tab, m + 1)
            if m == 0:
                sp.wait_ge(s_fill, 48)
                for p in range(2):
                    sp.wait_ge(s_sc[p], 64 * (NG // 2))
            else:
                for p in range(2):
                    sp.wait_ge(s_su[p], 64 * (NG // 2))
                sp.wait_ge(s_first, 1)
            lists = (list_c, list_u)[m]

            def body(i, u, t):
                row = sp.value_load(turn_of[m][0:1, 0, ds(i, 1)], min_val=0, max_val=NLIST - TL)
                wait_apart(sp, f_c[m], UT * (i - 1) + u + 1, marks_sp)
                wait_apart(sp, f_g[m][u], 16 * (m + 1) * i, marks_sp)
                sp.dma_start(ids[:, u, :], lists[ds(row + u * P, P), :]).then_inc(f_id[m][u], 16)
            turn(0, body)
            turns(sp, m, body)

        @block.sync
        def _(sp):
            sp.dma_start(xids[:, 0:SEQS], A["x_t"]).then_inc(s_ids, 16)
            for dst_, src in (
                (win_a[:, :], A["w_in"][0:P, :]), (win_b[:, :], A["w_in"][P:D, :]),
                (cw[:, :, :], A["conv_w"].rearrange("(m p) k -> p m k", p=P)),
                (cb[:, :], A["conv_b"]),
                (dtb[:, :], A["dt_bias"]), (nega[:, :], A["a_log"]), (dskip[:, :], A["d_skip"]),
                (nw[:, :], A["norm_w"]), (gate[:, :], A["gate"]),
                (wo[:, :, :], A["w_out"].rearrange("(m p) n -> p m n", p=P)),
                (wr_a[:, :], A["w_route"][0:P, :]), (wr_b[:, :], A["w_route"][P:D, :]), (rb[:, :], A["b_route"]),
                (w4[:, :], A["w4"]), (iota[:, :], A["iota"]), (base_e[:, :], A["base_e"]),
            ):
                sp.dma_start(dst_, src).then_inc(s_wa, 16)
            sp.wait_ge(s_const, 1)
            for lst_ in (list_c, list_u):
                sp.dma_start(lst_.rearrange("(p n) o -> p (n o)", p=P), fill[:, :]).then_inc(s_fill, 16)
            sp.dma_start(hr_dram[NT:NT + P, :], zrow[:, :]).then_inc(s_fill, 16)
            sp.wait_ge(s_xn, 1)
            load_biases(sp, (b1s, b2s), ("b1c", "b2c"), s_wc)
            for e in range(NE):
                load_expert(sp, e, (w1a, w1b, w2s), ("w1c", "w2c"), s_wc)

            def body(i, u):
                g = stages(i, u)[3]
                if g is not None:
                    sp.wait_ge(s_xn2, g + 1)
                    sp.dma_start(hr_by_seq[:, ds(GS * g, GS), :], hr[:, (u + 1) % 2, :, :]).then_inc(s_st[(u + 1) % 2], 16)
            pipeline(sp, body)

            experts_sp(sp, 0)
            experts_sp(sp, 1)

        @block.gpsimd
        def _(pool):
            chain = [0]

            def link(ins):
                chain[0] += 1
                ins.then_inc(c_pool, 1)
                pool.wait_ge(c_pool, chain[0])

            nc.gpsimd.memset(fill[:, :], DUMMY)
            link(nc.gpsimd.memset(zrow[:, :], 0.0))
            nc.gpsimd.memset(xids[:, SEQS:SEQS + GS], 0)
            nc.gpsimd.memset(neghalf[:, :], -0.5)
            nc.gpsimd.iota(tok[:, :], pattern=[[L, SEQS]], base=0, channel_multiplier=1)
            link(nc.gpsimd.memset(ones[:, :], 1.0))
            for t_, off, mul, pat in ((le, 0, -1, 1), (lt, -1, -1, 1), (gt, -1, 1, -1)):
                nc.gpsimd.affine_select(out=t_[:, :], in_=ones[:, :], compare_op=ALU.is_ge, fill=0.0, base=off,
                                        pattern=[[pat, P]], channel_multiplier=mul)
            link(nc.gpsimd.affine_select(out=ident[:, :], in_=ones[:, :], compare_op=ALU.is_equal, fill=0.0, base=0,
                                         pattern=[[-1, P]], channel_multiplier=1))
            for e in range(NE):
                last = nc.gpsimd.memset(acc[:, 0, e:e + 1], float(e * LIST // P))
            for s_ in (s_oh, s_el, s_dest, s_scd, s_rt, s_x2t, s_d, *s_st):
                pool.sem_inc(s_, CREDIT)
            pool.sem_inc(s_scd, 1)
            last.then_inc(s_const, 1)
            pool.wait_ge(s_const, 1)
            pool.wait_ge(s_ids, 16)

            def gather(g, u):
                p = u % 2
                wait_apart(pool, s_ve, g - 1, marks_pool)
                nc.gpsimd.tensor_copy(gidx[:, p, :], xids[:, ds(GS * g, GS)]).then_inc(s_idx, 1)
                wait_apart(pool, s_idx, g + 1, marks_pool)
                for j in range(GS):
                    nc.gpsimd.indirect_dma_start(
                        out=gath[:, p, j, :], out_offset=None, in_=A["table"][:, :],
                        in_offset=bass.IndirectOffsetOnAxis(ap=gidx[:, p, j:j + 1], axis=0)).then_inc(s_gath[p], 16)

            def body(i, u):
                g1, g2, g3, g4, g5 = stages(i, u)

                def seg_left(g, p, j):
                    wait_apart(pool, s_dt, g + 1, marks_pool)
                    wait_apart(pool, s_sg, GS * g + j - 1, marks_pool)
                    nc.gpsimd.tensor_tensor(seg_l[:, j % 2, :, :], le[:, :].unsqueeze(1).broadcast_to([P, HEADS, P]),
                                            dta[:, p, j, :].unsqueeze(2).broadcast_to([P, HEADS, P]),
                                            ALU.mult).then_inc(s_sl, 1)

                def gate_y(j):
                    if g3 is None:
                        return
                    p, js = u % 2, slice(j * L, (j + 1) * L)
                    if j == 0:
                        wait_apart(pool, s_z, g3 + 1, marks_pool)
                        wait_apart(pool, s_zc, ZT * (g3 + 1), marks_pool)
                    wait_apart(pool, s_yd, GS * g3 + j + 1, marks_pool)
                    nc.gpsimd.tensor_tensor(ybuf[:, p, :, js], ybuf[:, p, :, js], zs[:, p, :, js], ALU.mult).then_inc(s_y2, 1)

                if g4 is not None:
                    wait_apart(pool, s_sq, g4 + 1, marks_pool)
                    nc.gpsimd.tensor_tensor(ysq[:, 0, :], ysq[:, 0, :], ysq[:, 1, :], ALU.add).then_inc(c_sqa, 1)
                    wait_apart(pool, c_sqa, g4 + 1, marks_pool)
                    nc.gpsimd.tensor_tensor(ysq[:, 0, :], ysq[:, 0, :], ysq[:, 2, :], ALU.add).then_inc(s_sqa, 1)
                if g3 is not None:
                    seg_left(g3, u % 2, 2)
                gate_y(0)
                if g4 is not None:
                    wait_apart(pool, s_ms, g4 + 1, marks_pool)
                    nc.gpsimd.tensor_tensor(rs[:, :], ms[:, :], neghalf[:, :], ALU.pow).then_inc(s_rs, 1)
                if g3 is not None:
                    seg_left(g3, u % 2, 3)
                if g1 is not None:
                    wait_apart(pool, s_ve, g1 + 1, marks_pool)
                    nc.gpsimd.tensor_tensor(rstd1[:, u % 2, :], ve1[:, u % 2, :], neghalf[:, :], ALU.pow).then_inc(s_rstd, 1)
                    first = isinstance(g1, int) and g1 == 0
                    wait_apart(pool, s_rstd, g1 + 1, marks_pool)
                    wait_apart(pool, s_tr1, 2 * g1, marks_pool)
                    if not first:
                        for j in range(GS):
                            last = nc.gpsimd.tensor_scalar(xn[:, j, :], h0[:, j, :], mv1[:, j, 0:1],
                                                           rstd1[:, u % 2, j:j + 1], ALU.subtract, ALU.mult)
                        last.then_inc(s_xn, 1)
                gate_y(1)
                if g1 is not None:
                    gather(g1 + 1, u + 1)
                if g1 is not None:
                    wait_apart(pool, s_xn, g1 + 1, marks_pool)
                    wait_apart(pool, s_h1, 2 * (g1 - 3), marks_pool)
                    nc.gpsimd.tensor_tensor(hx[:, u % 4, :, :], h0[:, :, :], xn[:, :, :], ALU.add).then_inc(s_hx, 1)
                if g2 is not None:
                    seg_left(g2, (u + 1) % 2, 0)
                gate_y(2)
                if g4 is not None:
                    wait_apart(pool, s_ve2, g4 + 1, marks_pool)
                    nc.gpsimd.tensor_tensor(rstd2[:, :], ve2[:, :], neghalf[:, :], ALU.pow).then_inc(s_rstd2, 1)
                    wait_apart(pool, s_rstd2, g4 + 1, marks_pool)
                    nc.gpsimd.tensor_tensor(nm2[:, :], mv2[:, :, 0], rstd2[:, :], ALU.mult).then_inc(s_nm2, 1)
                    wait_apart(pool, s_nm2, g4 + 1, marks_pool)
                    nc.gpsimd.tensor_scalar(nm2[:, :], nm2[:, :], -1.0, 1.0, ALU.mult, ALU.mult).then_inc(s_nr2, 1)
                gate_y(3)
                if g2 is not None:
                    seg_left(g2, (u + 1) % 2, 1)
                if g5 is not None:
                    p = u % 2
                    wait_apart(pool, s_dest, CREDIT + g5 + 1, marks_pool)
                    for j in range(GS):
                        nc.gpsimd.indirect_dma_start(
                            out=list_c[:, :], out_offset=bass.IndirectOffsetOnAxis(ap=desti[:, p, j:j + 1], axis=0),
                            in_=toki[:, p, j:j + 1], in_offset=None).then_inc(s_sc[p], 16)
                if g5 is not None:
                    wait_apart(pool, s_sc[u % 2], 64 * (earlier(i, u, 4) + 1), marks_pool)
                    pool.sem_inc(s_scd, 1)

            gather(0, 0)
            wait_apart(pool, s_fill, 48, marks_pool)
            pipeline(pool, body)

            def list_dropped(i, p, half):
                g = 2 * i + p
                if half == 0:
                    wait_apart(pool, s_su[p], 64 * i, marks_pool)
                    nc.gpsimd.tensor_copy(slot4[:, p, :], slot_u[:, ds(GS * g, GS)])
                    nc.gpsimd.tensor_copy(tok4[:, p, :], tok[:, ds(GS * g, GS)]).then_inc(s_s4, 1)
                    wait_apart(pool, s_s4, g + 1, marks_pool)
                for j in range(GS // 2 * half, GS // 2 * (half + 1)):
                    nc.gpsimd.indirect_dma_start(
                        out=list_u[:, :], out_offset=bass.IndirectOffsetOnAxis(ap=slot4[:, p, j:j + 1], axis=0),
                        in_=tok4[:, p, j:j + 1], in_offset=None,
                        bounds_check=NE * LIST - 1, oob_is_err=False).then_inc(s_su[p], 16)

            def experts(m):
                def gather_tile(i, u, t):
                    wait_apart(pool, f_id[m][u], 16 * (i + 1), marks_pool)
                    wait_apart(pool, f_r[m], t - UT + 1, marks_pool)
                    wait_apart(pool, f_t[m], t - UT + 1, marks_pool)
                    nc.gpsimd.indirect_dma_start(
                        out=xg[:, u, :], out_offset=None, in_=hr_dram[:, :],
                        in_offset=bass.IndirectOffsetOnAxis(ap=ids[:, u, :], axis=0)).then_inc(f_g[m][u], 16)
                    if m == 1:
                        nc.gpsimd.indirect_dma_start(
                            out=og[:, u, :], out_offset=None, in_=out_rows,
                            in_offset=bass.IndirectOffsetOnAxis(ap=ids[:, u, :], axis=0),
                            bounds_check=NT - 1, oob_is_err=False).then_inc(f_g[m][u], 16)

                def scatter_tile(u, t):
                    wait_apart(pool, f_o[m], t + 1, marks_pool)
                    wait_apart(pool, f_c[m], t + 1, marks_pool)
                    nc.gpsimd.indirect_dma_start(
                        out=out_rows, out_offset=bass.IndirectOffsetOnAxis(ap=ids_s[:, u, :], axis=0),
                        in_=osb[:, u, :], in_offset=None, bounds_check=NT - 1, oob_is_err=False).then_inc(f_s[m][u], 16)

                def keep_numbers(u, t, i):
                    wait_apart(pool, f_s[m][u], 16 * i, marks_pool)
                    nc.gpsimd.tensor_copy(ids_s[:, u, :], ids[:, u, :]).then_inc(f_c[m], 1)

                def body(i, u, t, between=None):
                    if not (isinstance(t, int) and t < 1):
                        keep_numbers((u - 1) % UT, t - 1, i if u else i - 1)
                    gather_tile(i, u, t)
                    if between is not None:
                        between()
                    if not (isinstance(t, int) and t < UT):
                        scatter_tile(u, t - UT)

                def listing_turn(i):
                    for u in range(UT):
                        body(i, u, i * UT + u, lambda: list_dropped(i - LISTING, u // 2, u % 2))

                turn(0, body)
                turn(1, body)
                if m == 0:
                    with pool.Fori(2, LISTING) as i:
                        turn(i, body)
                    wait_apart(pool, s_slot, 1, marks_pool)
                    listing_turn(LISTING)
                    with pool.Fori(LISTING + 1, TS) as i:
                        listing_turn(i)
                    n = turns(pool, m, body, TS)
                    for g in range(TS - LISTING, NG // 2):
                        for k in range(4):
                            list_dropped(g, k // 2, k % 2)
                else:
                    n = turns(pool, m, body, 2)
                keep_numbers(UT - 1, UT * n - 1, n - 1)
                for u in range(UT):
                    scatter_tile(u, (n - 1) * UT + u)
                for u in range(UT):
                    wait_apart(pool, f_s[m][u], 16 * n, marks_pool)

            for p in range(2):
                wait_apart(pool, s_st[p], CREDIT + 16 * (NG // 2), marks_pool)
            experts(0)
            pool.sem_inc(s_first, 1)
            pool.wait_ge(s_tab, 2)
            experts(1)

        @block.scalar
        def _(act):
            act.wait_ge(s_wa, n_wa)
            nc.scalar.activation(nega[:, :], nega[:, :], ACT.Exp).then_inc(s_pe_, 1)
            nc.scalar.activation(gate[:, :], gate[:, :], ACT.Exp, scale=-1.0).then_inc(s_sig, 1)

            def body(i, u):
                g1, g2, g3, g4, g5 = stages(i, u)

                def decays(j):
                    if g3 is None:
                        return
                    act.wait_ge(s_sg, GS * g3 + j + 1)
                    wait(act, s_m, GS * g3 + j - 1)
                    nc.scalar.activation(dec[:, j % 2, 0:3, :], sg0[:, 0:3 * P].rearrange("p (h s) -> p h s", h=3), ACT.Exp)
                    nc.scalar.activation(dec[:, j % 2, 3:6, :], sg1[:, 0:3 * P].rearrange("p (h s) -> p h s", h=3),
                                         ACT.Exp).then_inc(s_e, 1)

                def start(m):
                    if g2 is None:
                        return
                    p = (u + 1) % 2
                    if m == 0:
                        wait(act, s_y2, GS * (g2 - 1))
                    act.wait_ge(s_mm, (XT + ZT) * g2 + m + 1)
                    if m < XT:
                        nc.scalar.activation(xbc[:, p, m, :], mm[m % 2][:, :], ACT.Identity, bias=cb[:, m:m + 1],
                                             scale=cw[:, m, TAPS - 1:TAPS]).then_inc(s_ci, 1)
                    elif m == XT:
                        nc.scalar.copy(zs[:, p, m - XT, :], mm[m % 2][:, :]).then_inc(s_zc, 1)
                    else:
                        nc.scalar.activation(zs[:, p, m - XT, :], mm[m % 2][:, :], ACT.Silu).then_inc(s_zc, 1)

                def silus():
                    if g2 is None:
                        return
                    p = (u + 1) % 2
                    act.wait_ge(s_cv, XT * (g2 + 1))
                    nc.scalar.activation(xbc[:, p, :, :], xbc[:, p, :, :], ACT.Silu).then_inc(s_xbc, 1)
                    act.wait_ge(s_zc, ZT * g2 + 1)
                    nc.scalar.activation(zs[:, p, 0, :], zs[:, p, 0, :], ACT.Silu).then_inc(s_z, 1)

                def from_tp(g, k, half):
                    rows = (P, DB)[half]
                    if g is None:
                        return
                    if k == 2:
                        act.wait_ge(s_tr2, 2 * g + half + 1)
                        wait(act, s_rt, CREDIT + g)
                        nc.scalar.copy((x2t_a, x2t_b)[half][:, :], tp[0:rows, :]).then_inc(s_x2t, 1)
                    else:
                        act.wait_ge(s_tr1, 2 * g + half + 1)
                        wait(act, s_mm, (XT + ZT) * (g - 1))
                        nc.scalar.copy((xt_a, xt_b)[half][:, u % 2, :], tp[0:rows, :]).then_inc(s_xt, 1)

                decays(0)
                if g2 is not None:
                    act.wait_ge(s_dab, g2 + 1)
                    nc.scalar.activation(dtu[:, (u + 1) % 2, :, :], dab[:, (u + 1) % 2, :, :], ACT.Exp,
                                         scale=-1.0).then_inc(s_u, 1)
                start(0)
                from_tp(g5, 2, 0)
                from_tp(g5, 2, 1)
                if g4 is not None:
                    act.wait_ge(s_y2, GS * (g4 + 1))
                    wait(act, s_ssq, g4)
                    nc.scalar.activation(ysq[:, :, :], ybuf[:, (u + 1) % 2, :, :], ACT.Square).then_inc(s_sq, 1)
                start(1)
                decays(1)
                start(2)
                start(3)
                decays(2)
                start(4)
                if g5 is not None:
                    act.wait_ge(s_d, CREDIT + g5 + 1)
                    wait(act, s_oh, CREDIT + g5)
                    nc.scalar.activation(el[:, :, :, :], dl[:, :, :, :], ACT.Exp).then_inc(s_el, 1)
                start(5)
                decays(3)
                silus()
                start(6)
                from_tp(g1, 1, 0)
                start(7)
                from_tp(g1, 1, 1)
                if g4 is not None:
                    p = (u + 1) % 2
                    act.wait_ge(s_nr2, g4 + 1)
                    for j in range(GS):
                        last = nc.scalar.activation(hr[:, p, j, D:2 * D], hr[:, p, j, 0:D], ACT.Identity,
                                                    bias=nm2[:, j:j + 1], scale=rstd2[:, j:j + 1])
                    last.then_inc(s_xn2, 1)

            pipeline(act, body)

            def experts(m):
                b1_ = (b1s, b1s_u)[m]

                def copy_x(T, u):
                    act.wait_ge(f_t[m], T + 1)
                    wait(act, f_m1[m], T - 1)
                    nc.scalar.copy(fx_a[:, u % 2, :], tp[:, 0:P])
                    for n in range(2):
                        last = nc.scalar.copy(fx_b[n * DB:(n + 1) * DB, u % 2, :], tp[0:DB, P:2 * P])
                    last.then_inc(f_x[m], 1)

                def gelus(T, u, e):
                    wait(act, f_m2[m], T - 1)
                    wait_apart(act, f_m1[m], T + 1, marks_act)
                    for k in range(FC):
                        c = k % 3
                        last = nc.scalar.activation(ht[:, u % 2, k * P:(k + 1) * P], hid[u % 2][k // 3][:, c * P:(c + 1) * P],
                                                    ACT.Gelu, bias=b1_[:, ds(e * FC + k, 1)])
                    last.then_inc(f_ge[m], 1)

                def body(i, u, t):
                    if not (isinstance(t, int) and t == 0):
                        e = act.value_load(turn_of[m][0:1, 1, ds(i if u else i - 1, 1)], min_val=0, max_val=NE - 1)
                    copy_x(t, u)
                    if not (isinstance(t, int) and t == 0):
                        gelus(t - 1, (u - 1) % UT, e)

                turn(0, body)
                if m == 0:
                    load_biases(act, (b1s_u, b2s_u), ("b1u", "b2u"), s_wu)
                    with act.Fori(1, NE + 1) as i:
                        turn(i, body)
                        load_expert(act, i - 1, (w1a_u, w1b_u, w2s_u), ("w1u", "w2u"), s_wu)
                n = turns(act, m, body, NE + 1 if m == 0 else 1)
                e = act.value_load(turn_of[m][0:1, 1, ds(n - 1, 1)], min_val=0, max_val=NE - 1)
                gelus(UT * n - 1, UT - 1, e)

            act.wait_ge(s_free, 1)
            act.wait_ge(s_tab, 1)
            act.wait_ge(s_wc, n_w)
            experts(0)
            act.wait_ge(s_wu, n_w)
            act.wait_ge(s_tab, 2)
            act.wait_ge(s_first, 1)
            experts(1)

        @block.tensor
        def _(pe):
            mmul = nc.tensor.matmul
            pe.wait_ge(s_const, 1)
            pe.wait_ge(s_wa, n_wa)
            pe.wait_ge(s_prep, 1)

            def body(i, u):
                g1, g2, g3, g4, g5 = stages(i, u)

                def cap(v):
                    return min(v, NG) if isinstance(v, int) else v

                def seg(j):
                    if g3 is None:
                        return
                    pe.wait_ge(s_sl, GS * g3 + j + 1)
                    wait(pe, s_e, GS * g3 + j)
                    for b, bank_ in enumerate((sg0, sg1)):
                        last = mmul(bank_[:, 0:3 * P], gt[:, :], seg_l[:, j % 2, 3 * b:3 * b + 3, :], start=True, stop=True)
                    last.then_inc(s_sg, 1)

                def cbx(j):
                    if g3 is None:
                        return
                    p, js = u % 2, slice(j * L, (j + 1) * L)
                    pe.wait_ge(s_xbc, g3 + 1)
                    wait(pe, s_xd, GS * g3 + j)
                    mmul(cx[:, 0:P], xbc[:, p, ZT, js], xbc[:, p, ZT + 1, js], start=True, stop=True)
                    for c in range(ZT):
                        last = nc.tensor.transpose(cx[:, (c + 1) * P:(c + 2) * P], xbc[:, p, c, js], ident[:, :])
                    last.then_inc(s_cx, 1)

                def y(j):
                    if g3 is None:
                        return
                    pe.wait_ge(s_m, GS * g3 + j + 1)
                    wait(pe, s_yd, GS * g3 + j)
                    for h in range(HEADS):
                        r = (h % 2) * HD
                        last = mmul(yb[r:r + HD, (h // 2) * P:(h // 2 + 1) * P], xd[:, j % 2, h * HD:(h + 1) * HD],
                                    mix[:, j % 2, h, :], start=True, stop=True)
                    last.then_inc(s_yp, 1)

                def dt():
                    if g2 is None:
                        return
                    p = (u + 1) % 2
                    pe.wait_ge(s_xt, 2 * (g2 + 1))
                    wait(pe, s_dab, g2)
                    wait(pe, s_h1, 2 * (g2 - 2))
                    if not (isinstance(g2, int) and g2 < 4):
                        pe.wait_ge(s_dest, CREDIT + g2 - 3)
                    for j in range(GS):
                        o = misc[:, DTC + j * HEADS:DTC + (j + 1) * HEADS]
                        js = slice(j * L, (j + 1) * L)
                        mmul(o, xt_a[:, p, js], win_a[:, PROJ - HEADS:PROJ], start=True, stop=False)
                        last = mmul(o, xt_b[:, p, js], win_b[:, PROJ - HEADS:PROJ], start=False, stop=True)
                    last.then_inc(s_dtp, 1)

                def project(m):
                    if g2 is None:
                        return
                    p = (u + 1) % 2
                    if m < 2:
                        wait(pe, s_zc, ZT * (g2 - 1) + m + 2)
                    elif m - 2 < XT:
                        pe.wait_ge(s_cv, XT * g2 + m - 1)
                    else:
                        pe.wait_ge(s_zc, ZT * g2 + m - 1 - XT)
                    c0 = INNER + m * P if m < XT else (m - XT) * P
                    mmul(mm[m % 2][:, :], win_a[:, c0:c0 + P], xt_a[:, p, :], start=True, stop=False)
                    mmul(mm[m % 2][:, :], win_b[:, c0:c0 + P], xt_b[:, p, :], start=False, stop=True).then_inc(s_mm, 1)

                def sums():
                    if g4 is None:
                        return
                    pe.wait_ge(s_sqa, g4 + 1)
                    wait(pe, s_ms, g4)
                    wait(pe, s_dab, cap(g4 + 2))
                    wait(pe, s_h1, 2 * g4)
                    if not (isinstance(g4, int) and g4 == 0):
                        pe.wait_ge(s_dest, CREDIT + g4 - 1)
                    for j in range(GS):
                        last = mmul(misc[:, SQC + j:SQC + j + 1], ysq[:, 0, j * L:(j + 1) * L], ones[:, 0:1],
                                    start=True, stop=True)
                    last.then_inc(s_ssq, 1)

                def out_product(q):
                    if g4 is None:
                        return
                    wait(pe, s_h1, 2 * g4 + q)
                    if q == 0:
                        pe.wait_ge(s_ms, g4 + 1)
                        wait(pe, s_d, CREDIT + g4)
                    for j in range(2):
                        for c in range(ZT):
                            last = mmul(misc[:, OUTC + j * D:OUTC + (j + 1) * D],
                                        ybuf[:, (u + 1) % 2, c, (2 * q + j) * L:(2 * q + j + 1) * L],
                                        wo[:, c, :], start=(c == 0), stop=(c == ZT - 1))
                    last.then_inc(s_o, 1)

                def to_tp(g, k, half):
                    if g is None:
                        return
                    rows, c0 = (P, DB)[half], half * P
                    if half == 0:
                        pe.wait_ge((s_xn, s_xn2)[k - 1], g + 1)
                        if k == 2:
                            wait(pe, s_x2t, CREDIT + 2 * g)
                            wait(pe, s_xt, 2 * (min(g + 4, NG) if isinstance(g, int) else g + 4))
                        else:
                            wait(pe, s_xt, 2 * g)
                            wait(pe, s_x2t, CREDIT + 2 * (g - 3))
                    else:
                        wait_apart(pe, (s_xt, s_x2t)[k - 1], (0, CREDIT)[k - 1] + 2 * g + 1, marks_pe)
                    for j in range(GS):
                        src = xn[:, j, c0:c0 + rows] if k == 1 else hr[:, u % 2, j, D + c0:D + c0 + rows]
                        last = nc.tensor.transpose(tp[0:rows, j * L:(j + 1) * L], src, ident[:, :])
                    last.then_inc((s_tr1, s_tr2)[k - 1], 1)

                def routers():
                    if g5 is None:
                        return
                    pe.wait_ge(s_x2t, CREDIT + 2 * g5 + 2)
                    wait(pe, s_d, CREDIT + g5)
                    wait(pe, s_dab, cap(g5 + 3))
                    wait(pe, s_ms, cap(g5 + 2))
                    wait(pe, s_h1, 2 * cap(g5 + 1))
                    wait(pe, s_dest, CREDIT + g5)
                    for j in range(GS):
                        o = misc[:, RTC + j * 2 * NE:RTC + (j + 1) * 2 * NE]
                        mmul(o, x2t_a[:, j * L:(j + 1) * L], wr_a[:, :], start=True, stop=False)
                        last = mmul(o, x2t_b[:, j * L:(j + 1) * L], wr_b[:, :], start=False, stop=True)
                    last.then_inc(s_rt, 1)

                def prefixes():
                    if g5 is None:
                        return
                    pe.wait_ge(s_oh, CREDIT + g5 + 1)
                    wait(pe, s_dest, CREDIT + g5)
                    wait(pe, s_h1, 2 * cap(g5 + 2))
                    mmul(misc[:, PFC:PFC + GS * NE], lt[:, :], oh[:, :, 0, :], start=True, stop=False)
                    mmul(misc[:, PFC:PFC + GS * NE], ones[:, :], acc[:, 0:GS, :], start=False, stop=True).then_inc(s_pf, 1)

                seg(0)
                dt()
                project(0)
                to_tp(g5, 2, 0)
                cbx(0)
                to_tp(g5, 2, 1)
                project(1)
                seg(1)
                y(0)
                sums()
                project(2)
                cbx(1)
                routers()
                project(3)
                seg(2)
                y(1)
                project(4)
                cbx(2)
                out_product(0)
                project(5)
                seg(3)
                y(2)
                project(6)
                out_product(1)
                cbx(3)
                to_tp(g1, 1, 0)
                project(7)
                to_tp(g1, 1, 1)
                prefixes()
                y(3)

            pipeline(pe, body)

            pe.wait_ge(s_cmp, 1)
            mmul(yb[:, 0:NE], ones[:, :], acc[:, 0, :], start=True, stop=True).then_inc(s_cnt, 1)

            def experts(m):
                w2_ = (w2s, w2s_u)[m]

                def transpose_x(i, u, T):
                    pe.wait_ge(f_g[m][u], 16 * (m + 1) * (i + 1))
                    wait(pe, f_x[m], T)
                    nc.tensor.transpose(tp[:, 0:P], xg[:, u, D:D + P], ident[:, :])
                    nc.tensor.transpose(tp[0:DB, P:2 * P], xg[:, u, D + P:2 * D], ident[:, :]).then_inc(f_t[m], 1)

                def hidden_product(i, u, T):
                    if u == 0:
                        pe.wait_ge(f_w[m], i + 1)
                    pe.wait_ge(f_x[m], T + 1)
                    wait(pe, f_ge[m], T - 1)
                    for c in range(3):
                        for n in range(2):
                            mmul(hid[u % 2][n][:, c * P:(c + 1) * P], w1a_t[:, (3 * n + c) * P:(3 * n + c + 1) * P],
                                 fx_a[:, u % 2, :], start=True, stop=False)
                        for n in range(2):
                            r = slice(n * DB, (n + 1) * DB)
                            last = mmul(hid[u % 2][n][:, c * P:(c + 1) * P], w1b_t[r, c * P:(c + 1) * P],
                                        fx_b[r, u % 2, :], start=False, stop=True)
                    last.then_inc(f_m1[m], 1)

                def out_product(i, u, T):
                    e = pe.value_load(turn_of[m][0:1, 1, ds(i, 1)], min_val=0, max_val=NE - 1)
                    pe.wait_ge(f_ge[m], T + 1)
                    wait(pe, f_o[m], T - 1)
                    for k in range(FC):
                        last = mmul(outp[u % 2][:, 0:D], ht[:, u % 2, k * P:(k + 1) * P],
                                    w2_[:, ds(e * (FC * D) + k * D, D)], start=(k == 0), stop=(k == FC - 1))
                    last.then_inc(f_m2[m], 1)
                    if m == 0:
                        count(T)

                def count(T):
                    pe.wait_ge(s_cmp, T + 2)
                    mmul(misc[:, 0:NC], ones_b[:, :], cnt_a[:, :], start=True, stop=False)
                    mmul(misc[:, 0:NC], lt_b[:, :], cnt_b[:, :], start=False, stop=True).then_inc(s_cnt, 1)

                def body(i, u, t):
                    transpose_x(i, u, t)
                    if not (isinstance(t, int) and t < 1):
                        hidden_product(i if u else i - 1, (u - 1) % UT, t - 1)
                    if not (isinstance(t, int) and t < 2):
                        out_product(i if u > 1 else i - 1, (u - 2) % UT, t - 2)

                turn(0, body)
                n = turns(pe, m, body)
                hidden_product(n - 1, UT - 1, UT * n - 1)
                for u in (UT - 2, UT - 1):
                    out_product(n - 1, u, UT * (n - 1) + u)

            pe.wait_ge(s_wc, n_w)
            pe.wait_ge(s_tab, 1)
            experts(0)
            pe.wait_ge(s_tab, 2)
            pe.wait_ge(s_wu, n_w)
            pe.wait_ge(s_first, 1)
            experts(1)

        @block.vector
        def _(dve):
            v = nc.vector
            ts, tt, stt = v.tensor_scalar, v.tensor_tensor, v.scalar_tensor_tensor
            n_setup = [0]

            def link(ins):
                n_setup[0] += 1
                ins.then_inc(c_setup, 1)
                dve.wait_ge(c_setup, n_setup[0])

            dve.wait_ge(s_sig, 1)
            link(ts(gate[:, :], gate[:, :], 1.0, None, ALU.add))
            link(v.reciprocal(gate[:, :], gate[:, :]))
            for c in range(ZT):
                ts(wo[:, c, :], wo[:, c, :], nw[:, c:c + 1], gate[:, 0:1], ALU.mult, ALU.mult)
            ts(nega[:, :], nega[:, :], -1.0, None, ALU.mult).then_inc(s_prep, 1)
            dve.wait_ge(s_prep, 1)
            dve.wait_ge(s_const, 1)

            def norm_stats(x, st, mv, ve, link):
                for j in range(GS):
                    last = v.bn_stats(st[:, j, :], x(j))
                link(last, marks_dve)
                for j in range(GS):
                    last = v.bn_aggr(mv[:, j, :], st[:, j, :])
                link(last)
                return ts(ve, mv[:, :, 1], LNEPS, None, ALU.add)

            def quantise(g, u, turn_):
                p, link = u % 2, Chain(dve, ch["quant"], g, STEPS["quant"])
                dve.wait_ge(s_gath[p], 64 * (turn_ + 1))
                link(v.tensor_reduce(q1[:, 0, :], gath[:, p, :, :], AX.X, ALU.max, apply_absolute_value=True))
                link(ts(q1[:, 1, :], q1[:, 0, :], 1.0 / QMAX, QEPS, ALU.mult, ALU.max))
                link(v.reciprocal(q1[:, 2, :], q1[:, 1, :]))
                wait(dve, s_hx, g)
                for j in range(GS):
                    last = ts(h0[:, j, :], gath[:, p, j, :], q1[:, 2, j:j + 1], MAGIC, ALU.mult, ALU.add)
                link(last)
                link.end()

            quantise(0, 0, 0)

            def body(i, u):
                g1, g2, g3, g4, g5 = stages(i, u)
                chains = {n: Chain(dve, ch[n], g, STEPS[n]) for n, g in (
                    ("clip", g1), ("dt0", g2), ("tap", g2), ("soft", g2), ("ssd", g3), ("h1", g4),
                    ("pick1", g5), ("pick2", g5)) if g is not None}
                r8 = lambda t_: t_[:, :, :, :].rearrange("p j r e -> p (j r) e")
                b8 = lambda t_: t_[:, :, :].rearrange("p j r -> p (j r)").unsqueeze(2).broadcast_to([P, GS * 2, NE])

                def clip():
                    if g1 is None:
                        return
                    p, link = u % 2, chains["clip"]
                    link(ts(h0[:, :, :], h0[:, :, :], MAGIC, QMAX, ALU.subtract, ALU.min))
                    for j in range(GS):
                        last = ts(h0[:, j, :], h0[:, j, :], -QMAX, q1[:, 1, j:j + 1], ALU.max, ALU.mult)
                    link(last)
                    norm_stats(lambda j: h0[:, j, :], st1, mv1, ve1[:, p, :], link).then_inc(s_ve, 1)
                    link.end()
                    if isinstance(g1, int) and g1 == 0:
                        dve.wait_ge(s_rstd, 1)
                        for j in range(GS):
                            last = ts(xn[:, j, :], h0[:, j, :], mv1[:, j, 0:1], rstd1[:, p, j:j + 1],
                                      ALU.subtract, ALU.mult)
                        last.then_inc(s_xn, 1)

                def steps_abs():
                    if g2 is None:
                        return
                    p, link = (u + 1) % 2, chains["dt0"]
                    dve.wait_ge(s_dtp, g2 + 1)
                    link(tt(dtr[:, p, :, :], misc[:, DTC:DTC + GS * HEADS].rearrange("p (j h) -> p j h", j=GS),
                            dtb[:, :].unsqueeze(1).broadcast_to([P, GS, HEADS]), ALU.add))
                    link.end()
                    x_ = dtr[:, p, :, :].rearrange("p j h -> p (j h)")
                    stt(out=dab[:, p, :, :].rearrange("p j h -> p (j h)"), in0=x_, scalar=-1.0, in1=x_,
                        op0=ALU.mult, op1=ALU.max).then_inc(s_dab, 1)

                def steps_softplus():
                    if g2 is None:
                        return
                    p, link = (u + 1) % 2, chains["soft"]
                    flat = lambda t_: t_.rearrange("p j h -> p (j h)")
                    U, DTR, DTS = flat(dtu[:, p, :, :]), flat(dtr[:, p, :, :]), flat(dts[:, p, :, :])
                    S1, S2, S3 = flat(sp1[:, :, :]), flat(sp2[:, :, :]), flat(sp3[:, :, :])
                    dve.wait_ge(s_u, g2 + 1)
                    link(ts(S1, U, 2.0, None, ALU.add))
                    link(v.reciprocal(S2, S1))
                    link(tt(S1, S2, U, ALU.mult))
                    link(tt(S2, S1, S1, ALU.mult))
                    link(ts(S3, S2, 1.0 / 13, None, ALU.mult))
                    for d in (11, 9, 7, 5, 3):
                        link(stt(out=S3, in0=S3, scalar=1.0 / d, in1=S2, op0=ALU.add, op1=ALU.mult))
                    link(stt(out=S3, in0=S3, scalar=1.0, in1=S1, op0=ALU.add, op1=ALU.mult))
                    ts(S2, DTR, 0.0, None, ALU.max)
                    link(ts(S3, S3, 2.0, None, ALU.mult))
                    link.end()
                    tt(DTS, S3, S2, ALU.add).then_inc(s_dts, 1)
                    dve.wait_ge(s_dts, g2 + 1)
                    tt(dta[:, p, :, :], dts[:, p, :, :], nega[:, :].unsqueeze(1).broadcast_to([P, GS, HEADS]),
                       ALU.mult).then_inc(s_dt, 1)

                def conv(m):
                    if g2 is None:
                        return
                    p, link = (u + 1) % 2, chains["tap"]
                    dve.wait_ge(s_ci, XT * g2 + m + 1)
                    src = mm[m % 2][:, :].rearrange("p (j t) -> p j t", j=GS)
                    dst_ = xbc[:, p, m, :].rearrange("p (j t) -> p j t", j=GS)
                    for back in range(1, TAPS):
                        ins = stt(out=dst_[:, :, back:L], in0=src[:, :, 0:L - back],
                                  scalar=cw[:, m, TAPS - 1 - back:TAPS - back], in1=dst_[:, :, back:L],
                                  op0=ALU.mult, op1=ALU.add)
                        if back < TAPS - 1:
                            link(ins)
                    ins.then_inc(s_cv, 1)

                def weights(j):
                    if g3 is None:
                        return
                    p, link = u % 2, chains["ssd"]
                    dve.wait_ge(s_cx, GS * g3 + j + 1)
                    wait(dve, s_m, GS * g3 + j)
                    link(tt(cbm[:, :], cx[:, 0:P], le[:, :], ALU.mult))
                    wait(dve, s_yp, GS * g3 + j - 1)
                    tt(xd[:, j % 2, :].rearrange("p (h n) -> p h n", h=HEADS),
                       cx[:, P:4 * P].rearrange("p (h n) -> p h n", h=HEADS),
                       dts[:, p, j, :].unsqueeze(2).broadcast_to([P, HEADS, HD]), ALU.mult).then_inc(s_xd, 1)
                    dve.wait_ge(s_e, GS * g3 + j + 1)
                    tt(mix[:, j % 2, :, :], dec[:, j % 2, :, :], cbm[:, :].unsqueeze(1).broadcast_to([P, HEADS, P]),
                       ALU.mult).then_inc(s_m, 1)

                def y(j):
                    if g3 is None:
                        return
                    p, js = u % 2, slice(j * L, (j + 1) * L)
                    if j == 0:
                        wait(dve, s_o, 2 * (g3 - 1))
                    dve.wait_ge(s_yp, GS * g3 + j + 1)
                    for c in range(ZT):
                        last = stt(out=ybuf[:, p, c, js], in0=xbc[:, p, c, js], scalar=dskip[:, c:c + 1],
                                   in1=yb[:, c * P:(c + 1) * P], op0=ALU.mult, op1=ALU.add)
                    last.then_inc(s_yd, 1)

                def mean_square():
                    if g4 is None:
                        return
                    dve.wait_ge(s_ssq, g4 + 1)
                    ts(ms[:, :], misc[:, SQC:SQC + GS], 1.0 / INNER, LNEPS, ALU.mult, ALU.add).then_inc(s_ms, 1)

                def residual(q):
                    if g4 is None:
                        return
                    p = (u + 1) % 2
                    if q == 0:
                        dve.wait_ge(s_rs, g4 + 1)
                        dve.wait_ge(s_hx, g4 + 1)
                        wait(dve, s_st[p], CREDIT + 16 * earlier(i, u, 3))
                    dve.wait_ge(s_o, 2 * g4 + q + 1)
                    for j in range(2):
                        last = stt(out=hr[:, p, 2 * q + j, 0:D], in0=misc[:, OUTC + j * D:OUTC + (j + 1) * D],
                                   scalar=rs[:, 2 * q + j:2 * q + j + 1], in1=hx[:, (u + 1) % 4, 2 * q + j, :],
                                   op0=ALU.mult, op1=ALU.add)
                    last.then_inc(s_h1, 1)

                def stats2():
                    if g4 is None:
                        return
                    dve.wait_ge(s_h1, 2 * g4 + 2)
                    norm_stats(lambda j: hr[:, (u + 1) % 2, j, 0:D], st2, mv2, ve2[:, :], chains["h1"]).then_inc(s_ve2, 1)
                    chains["h1"].end()

                def logits():
                    if g5 is None:
                        return
                    link = chains["pick1"]
                    dve.wait_ge(s_rt, CREDIT + g5 + 1)
                    wait(dve, s_el, CREDIT + g5)
                    link(tt(lg[:, :, :, :].rearrange("p j r e -> p j (r e)"),
                            misc[:, RTC:RTC + GS * 2 * NE].rearrange("p (j n) -> p j n", j=GS),
                            rb[:, :].unsqueeze(1).broadcast_to([P, GS, 2 * NE]), ALU.add))
                    link(v.tensor_reduce(m8[:, :, :], lg[:, :, :, :], AX.X, ALU.max))
                    tt(r8(dl), r8(lg), b8(m8), ALU.subtract).then_inc(s_d, 1)
                    link.end()

                def pick():
                    if g5 is None:
                        return
                    link = chains["pick2"]
                    dve.wait_ge(s_el, CREDIT + g5 + 1)
                    wait(dve, s_dest, CREDIT + g5)
                    link(v.tensor_reduce(e8[:, :, :], el[:, :, :, :], AX.X, ALU.max))
                    v.tensor_reduce(s8[:, :, :], el[:, :, :, :], AX.X, ALU.add)
                    link(tt(r8(pk), r8(el), b8(e8), ALU.is_equal))
                    link(tt(r8(pk), r8(pk), w4[:, :].unsqueeze(1).broadcast_to([P, GS * 2, NE]), ALU.mult))
                    link(v.tensor_reduce(m8[:, :, :], pk[:, :, :, :], AX.X, ALU.max))
                    link(tt(r8(oh), r8(pk), b8(m8), ALU.is_equal))
                    link(v.reciprocal(s8[:, :, :], s8[:, :, :]))
                    tt(conf[:, ds(GS * g5, GS)], s8[:, :, 0], e8[:, :, 0], ALU.mult)
                    v.tensor_copy(ohc[:, ds(GS * g5, GS), :], oh[:, :, 0, :])
                    v.tensor_copy(ohu[:, ds(GS * g5, GS), :], oh[:, :, 1, :])
                    for j in range(GS):
                        ins = tt(acc[:, j + 1, :], acc[:, j, :], oh[:, j, 0, :], ALU.add)
                        if j < GS - 1:
                            link(ins)
                    ins.then_inc(s_oh, 1)

                def places():
                    if g5 is None:
                        return
                    p, link = u % 2, chains["pick2"]
                    dve.wait_ge(s_pf, g5 + 1)
                    link(tt(dst[:, :, :], misc[:, PFC:PFC + GS * NE].rearrange("p (j e) -> p j e", j=GS), oh[:, :, 0, :],
                            ALU.mult))
                    link(v.tensor_reduce(dest[:, :], dst[:, :, :], AX.X, ALU.add))
                    link.end()
                    wait(dve, s_scd, CREDIT + g5)
                    v.tensor_copy(acc[:, 0, :], acc[:, GS, :])
                    v.tensor_copy(desti[:, p, :], dest[:, :])
                    v.tensor_copy(toki[:, p, :], tok[:, ds(GS * g5, GS)]).then_inc(s_dest, 1)

                steps_abs()
                conv(0)
                weights(0)
                clip()
                conv(1)
                y(0)
                mean_square()
                conv(2)
                weights(1)
                steps_softplus()
                conv(3)
                logits()
                y(1)
                conv(4)
                weights(2)
                residual(0)
                pick()
                y(2)
                residual(1)
                weights(3)
                stats2()
                y(3)
                places()
                if g1 is not None:
                    quantise(g1 + 1, u + 1, earlier(i, u + 1, 0))
                for n in ("tap", "ssd", "soft"):
                    if n in chains:
                        chains[n].end()

            pipeline(dve, body)
            nf = [0]

            def link(ins):
                nf[0] += 1
                ins.then_inc(c_find, 1)
                dve.wait_ge(c_find, nf[0])

            dve.wait_ge(s_dest, CREDIT + NG)
            dve.sem_inc(s_cmp, 1)
            link(v.tensor_copy(trow[:, 0, :], iota[:, :]))
            dve.wait_ge(s_cnt, 1)

            def turn_table(m, counts):
                link(tt(lst[:, 0, :], counts, base_e[:, :], ALU.subtract))
                link(ts(lst[:, 1, :], lst[:, 0, :], float(TL - 1), 1.0 / TL, ALU.add, ALU.mult))
                link(ts(lst[:, 1, :], lst[:, 1, :], 0.5 - 0.5 / TL, MAGIC, ALU.subtract, ALU.add))
                link(ts(lst[:, 1, :], lst[:, 1, :], MAGIC, None, ALU.subtract))
                link(ts(lst[:, 1, 0:1], lst[:, 1, 0:1], 1.0, None, ALU.max))
                link(v.tensor_copy(lst[:, 2, 0:1], lst[:, 1, 0:1]))
                for e in range(1, NE):
                    link(tt(lst[:, 2, e:e + 1], lst[:, 2, e - 1:e], lst[:, 1, e:e + 1], ALU.add))
                link(ts(lst[:, 3, :], lst[:, 1, :], -float(TL), float(LIST), ALU.mult, ALU.add))
                r = trow[:, :, 0:TT[m] + 1]
                link(ts(r[:, 1, :], r[:, 0, :], float(TL), None, ALU.mult))
                link(v.memset(r[:, 2, :], 0.0))
                for e in range(NE - 1):
                    link(ts(r[:, 3, :], r[:, 0, :], lst[:, 2, e:e + 1], None, ALU.is_ge))
                    tt(r[:, 2, :], r[:, 2, :], r[:, 3, :], ALU.add)
                    link(stt(out=r[:, 1, :], in0=r[:, 3, :], scalar=lst[:, 3, e:e + 1], in1=r[:, 1, :],
                             op0=ALU.mult, op1=ALU.add))
                v.tensor_copy(turn_of[m][:, 0, :], r[:, 1, :])
                v.tensor_copy(turn_of[m][:, 1, :], r[:, 2, :])
                ts(turns_n[m][:, :], lst[:, 2, NE - 1:NE], 2.0, -2.0, ALU.max, ALU.add).then_inc(s_tab, 1)

            turn_table(0, yb[0:1, 0:NE])

            for p in range(2):
                dve.wait_ge(s_st[p], CREDIT + 16 * (NG // 2))
                dve.wait_ge(s_sc[p], 64 * (NG // 2))
            dve.wait_ge(s_gath[0], 64 * (NG // 2 + 1))
            dve.sem_inc(s_free, 1)

            def turn_weights(m, i):
                w1a_, w1b_ = ((w1a, w1b), (w1a_u, w1b_u))[m]
                e = dve.value_load(turn_of[m][0:1, 1, ds(i, 1)], min_val=0, max_val=NE - 1)
                wait(dve, f_m1[m], UT * i)
                v.tensor_copy(w1a_t[:, :], w1a_[:, ds(e * F, F)])
                v.tensor_copy(w1b_t[:, :], w1b_[:, ds(e * FH, FH)]).then_inc(f_w[m], 1)

            dve.wait_ge(s_tab, 1)
            dve.wait_ge(s_wc, n_w)
            turn_weights(0, 0)
            v.memset(cnt_a[:, :], 0.0)
            v.memset(cnt_b[:, :], 0.0)
            v.memset(ones_b[:, :], 1.0)
            v.tensor_copy(lt_b[:, :], lt[:, :])
            v.memset(zero[:, :], 0.0)
            v.memset(og[:, :, :], 0.0)
            link(v.memset(step[:, :], 1.0))
            link(v.memset(thr[:, :], 0.0))

            by_e = lambda t_: t_[:, :, :].rearrange("p b e -> p e b")
            confb = conf[:, :].unsqueeze(1).broadcast_to([P, NE, SEQS])
            eb = lambda t_: t_[:, :].unsqueeze(2).broadcast_to([P, NE, SEQS])
            link(tt(key[:, :, :], by_e(ohc), confb, ALU.mult))
            link(stt(out=key[:, :, :], in0=by_e(ohc), scalar=1.0, in1=key[:, :, :], op0=ALU.subtract, op1=ALU.add))
            cnt = lambda t_: t_[:, 0:NE * SEQS].rearrange("p (e b) -> p e b", e=NE)
            counts = cnt(misc)
            link(tt(cand[:, :], thr[:, :], step[:, :], ALU.add))
            tt(cnt(cnt_a), key[:, :, :], eb(cand), ALU.is_ge).then_inc(s_cmp, 1)

            def search(t):
                link = Chain(dve, ch["find"], t, STEPS["find"])
                dve.wait_ge(s_cnt, t + 2)
                link(v.tensor_reduce(tot[:, :], counts, AX.X, ALU.add))
                link(ts(tot[:, :], tot[:, :], float(CAP), None, ALU.is_ge))
                link(tt(tot[:, :], tot[:, :], step[:, :], ALU.mult))
                link(tt(thr[:, :], thr[:, :], tot[:, :], ALU.add))
                link(ts(step[:, :], step[:, :], 0.5, None, ALU.mult))
                link(tt(cand[:, :], thr[:, :], step[:, :], ALU.add))
                link.end()
                tt(cnt(cnt_a), key[:, :, :], eb(cand), ALU.is_ge).then_inc(s_cmp, 1)

            def above():
                dve.wait_ge(s_cnt, BITS + 2)
                tt(cmp_[:, :, :], key[:, :, :], eb(thr), ALU.is_gt)
                link(tt(eqk[:, :, :], key[:, :, :], eb(thr), ALU.is_equal))
                v.tensor_copy(cnt(cnt_a), cmp_[:, :, :]).then_inc(s_cmp, 1)

            def at_threshold():
                dve.wait_ge(s_cnt, BITS + 3)
                link(v.tensor_reduce(tot[:, :], counts, AX.X, ALU.add))
                link(ts(need[:, :], tot[:, :], -1.0, float(CAP), ALU.mult, ALU.add))
                for e in range(NE):
                    last = v.tensor_tensor_scan(out=scn[:, e, :], data0=eqk[:, e, :], data1=zero[:, :], initial=0.0,
                                                op0=ALU.add, op1=ALU.add)
                link(last)
                v.tensor_copy(cnt(cnt_b), eqk[:, :, :])
                tt(cnt(cnt_a), scn[:, :, :], eqk[:, :, :], ALU.subtract).then_inc(s_cmp, 1)

            def dropped():
                dve.wait_ge(s_cnt, BITS + 4)
                link(tt(tmp[:, :, :], counts, eb(need), ALU.is_lt))
                link(tt(tmp[:, :, :], tmp[:, :, :], eqk[:, :, :], ALU.mult))
                link(tt(tmp[:, :, :], tmp[:, :, :], cmp_[:, :, :], ALU.add))
                link(ts(tmp[:, :, :], tmp[:, :, :], -1.0, 1.0, ALU.mult, ALU.add))
                link(tt(tmp[:, :, :], tmp[:, :, :], by_e(ohc), ALU.mult))
                link(v.tensor_reduce(drop[:, :], tmp[:, :, :].rearrange("p e b -> p b e"), AX.X, ALU.add))
                link(tt(cmp_[:, :, :], by_e(ohu), drop[:, :].unsqueeze(1).broadcast_to([P, NE, SEQS]), ALU.mult))
                for e in range(NE):
                    last = v.tensor_tensor_scan(out=scn[:, e, :], data0=cmp_[:, e, :], data1=zero[:, :],
                                                initial=float(e * LIST // P), op0=ALU.add, op1=ALU.add)
                link(last)
                v.tensor_copy(cnt_a[:, NE * SEQS:NC], scn[:, :, SEQS - 1])
                v.tensor_copy(cnt(cnt_b), cmp_[:, :, :])
                tt(cnt(cnt_a), scn[:, :, :], cmp_[:, :, :], ALU.subtract).then_inc(s_cmp, 1)

            def slots():
                dve.wait_ge(s_cnt, BITS + 5)
                link(tt(tmp[:, :, :], counts, cmp_[:, :, :], ALU.mult))
                link(v.tensor_reduce(slotf[:, :], tmp[:, :, :].rearrange("p e b -> p b e"), AX.X, ALU.add))
                link(ts(drop[:, :], drop[:, :], -NO_SLOT, NO_SLOT, ALU.mult, ALU.add))
                link(tt(slotf[:, :], slotf[:, :], drop[:, :], ALU.add))
                v.tensor_copy(slot_u[:, :], slotf[:, :]).then_inc(s_slot, 1)
                turn_table(1, misc[0:1, NE * SEQS:NC])
                dve.sem_inc(s_cmp, 1)

            def experts(m):
                b2_ = (b2s, b2s_u)[m]
                def body(i, u, t):
                    rest = xg[:, u, 0:D] if m == 0 else og[:, u, :]
                    e = dve.value_load(turn_of[m][0:1, 1, ds(i, 1)], min_val=0, max_val=NE - 1)
                    dve.wait_ge(f_g[m][u], 16 * (m + 1) * (i + 1))
                    wait(dve, f_s[m][u], 16 * i)
                    tt(osb[:, u, :], rest, b2_[:, ds(e * D, D)], ALU.add).then_inc(f_r[m], 1)
                    if u == 2:
                        turn_weights(m, i + 1)
                    dve.wait_ge(f_r[m], t + 1)
                    dve.wait_ge(f_m2[m], t + 1)
                    tt(osb[:, u, :], outp[u % 2][:, 0:D], osb[:, u, :], ALU.add).then_inc(f_o[m], 1)

                def searching(i, u, t):
                    body(i, u, t)
                    search(t)

                def ranking(i, u, t):
                    body(i, u, t)
                    (above, at_threshold, dropped, slots)[u]()

                def passing(i, u, t):
                    body(i, u, t)
                    dve.sem_inc(s_cmp, 1)

                if m == 1:
                    turn_weights(1, 0)
                if m == 0:
                    turn(0, searching)
                    with dve.Fori(1, SEARCH) as i:
                        turn(i, searching)
                    turn(SEARCH, ranking)
                    turns(dve, m, passing, SEARCH + 1)
                else:
                    turn(0, body)
                    turns(dve, m, body)

            experts(0)
            dve.wait_ge(s_tab, 2)
            dve.wait_ge(s_wu, n_w)
            dve.wait_ge(s_first, 1)
            experts(1)


_INS = ["x_t", "table", "w_in", "conv_w", "conv_b", "dt_bias", "a_log", "d_skip", "norm_w", "gate", "w_out",
        "w_route", "b_route", "w4", "iota", "base_e", "w1c", "w2c", "b1c", "b2c", "w1u", "w2u", "b1u", "b2u"]


def kernel(x, L0_tok_weight, L0_attn_gate1, L0_attn_in_proj_w, L0_attn_conv_w, L0_attn_conv_b, L0_attn_dt_bias,
           L0_attn_A_log, L0_attn_D, L0_attn_norm_w, L0_attn_out_proj_w, L0_ffn_Wsc, L0_ffn_bsc, L0_ffn_W1c, L0_ffn_b1c,
           L0_ffn_W2c, L0_ffn_b2c, L0_ffn_Wsu, L0_ffn_bsu, L0_ffn_W1u, L0_ffn_b1u, L0_ffn_W2u, L0_ffn_b2u):
    import numpy as np
    import concourse.bacc as bacc
    from concourse.bass_utils import run_bass_kernel_spmd as run

    def rows(v):
        return np.broadcast_to(np.asarray(v).reshape(1, -1), (P, np.asarray(v).size))

    def by_part(b):
        return np.asarray(b).reshape(NE * FC, P).T

    a = {
        "x_t": np.asarray(x).T, "table": L0_tok_weight, "w_in": np.asarray(L0_attn_in_proj_w).T, "conv_w": L0_attn_conv_w,
        "conv_b": np.asarray(L0_attn_conv_b).reshape(XT, P).T, "dt_bias": rows(L0_attn_dt_bias), "a_log": rows(L0_attn_A_log),
        "d_skip": np.repeat(np.asarray(L0_attn_D), HD).reshape(ZT, P).T, "norm_w": np.asarray(L0_attn_norm_w).reshape(ZT, P).T,
        "gate": rows(L0_attn_gate1), "w_out": np.asarray(L0_attn_out_proj_w).T,
        "w_route": np.concatenate([L0_ffn_Wsc, L0_ffn_Wsu], axis=1),
        "b_route": rows(np.concatenate([L0_ffn_bsc, L0_ffn_bsu])),
        "w4": np.broadcast_to(np.arange(NE, 0, -1, dtype=np.float32), (P, NE)),
        "iota": np.arange(TT[0] + 1, dtype=np.float32).reshape(1, TT[0] + 1),
        "base_e": (np.arange(NE) * LIST).astype(np.float32).reshape(1, NE),
        "w1c": L0_ffn_W1c, "w2c": L0_ffn_W2c, "b1c": by_part(L0_ffn_b1c), "b2c": rows(L0_ffn_b2c),
        "w1u": L0_ffn_W1u, "w2u": L0_ffn_W2u, "b1u": by_part(L0_ffn_b1u), "b2u": rows(L0_ffn_b2u),
    }
    nc = bacc.Bacc("TRN2", target_bir_lowering=False, num_devices=1)
    arrays, args = {}, {}
    for name in _INS:
        arrays[f"in_{name}_dram"] = np.ascontiguousarray(a[name])
        args[name] = nc.dram_tensor(f"in_{name}_dram", arrays[f"in_{name}_dram"].shape,
                                    mybir.dt.from_np(arrays[f"in_{name}_dram"].dtype), kind="ExternalInput").ap()
    out = nc.dram_tensor("out_0_dram", (SEQS, L, D), F32, kind="ExternalOutput").ap()
    build(nc, args, out)
    r = run(nc, [arrays], core_ids=[0])
    return r.results[0]["out_0_dram"]
```
